# Optimizing a Trainium2 kernel written in Bass

```python
import numpy as np
import jax
import jax.numpy as jnp

def _softmax(x, axis=-1):
    return jax.nn.softmax(x, axis=axis)

def _gelu(x):
    return jax.nn.gelu(x, approximate=True)

def _silu(x):
    return jax.nn.silu(x)

def _sigmoid(x):
    return jax.nn.sigmoid(x)

def _layernorm(x, axis=-1, eps=1e-05):
    m = jnp.mean(x, axis=axis, keepdims=True)
    v = jnp.var(x, axis=axis, keepdims=True)
    return (x - m) / jnp.sqrt(v + eps)

def _scatter_add(tgt, idx, src, axis=0):
    return tgt.at[idx].add(src)

def _segment_sum(src, seg, n):
    return jax.ops.segment_sum(src, seg, n)
kernel_name = 'mk_prb_d1_jaxref_r8_18a394'

def setup_inputs(seed: int=0):
    np.random.seed(seed)
    _w = jnp.asarray

    def _L0_attn_setup():
        import jax, jax.numpy as jnp
        import numpy as np
        N_HEAD = 16
        LATENT = 32

        def _rotate_half(x):
            xe = x[..., ::2]
            xo = x[..., 1::2]
            return jnp.stack((-xo, xe), axis=-1).reshape(x.shape)

        def _rope_tables(T, latent_dim, dtype):
            inv_freq = 1.0 / 10000.0 ** (jnp.arange(0, latent_dim, 2, dtype=jnp.float32) / latent_dim)
            t = jnp.arange(T, dtype=jnp.float32)
            freqs = jnp.outer(t, inv_freq)
            cos = jnp.repeat(jnp.cos(freqs), 2, axis=-1)[:, :latent_dim]
            sin = jnp.repeat(jnp.sin(freqs), 2, axis=-1)[:, :latent_dim]
            return (cos.astype(dtype), sin.astype(dtype))
        key = jax.random.key(seed)
        ks = jax.random.split(key, 14)
        C = 128
        hd = C // N_HEAD
        L = LATENT
        s = 0.02
        return {'x': jax.random.normal(ks[0], (4, 256, C), jnp.float32), 'c_attn_w': jax.random.normal(ks[1], (3 * C, C), jnp.float32) * s, 'c_attn_b': jnp.zeros((3 * C,), jnp.float32), 'q2l_w': jax.random.normal(ks[2], (L, hd), jnp.float32) * s, 'q2l_b': jnp.zeros((L,), jnp.float32), 'kv2l_w': jax.random.normal(ks[3], (L, hd), jnp.float32) * s, 'kv2l_b': jnp.zeros((L,), jnp.float32), 'l2o_w': jax.random.normal(ks[4], (hd, L), jnp.float32) * s, 'l2o_b': jnp.zeros((hd,), jnp.float32), 'wqk_w': jax.random.normal(ks[5], (L, L), jnp.float32) * s, 'wqk_b': jnp.zeros((L,), jnp.float32), 'cproj_w': jax.random.normal(ks[6], (C, C), jnp.float32) * s, 'cproj_b': jnp.zeros((C,), jnp.float32)}
    _L0_attn_in = _L0_attn_setup()

    def _L0_ffn_setup():
        import jax, jax.numpy as jnp
        import numpy as np
        B, T, C, I, E = (4, 256, 128, 352, 7)

        def _swiglu(h, w1, w2, w3):
            return jax.nn.silu(h @ w1.T) * (h @ w3.T) @ w2.T
        key = jax.random.key(seed)
        ks = jax.random.split(key, 9)
        sc_c = 1.0 / np.sqrt(C)
        sc_i = 1.0 / np.sqrt(I)
        return {'x': jax.random.normal(ks[0], (B, T, C), jnp.float32), 'router_w': jax.random.normal(ks[1], (E, C), jnp.float32) * sc_c, 'routing_bias': jnp.zeros((E,), jnp.float32), 'sw1': jax.random.normal(ks[2], (I, C), jnp.float32) * sc_c, 'sw2': jax.random.normal(ks[3], (C, I), jnp.float32) * sc_i, 'sw3': jax.random.normal(ks[4], (I, C), jnp.float32) * sc_c, 'ew1': jax.random.normal(ks[5], (E, I, C), jnp.float32) * sc_c, 'ew2': jax.random.normal(ks[6], (E, C, I), jnp.float32) * sc_i, 'ew3': jax.random.normal(ks[7], (E, I, C), jnp.float32) * sc_c}
    _L0_ffn_in = _L0_ffn_setup()
    _d = {'L0_attn_x': _L0_attn_in['x'], 'L0_attn_c_attn_w': _L0_attn_in['c_attn_w'], 'L0_attn_c_attn_b': _L0_attn_in['c_attn_b'], 'L0_attn_q2l_w': _L0_attn_in['q2l_w'], 'L0_attn_q2l_b': _L0_attn_in['q2l_b'], 'L0_attn_kv2l_w': _L0_attn_in['kv2l_w'], 'L0_attn_kv2l_b': _L0_attn_in['kv2l_b'], 'L0_attn_l2o_w': _L0_attn_in['l2o_w'], 'L0_attn_l2o_b': _L0_attn_in['l2o_b'], 'L0_attn_wqk_w': _L0_attn_in['wqk_w'], 'L0_attn_wqk_b': _L0_attn_in['wqk_b'], 'L0_attn_cproj_w': _L0_attn_in['cproj_w'], 'L0_attn_cproj_b': _L0_attn_in['cproj_b'], 'L0_ffn_router_w': _L0_ffn_in['router_w'], 'L0_ffn_routing_bias': _L0_ffn_in['routing_bias'], 'L0_ffn_sw1': _L0_ffn_in['sw1'], 'L0_ffn_sw2': _L0_ffn_in['sw2'], 'L0_ffn_sw3': _L0_ffn_in['sw3'], 'L0_ffn_ew1': _L0_ffn_in['ew1'], 'L0_ffn_ew2': _L0_ffn_in['ew2'], 'L0_ffn_ew3': _L0_ffn_in['ew3']}
    _x0 = _d['L0_attn_x']
    _d['L0_attn_x'] = jax.random.normal(jax.random.fold_in(jax.random.key(seed), 1), (8, 512, 128), dtype=_x0.dtype)
    del _x0
    return _d

def reference(L0_attn_x, L0_attn_c_attn_w, L0_attn_c_attn_b, L0_attn_q2l_w, L0_attn_q2l_b, L0_attn_kv2l_w, L0_attn_kv2l_b, L0_attn_l2o_w, L0_attn_l2o_b, L0_attn_wqk_w, L0_attn_wqk_b, L0_attn_cproj_w, L0_attn_cproj_b, L0_ffn_router_w, L0_ffn_routing_bias, L0_ffn_sw1, L0_ffn_sw2, L0_ffn_sw3, L0_ffn_ew1, L0_ffn_ew2, L0_ffn_ew3):

    def _L0_attn_ref(x, c_attn_w, c_attn_b, q2l_w, q2l_b, kv2l_w, kv2l_b, l2o_w, l2o_b, wqk_w, wqk_b, cproj_w, cproj_b):
        import jax, jax.numpy as jnp
        import numpy as np
        N_HEAD = 16
        LATENT = 32

        def _rotate_half(x):
            xe = x[..., ::2]
            xo = x[..., 1::2]
            return jnp.stack((-xo, xe), axis=-1).reshape(x.shape)

        def _rope_tables(T, latent_dim, dtype):
            inv_freq = 1.0 / 10000.0 ** (jnp.arange(0, latent_dim, 2, dtype=jnp.float32) / latent_dim)
            t = jnp.arange(T, dtype=jnp.float32)
            freqs = jnp.outer(t, inv_freq)
            cos = jnp.repeat(jnp.cos(freqs), 2, axis=-1)[:, :latent_dim]
            sin = jnp.repeat(jnp.sin(freqs), 2, axis=-1)[:, :latent_dim]
            return (cos.astype(dtype), sin.astype(dtype))
        B, T, C = x.shape
        H = N_HEAD
        hd = C // H
        L = q2l_w.shape[0]
        qkv = x @ c_attn_w.T + c_attn_b
        q, k, v = jnp.split(qkv, 3, axis=2)

        def heads(t):
            return t.reshape(B, T, H, hd).transpose(0, 2, 1, 3)
        q, k, v = (heads(q), heads(k), heads(v))
        q_lat = q @ q2l_w.T + q2l_b
        k_lat = k @ kv2l_w.T + kv2l_b
        v_lat = v @ kv2l_w.T + kv2l_b
        cos, sin = _rope_tables(T, L, x.dtype)
        cos = cos[None, None]
        sin = sin[None, None]
        q_lat = q_lat * cos + _rotate_half(q_lat) * sin
        k_lat = k_lat * cos + _rotate_half(k_lat) * sin
        q_for_k = q_lat @ wqk_w.T + wqk_b
        att = jnp.einsum('bhql,bhkl->bhqk', q_for_k, k_lat) * L ** (-0.5)
        causal = jnp.tril(jnp.ones((T, T), dtype=bool))
        att = jnp.where(causal[None, None], att, -jnp.inf)
        att = jax.nn.softmax(att, axis=-1)
        y_lat = jnp.einsum('bhqk,bhkl->bhql', att, v_lat)
        y = y_lat @ l2o_w.T + l2o_b
        y = y.transpose(0, 2, 1, 3).reshape(B, T, C)
        return y @ cproj_w.T + cproj_b

    def _L0_ffn_ref(x, router_w, routing_bias, sw1, sw2, sw3, ew1, ew2, ew3):
        import jax, jax.numpy as jnp
        import numpy as np
        B, T, C, I, E = (4, 256, 128, 352, 7)

        def _swiglu(h, w1, w2, w3):
            return jax.nn.silu(h @ w1.T) * (h @ w3.T) @ w2.T
        b, t, c = x.shape
        shared_out = _swiglu(x, sw1, sw2, sw3)
        logits = jnp.clip(x @ router_w.T + routing_bias, -50.0, 50.0)
        probs = jax.nn.sigmoid(logits)
        num_switched = 1
        topk_probs, topk_idx = jax.lax.top_k(probs, num_switched)
        topk_probs = jnp.clip(topk_probs, 1e-08, 1.0 - 1e-08)
        xf = x.reshape(-1, c)
        sel = topk_idx.reshape(-1)
        p = topk_probs.reshape(-1)
        switched = jnp.zeros_like(xf)
        n_experts = ew1.shape[0]
        for e in range(n_experts):
            y = _swiglu(xf, ew1[e], ew2[e], ew3[e])
            w = jnp.where(sel == e, p, 0.0)
            switched = switched + w[:, None] * y
        switched = switched.reshape(b, t, c)
        total_weight = 0.5 + topk_probs.sum(axis=-1)
        total_weight = jnp.clip(total_weight[..., None] + 1e-08, 0.5, 2.0)
        return 0.5 / total_weight * shared_out + switched / total_weight
    x = L0_attn_x
    xn = _layernorm(x, axis=-1)
    x = x + _L0_attn_ref(xn, L0_attn_c_attn_w, L0_attn_c_attn_b, L0_attn_q2l_w, L0_attn_q2l_b, L0_attn_kv2l_w, L0_attn_kv2l_b, L0_attn_l2o_w, L0_attn_l2o_b, L0_attn_wqk_w, L0_attn_wqk_b, L0_attn_cproj_w, L0_attn_cproj_b) + _L0_ffn_ref(xn, L0_ffn_router_w, L0_ffn_routing_bias, L0_ffn_sw1, L0_ffn_sw2, L0_ffn_sw3, L0_ffn_ew1, L0_ffn_ew2, L0_ffn_ew3)
    return x

_drawn_inputs = setup_inputs


def setup_inputs(seed=0):
    import zlib

    import numpy as np

    out = dict(_drawn_inputs(seed))
    spreads = {'L0_attn_c_attn_b': (0.0, 0.8),
     'L0_attn_q2l_b': (0.0, 2.0),
     'L0_attn_kv2l_b': (0.0, 0.8),
     'L0_attn_l2o_b': (0.0, 0.304),
     'L0_attn_wqk_b': (0.0, 2.0),
     'L0_attn_cproj_b': (0.0, 0.1),
     'L0_ffn_routing_bias': (0.0, 0.1)}
    factors = {'L0_attn_c_attn_w': 8.0,
     'L0_attn_q2l_w': 8.0,
     'L0_attn_kv2l_w': 8.0,
     'L0_attn_l2o_w': 8.0,
     'L0_attn_wqk_w': 8.0}
    for name, (base, spread) in spreads.items():
        noise = np.random.default_rng([zlib.crc32(name.encode()), seed]).standard_normal(out[name].shape)
        drawn = base * np.exp(spread * noise) if base else spread * noise
        out[name] = jnp.asarray(drawn.astype(out[name].dtype))
    for name, factor in factors.items():
        out[name] = (out[name] * factor).astype(out[name].dtype)
    return out
```

```python
import numpy as np

import concourse.bass as bass
from concourse import mybir
from contextlib import ExitStack

F32 = mybir.dt.float32
F32R = mybir.dt.float32r
BF16 = mybir.dt.bfloat16
I32 = mybir.dt.int32
U32 = mybir.dt.uint32
ALU = mybir.AluOpType
ACT = mybir.ActivationFunctionType
AX = mybir.AxisListType

B, T, C = 8, 512, 128
H = 16
HD = C // H
L = 32
I = 352
E = 7
P = 128
N = B * T
NT = N // P
HG = P // L
G_PER_PAIR = H // HG
PAIRS = B // 2
PT = 2 * T
QT = T // P
STEPS = PAIRS * H
GROUPS = STEPS // HG
SLOTS = 8
KROWS = 3 * L
SROWS = KROWS + 2
VW = HD + 1
PW = [T, T, T // 2, P]
POFF = [0, T, 2 * T, 2 * T + T // 2]
PCOLS = sum(PW)
IC = [P, P, I - 2 * P]
ETILES = NT + E - 1
ETABLE = ETILES + 2
MASKED = -3.0e38
SCALE = float(L) ** -0.5

CONSTS = ["ident", "mask", "cosr", "sinr", "sumsel", "tri", "ones", "rank", "thresh", "tileno"]


def shape_constants():
    inv = (1.0 / np.float32(10000.0) ** (np.arange(0, L, 2, dtype=np.float32) / np.float32(L))).astype(np.float32)
    ang = np.outer(np.arange(T, dtype=np.float32), inv).astype(np.float32)
    cos = np.repeat(np.cos(ang), 2, axis=1).T
    sin = np.repeat(np.sin(ang), 2, axis=1).T
    sign = np.where(np.arange(L) % 2 == 0, -1.0, 1.0)[:, None]
    mask = np.zeros((P, T), np.float32)
    mask[:, T - P:] = np.where(np.arange(P)[None, :] <= np.arange(P)[:, None], 0.0, MASKED)
    sumsel = np.zeros((P, 2 * VW), np.float32)
    for q in range(4):
        for d in range(VW):
            sumsel[L * q + d, (q // 2) * VW + d] = 1.0
    r = np.arange(P)
    return {
        "ident": np.eye(P, dtype=np.float32),
        "mask": mask,
        "cosr": np.ascontiguousarray(np.tile(cos, (HG, 1)).astype(np.float32)),
        "sinr": np.ascontiguousarray(np.tile(sin * sign, (HG, 1)).astype(np.float32)),
        "sumsel": sumsel,
        "tri": (r[:, None] < r[None, :]).astype(np.float32),
        "ones": np.ones((P, P), np.float32),
        "rank": np.ascontiguousarray(np.broadcast_to(np.arange(E, 0, -1, dtype=np.float32), (P, E))),
        "thresh": np.ascontiguousarray(np.broadcast_to(np.arange(NT, dtype=np.float32) * P, (P, NT))),
        "tileno": np.ascontiguousarray(np.broadcast_to(np.arange(ETABLE, dtype=np.float32), (P, ETABLE))),
    }


def build(nc, d, out):
    ctx = ExitStack()
    with ctx:
        def keep(name, shape, dt):
            return ctx.enter_context(nc.sbuf_tensor(name, shape, dt))

        def sem(name):
            return ctx.enter_context(nc.semaphore(name))

        bank = [ctx.enter_context(nc.psum_tensor(f"bank{i}", [P, 512], F32)) for i in range(8)]

        xn_rows = nc.dram_tensor("xn_rows", [N, C], F32, kind="Internal").ap()
        sorted_x = nc.dram_tensor("sorted_x", [ETABLE * P, C], F32, kind="Internal").ap()
        sorted_y = nc.dram_tensor("sorted_y", [ETILES * P, C], F32, kind="Internal").ap()
        mixed = nc.dram_tensor("mixed", [N, C], F32, kind="Internal").ap()

        ident = keep("ident_sb", [P, P], F32)
        xnT = keep("xnT", [C, N], F32)
        pos = keep("pos", [P, NT], U32)
        w_shared = keep("w_shared", [P, NT], F32)
        w_expert = keep("w_expert", [P, NT], F32)
        tile_expert = keep("tile_expert", [P, ETABLE], I32)

        attn_stack = ExitStack()
        with attn_stack:
            def sb(name, shape, dt):
                return attn_stack.enter_context(nc.sbuf_tensor(name, shape, dt))

            xH = sb("xH", [C, PT], F32R)
            xL = sb("xL", [C, PT], F32R)
            wf = sb("wf", [C, 4, 2, H * L], F32R)
            biases = sb("biases", [P, 4 * G_PER_PAIR + G_PER_PAIR], F32)
            wqk = sb("wqk", [P, P], F32)
            wqk_b = sb("wqk_b", [P, 1], F32)
            wvT = sb("wvT", [C, C], F32)
            wout = sb("wout", [C, C], F32)
            const_row = sb("const_row", [P, C], F32)
            cosr = sb("cosr_sb", [P, T], F32)
            sinr = sb("sinr_sb", [P, T], F32)
            mask = sb("mask_sb", [P, T], F32)
            sumsel = sb("sumsel_sb", [P, 2 * VW], F32)

            prologue(nc, d, bank, sem, ident, xnT, pos, w_shared, w_expert, tile_expert, wf, biases, wqk, wqk_b,
                     wvT, wout, const_row, cosr, sinr, mask, sumsel, xn_rows, sorted_x)
            attention(nc, d, bank, sem, sb, ident, xnT, pos, xH, xL, wf, biases, wqk, wqk_b, wvT, wout, const_row,
                      cosr, sinr, mask, sumsel, xn_rows, sorted_x, mixed)
        experts(nc, d, bank, sem, ident, xnT, pos, w_shared, w_expert, tile_expert, sorted_x, sorted_y, mixed, out)


def prologue(nc, d, bank, sem, ident, xnT, pos, w_shared, w_expert, tile_expert, wf, biases, wqk, wqk_b, wvT, wout,
             const_row, cosr, sinr, mask, sumsel, xn_rows, sorted_x):
    tmp = ExitStack()
    with tmp:
        def sb(name, shape, dt):
            return tmp.enter_context(nc.sbuf_tensor(name, shape, dt))

        x = sb("x", [P, NT, C], F32)
        stats = sb("stats", [P, NT, 6], F32)
        mv = sb("mv", [P, NT, 2], F32)
        sd = sb("sd", [P, NT], F32)
        rstd = sb("rstd", [P, NT], F32)
        wqk_nat = sb("wqk_nat", [P, 2, C], F32)
        spread = sb("spread", [P, 4, H * L], F32)
        kvT = sb("kvT", [P, G_PER_PAIR, C], F32)
        oproj = sb("oproj", [P, G_PER_PAIR, C], F32)
        bqkv = sb("bqkv", [P, 3], F32)
        lat_b = sb("lat_b", [P, 5 * G_PER_PAIR], F32)
        out_b = sb("out_b", [P, 1], F32)
        cprojT = sb("cprojT", [C, C], F32)
        cproj_b = sb("cproj_b", [P, C], F32)
        m1T = sb("m1T", [C, C], F32)
        o_col = sb("o_col", [C, 1], F32)
        o_rep = sb("o_rep", [C, C], F32)
        routerT = sb("routerT", [C, E], F32)
        router_b = sb("router_b", [P, E], F32)
        tri = sb("tri_sb", [P, P], F32)
        ones = sb("ones_sb", [P, P], F32)
        rank = sb("rank_sb", [P, E], F32)
        thresh = sb("thresh_sb", [P, NT], F32)
        tileno = sb("tileno_sb", [P, ETABLE], F32)
        zeros = sb("zeros", [P, 4 * C], F32)
        lg = sb("lg", [P, E, NT], F32)
        pr = sb("pr", [P, E, NT], F32)
        oh = sb("oh", [P, E, NT], F32)
        pm = sb("pm", [P, NT], F32)
        ms = sb("ms", [P, NT], F32)
        tot = sb("tot", [P, E, NT], F32)
        cum = sb("cum", [P, E, NT], F32)
        before = sb("before", [P, E], F32)
        cnt = sb("cnt", [P, E], F32)
        gt = sb("gt", [P, E, NT], F32)
        nt_e = sb("nt_e", [P, E], F32)
        end_e = sb("end_e", [P, E], F32)
        off_e = sb("off_e", [P, E], F32)
        ge = sb("ge", [P, ETABLE, E], F32)
        te = sb("te", [P, ETABLE], F32)
        posf = sb("posf", [P, NT], F32)
        small = sb("small", [P, NT], F32)

        first_in = sem("first_in")
        x_in = [sem(f"x_in{i}") for i in range(4)]
        fold_in = sem("fold_in")
        rest_in = sem("rest_in")
        zeros_set = sem("zeros_set")
        zero_rows = sem("zero_rows")
        norm_step = sem("norm_step")
        sd_ready = sem("sd_ready")
        xn_ready = sem("xn_ready")
        xn_stored = sem("xn_stored")
        xt_ready = sem("xt_ready")
        xt_copied = sem("xt_copied")
        fold_ready = sem("fold_ready")
        fold_high = sem("fold_high")
        fold_low = sem("fold_low")
        bias_ready = sem("bias_ready")
        m1_ready = sem("m1_ready")
        vec = sem("vec")
        o_ready = sem("o_ready")
        o_spread = sem("o_spread")
        wout_ready = sem("wout_ready")
        bias_used = sem("bias_used")
        logits_ready = sem("logits_ready")
        neg_exp = sem("neg_exp")
        l_clipped = sem("l_clipped")
        onehot_ready = sem("onehot_ready")
        prefix_ready = sem("prefix_ready")
        XB = NT // 4
        X3 = d["x"].rearrange("(t p) c -> p t c", p=P)
        FOLD = [(wqk_nat[:], d["wqk_nat"]), (spread[:], d["spread"])]
        REST = [(kvT[:], d["kvT"]), (oproj[:], d["oproj"]), (bqkv[:], d["bqkv"]), (lat_b[:], d["lat_b"]),
                (out_b[:], d["out_b"]), (cprojT[:], d["cprojT"]), (cproj_b[:], d["cproj_b"]),
                (routerT[:], d["routerT"]), (router_b[:], d["router_b"]), (tri[:], d["tri"]), (ones[:], d["ones"]),
                (rank[:], d["rank"]), (thresh[:], d["thresh"]), (tileno[:], d["tileno"]), (wqk[:], d["wqk_bd"]),
                (wqk_b[:], d["wqk_b"]), (wvT[:], d["wvT"]), (cosr[:], d["cosr"]), (sinr[:], d["sinr"]),
                (mask[:], d["mask"]), (sumsel[:], d["sumsel"])]

        with nc.Block() as block:
            @block.sync
            def _(sp):
                sp.dma_start(ident[:], d["ident"]).then_inc(first_in, 16)
                for i in range(4):
                    sp.dma_start(x[:, XB * i:XB * (i + 1), :], X3[:, XB * i:XB * (i + 1), :]).then_inc(x_in[i], 16)
                for dst, src in REST[4:]:
                    sp.dma_start(dst, src).then_inc(rest_in, 16)
                sp.wait_ge(xn_ready, NT)
                sp.dma_start(xn_rows.rearrange("(t p) c -> p t c", p=P), x[:]).then_inc(xn_stored, 16)
                sp.wait_ge(xn_stored, 16)
                sp.wait_ge(zero_rows, 16 * (ETABLE // 4))

            @block.gpsimd
            def _(pool):
                nc.gpsimd.memset(zeros[:], 0.0).then_inc(zeros_set, 1)
                pool.wait_ge(zeros_set, 1)
                for i in range(ETABLE // 4):
                    pool.dma_start(sorted_x[4 * P * i:4 * P * (i + 1), :].rearrange("(p a) c -> p (a c)", p=P),
                                   zeros[:]).then_inc(zero_rows, 16)

            @block.scalar
            def _(act):
                for dst, src in FOLD:
                    act.dma_start(dst, src).then_inc(fold_in, 16)
                for dst, src in REST[:4]:
                    act.dma_start(dst, src).then_inc(rest_in, 16)
                for k in range(4):
                    act.wait_ge(fold_ready, k + 1)
                    nc.scalar.copy(wf[:, k, 0, :], bank[4 + k][:]).then_inc(fold_high, 1)
                act.wait_ge(norm_step, 2)
                nc.scalar.activation(sd[:], sd[:], ACT.Sqrt).then_inc(sd_ready, 1)
                for i in range(NT // 4):
                    act.wait_ge(xt_ready, 4 * i + 4)
                    nc.scalar.copy(xnT[:, 512 * i:512 * (i + 1)], bank[i % 2][:]).then_inc(xt_copied, 1)
                act.wait_ge(l_clipped, 1)
                nc.scalar.activation(pr[:], lg[:], ACT.Exp, scale=-1.0).then_inc(neg_exp, 1)

            @block.tensor
            def _(pe):
                pe.wait_ge(fold_in, 32)
                for k in range(4):
                    nc.tensor.matmul(bank[4 + k][:], wqk_nat[:, k // 2, :], spread[:, k, :],
                                     start=True, stop=True).then_inc(fold_ready, 1)
                pe.wait_ge(rest_in, 16 * len(REST))
                for k in range(5):
                    for g in range(G_PER_PAIR):
                        at = k * G_PER_PAIR + g
                        kind, col = (k, k // 2) if k < 4 else (2, 2)
                        last = nc.tensor.matmul(bank[3][:, at:at + 1], spread[:, kind, P * g:P * (g + 1)],
                                                bqkv[:, col:col + 1], start=True, stop=True)
                last.then_inc(bias_ready, 1)
                for g in range(G_PER_PAIR):
                    last = nc.tensor.matmul(bank[2][:, 0:C], oproj[:, g, :], kvT[:, g, :],
                                            start=(g == 0), stop=(g == G_PER_PAIR - 1))
                last.then_inc(m1_ready, 1)
                pe.wait_ge(vec, 2)
                for g in range(G_PER_PAIR):
                    at = 4 * G_PER_PAIR + g
                    last = nc.tensor.matmul(bank[2][:, C:C + 1], oproj[:, g, :], biases[:, at:at + 1],
                                            start=(g == 0), stop=(g == G_PER_PAIR - 1))
                last.then_inc(o_ready, 1)
                pe.wait_ge(o_spread, 2)
                nc.tensor.matmul(bank[2][:, 2 * C:3 * C], m1T[:], cprojT[:], start=True, stop=True)
                nc.tensor.matmul(bank[2][:, 3 * C:4 * C], o_rep[:], cprojT[:], start=True,
                                 stop=True).then_inc(wout_ready, 1)
                pe.wait_ge(first_in, 16)
                for t in range(NT):
                    pe.wait_ge(xn_ready, t + 1)
                    if t % 4 == 0 and t >= 8:
                        pe.wait_ge(xt_copied, t // 4 - 1)
                    nc.tensor.transpose(bank[t // 4 % 2][:, P * (t % 4):P * (t % 4 + 1)], x[:, t, :],
                                        ident[:]).then_inc(xt_ready, 1)
                pe.wait_ge(bias_used, 1)
                for t in range(NT):
                    pe.wait_ge(xt_copied, t // 4 + 1)
                    last = nc.tensor.matmul(bank[3][:, E * t:E * (t + 1)], xnT[:, P * t:P * (t + 1)], routerT[:],
                                            start=True, stop=True)
                last.then_inc(logits_ready, 1)
                pe.wait_ge(onehot_ready, 1)
                pe.wait_ge(fold_low, 4)
                nc.tensor.matmul(bank[4][:, 0:E * NT], tri[:], oh[:].rearrange("p e t -> p (e t)"),
                                 start=True, stop=True)
                nc.tensor.matmul(bank[5][:, 0:E * NT], ones[:], oh[:].rearrange("p e t -> p (e t)"),
                                 start=True, stop=True).then_inc(prefix_ready, 1)

            @block.vector
            def _(dve):
                chained = [0]

                def chain(ins):
                    chained[0] += 1
                    ins.then_inc(vec, 1)
                    dve.wait_ge(vec, chained[0])

                dve.wait_ge(bias_ready, 1)
                chain(nc.vector.tensor_tensor(biases[:], bank[3][:, 0:5 * G_PER_PAIR], lat_b[:], ALU.add))
                dve.sem_inc(bias_used, 1)
                dve.wait_ge(m1_ready, 1)
                chain(nc.vector.tensor_copy(m1T[:], bank[2][:, 0:C]))
                for k in range(4):
                    dve.wait_ge(fold_high, k + 1)
                    nc.vector.tensor_tensor(wf[:, k, 1, :], bank[4 + k][:], wf[:, k, 0, :].bitcast(F32),
                                            ALU.subtract).then_inc(fold_low, 1)
                dve.wait_ge(o_ready, 1)
                nc.vector.tensor_tensor(o_col[:], bank[2][:, C:C + 1], out_b[:], ALU.add).then_inc(o_spread, 1)
                dve.wait_ge(o_spread, 1)
                nc.vector.tensor_scalar(o_rep[:], ones[:], o_col[:, 0:1], None, ALU.mult).then_inc(o_spread, 1)
                dve.wait_ge(wout_ready, 1)
                nc.vector.tensor_copy(wout[:], bank[2][:, 2 * C:3 * C])
                nc.vector.tensor_tensor(const_row[:], bank[2][:, 3 * C:4 * C], cproj_b[:], ALU.add)

                for t in range(NT):
                    if t % XB == 0:
                        dve.wait_ge(x_in[t // XB], 16)
                    ins = nc.vector.bn_stats(stats[:, t, :], x[:, t, :])
                chain(ins)
                for t in range(NT):
                    ins = nc.vector.bn_aggr(mv[:, t, :], stats[:, t, :])
                ins.then_inc(norm_step, 1)
                dve.wait_ge(norm_step, 1)
                nc.vector.tensor_scalar(sd[:], mv[:, :, 1], 1e-5, None, ALU.add).then_inc(norm_step, 1)
                dve.wait_ge(sd_ready, 1)
                chain(nc.vector.reciprocal(rstd[:], sd[:]))
                for t in range(NT):
                    nc.vector.tensor_scalar(x[:, t, :], x[:, t, :], mv[:, t, 0:1], rstd[:, t:t + 1],
                                            ALU.subtract, ALU.mult).then_inc(xn_ready, 1)

                dve.wait_ge(logits_ready, 1)
                chain(nc.vector.tensor_tensor(lg[:], bank[3][:, 0:E * NT].rearrange("p (t e) -> p e t", e=E),
                                              router_b[:].unsqueeze(2).to_broadcast([P, E, NT]), ALU.add))
                nc.vector.tensor_scalar(lg[:], lg[:], -50.0, 50.0, ALU.max, ALU.min).then_inc(l_clipped, 1)
                dve.wait_ge(neg_exp, 1)
                chain(nc.vector.tensor_scalar(pr[:], pr[:], 1.0, None, ALU.add))
                chain(nc.vector.reciprocal(pr[:], pr[:]))
                chain(nc.vector.tensor_reduce(pm[:], pr[:].rearrange("p e t -> p t e"), AX.X, ALU.max))
                chain(nc.vector.tensor_tensor(oh[:], pr[:], pm[:].unsqueeze(1).to_broadcast([P, E, NT]),
                                              ALU.is_equal))
                chain(nc.vector.tensor_tensor(oh[:], oh[:], rank[:].unsqueeze(2).to_broadcast([P, E, NT]), ALU.mult))
                chain(nc.vector.tensor_reduce(ms[:], oh[:].rearrange("p e t -> p t e"), AX.X, ALU.max))
                nc.vector.tensor_tensor(oh[:], oh[:], ms[:].unsqueeze(1).to_broadcast([P, E, NT]),
                                        ALU.is_equal).then_inc(onehot_ready, 1)
                chain(nc.vector.tensor_scalar(pm[:], pm[:], 1e-8, 1.0, ALU.max, ALU.min))
                chain(nc.vector.tensor_scalar(small[:], pm[:], 0.5, 1e-8, ALU.add, ALU.add))
                chain(nc.vector.tensor_scalar(small[:], small[:], 0.5, 2.0, ALU.max, ALU.min))
                chain(nc.vector.reciprocal(small[:], small[:]))
                nc.vector.tensor_scalar(w_shared[:], small[:], 0.5, None, ALU.mult)
                nc.vector.tensor_tensor(w_expert[:], small[:], pm[:], ALU.mult)
                dve.wait_ge(prefix_ready, 1)
                chain(nc.vector.tensor_copy(tot[:].rearrange("p e t -> p (e t)"), bank[5][:, 0:E * NT]))
                chain(nc.vector.tensor_tensor_scan(cum[:].rearrange("p e t -> p (e t)"),
                                                   tot[:].rearrange("p e t -> p (e t)"),
                                                   tot[:].rearrange("p e t -> p (e t)"), 0.0, ALU.add, ALU.bypass))
                nc.vector.memset(before[:, 0:1], 0.0)
                chain(nc.vector.tensor_copy(before[:, 1:E], cum[:, 0:E - 1, NT - 1]))
                chain(nc.vector.tensor_tensor(cnt[:], cum[:, :, NT - 1], before[:], ALU.subtract))
                chain(nc.vector.tensor_tensor(gt[:], cnt[:].unsqueeze(2).to_broadcast([P, E, NT]),
                                              thresh[:].unsqueeze(1).to_broadcast([P, E, NT]), ALU.is_gt))
                chain(nc.vector.tensor_reduce(nt_e[:], gt[:], AX.X, ALU.add))
                chain(nc.vector.tensor_tensor_scan(end_e[:], nt_e[:], nt_e[:], 0.0, ALU.add, ALU.bypass))
                chain(nc.vector.tensor_tensor(ge[:], tileno[:].unsqueeze(2).to_broadcast([P, ETABLE, E]),
                                              end_e[:].unsqueeze(1).to_broadcast([P, ETABLE, E]), ALU.is_ge))
                chain(nc.vector.tensor_reduce(te[:], ge[:], AX.X, ALU.add))
                nc.vector.tensor_scalar(tile_expert[:], te[:], float(E - 1), None, ALU.min)
                chain(nc.vector.tensor_tensor(off_e[:], end_e[:], nt_e[:], ALU.subtract))
                chain(nc.vector.scalar_tensor_tensor(off_e[:], off_e[:], float(P), before[:], ALU.mult,
                                                     ALU.subtract))
                chain(nc.vector.tensor_tensor(cum[:], cum[:], tot[:], ALU.subtract))
                chain(nc.vector.tensor_tensor(cum[:].rearrange("p e t -> p (e t)"),
                                              cum[:].rearrange("p e t -> p (e t)"), bank[4][:, 0:E * NT], ALU.add))
                chain(nc.vector.tensor_tensor(cum[:], cum[:], off_e[:].unsqueeze(2).to_broadcast([P, E, NT]),
                                              ALU.add))
                chain(nc.vector.tensor_tensor(cum[:], cum[:], oh[:], ALU.mult))
                chain(nc.vector.tensor_reduce(posf[:], cum[:].rearrange("p e t -> p t e"), AX.X, ALU.add))
                nc.vector.tensor_copy(pos[:], posf[:])


def attention(nc, d, bank, sem, sb, ident, xnT, pos, xH, xL, wf, biases, wqk, wqk_b, wvT, wout, const_row, cosr,
              sinr, mask, sumsel, xn_rows, sorted_x, mixed):
    Kst = sb("Kst", [P, SLOTS, PT], F32R)
    Qst = sb("Qst", [P, SLOTS, PT], F32R)
    dKH = sb("dKH", [P, 2, PT], F32R)
    dKL = sb("dKL", [P, 2, PT], F32R)
    dQH = sb("dQH", [P, 2, PT], F32R)
    dQL = sb("dQL", [P, 2, PT], F32R)
    tk1 = sb("tk1", [P, PT], F32)
    tq1 = sb("tq1", [P, PT], F32)
    t2 = sb("t2", [P, PT], F32)
    prob = sb("prob", [P, 2, 2, PCOLS], F32)
    v = sb("v", [P, 3, 2 * QT, HG, VW], F32)
    ysb = sb("ysb", [P, T], F32)
    yn = sb("yn", [P, 2, 2 * QT, C], F32)
    yT = sb("yT", [C, QT * P], F32)
    xres = sb("xres", [P, 2 * QT, C], F32)
    scratch = sb("scratch", [P, 2, T], BF16)
    mx = sb("mx", [P, 2, 2 * QT], F32)
    nm = sb("nm", [P, 2, 4 * QT], F32R)
    nmT = sb("nmT", [4 * QT, 2, P], F32R)
    rz = sb("rz", [P, QT, 2], F32)
    xrow = sb("xrow", [P, 4, C], F32)

    S = bank[0:2]
    ST = bank[2:4]
    Y, PA, PB, M = bank[4], bank[5], bank[6], bank[7]

    set_up = sem("set_up")
    y_clear = sem("y_clear")
    xh_ready, xl_ready = sem("xh_ready"), sem("xl_ready")
    pa_ready, pb_ready, pa_used, pb_used = sem("pa_ready"), sem("pb_ready"), sem("pa_used"), sem("pb_used")
    k_roped, q_roped, kh_ready, kl_ready, qh_ready = (sem("k_roped"), sem("q_roped"), sem("kh_ready"),
                                                      sem("kl_ready"), sem("qh_ready"))
    filled = [sem(f"filled{i}") for i in range(SLOTS)]
    neg_in = [sem(f"neg_in{i}") for i in range(2)]
    s_ready, s_max = sem("s_ready"), sem("s_max")
    neg_high, neg_ready, negT_ready, negT_copied = (sem("neg_high"), sem("neg_ready"), sem("negT_ready"),
                                                    sem("negT_copied"))
    st_ready, exp_done, cut_done, pv_done = sem("st_ready"), sem("exp_done"), sem("cut_done"), sem("pv_done")
    y_copied, z_ready, rz_ready, z_used = sem("y_copied"), sem("z_ready"), sem("rz_ready"), sem("z_used")
    ynT_ready, ynT_copied, o_ready2, o_added = sem("ynT_ready"), sem("ynT_copied"), sem("o_ready2"), sem("o_added")
    xres_in, xres_const, mixed_out = sem("xres_in"), sem("xres_const"), sem("mixed_out")
    row_in = [sem(f"row_in{i}") for i in range(4)]
    row_sorted = [sem(f"row_sorted{i}") for i in range(4)]

    FIRST, LAST = -2 * HG - 2, STEPS + 5

    def chunk(n):
        G = n // HG + 2
        return (G, n % HG) if 0 <= G < GROUPS and n >= -2 * HG else (None, None)

    def split_pair(n):
        return (n + 10) // H if (n + 10) % H == 0 and (n + 10) // H < PAIRS else None

    def out_part(n):
        pair, part = n // H - 1, n % H - 1
        return (pair, part) if 0 <= pair < PAIRS and 0 <= part < 4 else (None, None)

    with nc.Block() as block:
        @block.sync
        def _(sp):
            for n in range(FIRST, LAST):
                m = n + HG
                if 0 <= m < STEPS:
                    G, h, slot = m // HG, m % HG, m % SLOTS
                    if h == 0:
                        sp.wait_ge(kh_ready, G + 1)
                        sp.wait_ge(kl_ready, G + 1)
                        sp.wait_ge(qh_ready, 2 * G + 2)
                        sp.wait_ge(pa_used, 6 * G + 6)
                    if m == 0:
                        sp.wait_ge(set_up, 4)
                    if m >= SLOTS:
                        sp.wait_ge(st_ready, 8 * (m - SLOTS) + 8)
                    rows = slice(L * h, L * h + L)
                    for r, (kd, qd) in enumerate(((dKH, dQH), (dKL, dQH), (dKH, dQL))):
                        sp.dma_start(Kst[L * r:L * r + L, slot, :].bitcast(F32), kd[rows, G % 2, :].bitcast(F32)).then_inc(filled[slot], 16)
                        sp.dma_start(Qst[L * r:L * r + L, slot, :].bitcast(F32), qd[rows, G % 2, :].bitcast(F32)).then_inc(filled[slot], 16)
                if 0 <= n < NT:
                    if n >= 4:
                        sp.wait_ge(row_sorted[n % 4], 16 * (n // 4))
                    sp.dma_start(xrow[:, n % 4, :], xn_rows[P * n:P * (n + 1), :]).then_inc(row_in[n % 4], 16)
                m = n + 1
                if 0 <= m < STEPS:
                    sp.wait_ge(negT_copied, m + 1)
                    if m < 2:
                        sp.wait_ge(set_up, 4)
                    if m >= SLOTS:
                        sp.wait_ge(st_ready, 8 * (m - SLOTS) + 8)
                    sp.dma_start(Qst[KROWS:SROWS, m % SLOTS, :].bitcast(F32), nmT[:, m % 2, :].bitcast(F32)).then_inc(neg_in[m % 2], 16)
                if n % H == 7 and 0 <= n < STEPS:
                    pair = n // H
                    if pair:
                        sp.wait_ge(mixed_out, 16 * pair)
                    sp.dma_start(xres[:], d["x"][PT * pair:PT * (pair + 1), :].rearrange("(t p) c -> p t c", p=P)
                                 ).then_inc(xres_in, 16)
                pair, part = out_part(n)
                if part == 3:
                    sp.wait_ge(o_added, 2 * pair + 2)
                    sp.dma_start(mixed[PT * pair:PT * (pair + 1), :].rearrange("(t p) c -> p t c", p=P),
                                 xres[:]).then_inc(mixed_out, 16)
            sp.wait_ge(mixed_out, 16 * PAIRS)
            for i in range(4):
                sp.wait_ge(row_sorted[i], 16 * (NT // 4))

        @block.gpsimd
        def _(pool):
            nc.gpsimd.memset(Kst[KROWS:P, :, :].bitcast(F32), 1.0).then_inc(set_up, 1)
            pool.wait_ge(set_up, 1)
            nc.gpsimd.memset(v[:, :, :, :, HD:VW], 1.0).then_inc(set_up, 1)
            for par in range(2):
                nc.gpsimd.memset(prob[:, par, :, POFF[1]:POFF[1] + P], 0.0).then_inc(set_up, 1)
            for n in range(FIRST, LAST):
                pair = split_pair(n)
                if pair is not None:
                    pool.wait_ge(xh_ready, pair + 1)
                    nc.gpsimd.tensor_tensor(xL[:], xnT[:, PT * pair:PT * (pair + 1)], xH[:].bitcast(F32),
                                            ALU.subtract).then_inc(xl_ready, 1)
                if 0 <= n < STEPS:
                    for j in range(QT):
                        pool.wait_ge(exp_done, 8 * n + 2 * j + 2)
                        at = POFF[j] + (P if j == 1 else 0)
                        diag = prob[:, n % 2, :, at:at + P]
                        nc.gpsimd.affine_select(out=diag, in_=diag, compare_op=ALU.is_ge, fill=0.0, base=0,
                                                pattern=[[0, 2], [1, P]], channel_multiplier=-1
                                                ).then_inc(cut_done, 1)
                G, part = chunk(n)
                if part == 0:
                    pool.wait_ge(pa_used, 6 * G + 2)
                    pool.wait_ge(pb_used, 5 * G + 2)
                    nc.gpsimd.tensor_tensor(tk1[:], tk1[:], t2[:], ALU.add).then_inc(k_roped, 1)
                    pool.wait_ge(kh_ready, G + 1)
                    nc.gpsimd.tensor_tensor(dKL[:, G % 2, :], tk1[:], dKH[:, G % 2, :].bitcast(F32),
                                            ALU.subtract).then_inc(kl_ready, 1)
                if part == 1:
                    pool.wait_ge(pa_used, 6 * G + 4)
                    pool.wait_ge(pb_used, 5 * G + 4)
                    nc.gpsimd.tensor_tensor(tq1[:], tq1[:], t2[:], ALU.add).then_inc(q_roped, 1)
                if 0 <= n < NT:
                    pool.wait_ge(row_in[n % 4], 16 * (n // 4 + 1))
                    pool.indirect_dma_start(sorted_x, bass.IndirectOffsetOnAxis(pos[:, n:n + 1], 0),
                                            xrow[:, n % 4, :], None).then_inc(row_sorted[n % 4], 16)
                if n % H == 11 and 0 <= n < STEPS:
                    pair = n // H
                    pool.wait_ge(xres_in, 16 * (pair + 1))
                    nc.gpsimd.tensor_tensor(xres[:], xres[:], const_row[:].unsqueeze(1).to_broadcast([P, 2 * QT, C]),
                                            ALU.add).then_inc(xres_const, 1)

        @block.scalar
        def _(act):
            for n in range(FIRST, LAST):
                pair = split_pair(n)
                if pair is not None:
                    if pair:
                        act.wait_ge(pa_ready, 6 * (G_PER_PAIR * pair - 1) + 4)
                        act.wait_ge(pb_ready, 5 * (G_PER_PAIR * pair - 1) + 4)
                        act.wait_ge(xl_ready, pair)
                    nc.scalar.copy(xH[:], xnT[:, PT * pair:PT * (pair + 1)]).then_inc(xh_ready, 1)
                if 0 <= n - 1 < STEPS:
                    act.wait_ge(pv_done, n)
                    if n >= 2:
                        act.wait_ge(z_ready, n - 1)
                    nc.scalar.copy(ysb[:], Y[:]).then_inc(y_copied, 1)
                m = n + 1
                if 0 <= m < STEPS:
                    act.wait_ge(negT_ready, m + 1)
                    if m >= 2:
                        act.wait_ge(neg_in[m % 2], 16 * (m // 2))
                    nc.scalar.copy(nmT[:, m % 2, :], M[0:4 * QT, 0:P]).then_inc(negT_copied, 1)
                if 0 <= n < STEPS:
                    if n >= 2:
                        act.wait_ge(pv_done, n - 1)
                    for i in range(8):
                        j, b = i // 2, i % 2
                        act.wait_ge(st_ready, 8 * n + i + 1)
                        lo, q0 = P * j, min(P * j, T - 2 * P)
                        at = POFF[j] + (P if j == 1 else 0)
                        nc.scalar.activation(prob[:, n % 2, b, at:at + T - lo], ST[i % 2][:, lo - q0:T - q0],
                                             ACT.Exp, scale=SCALE).then_inc(exp_done, 1)
                pair, part = out_part(n)
                if part in (0, 2):
                    act.wait_ge(ynT_ready, 2 * pair + part // 2 + 1)
                    if 2 * pair + part // 2:
                        act.wait_ge(o_ready2, 2 * pair + part // 2)
                    nc.scalar.copy(yT[:], M[:]).then_inc(ynT_copied, 1)
                G, part = chunk(n)
                if part == 1:
                    act.wait_ge(k_roped, G + 1)
                    if G >= 2:
                        for h in range(HG):
                            m = HG * (G - 2) + h
                            act.wait_ge(filled[m % SLOTS], 96 * (m // SLOTS + 1))
                if part == 0:
                    act.wait_ge(k_roped, G + 1)
                    if G >= 2:
                        for h in range(HG):
                            m = HG * (G - 2) + h
                            act.wait_ge(filled[m % SLOTS], 96 * (m // SLOTS + 1))
                    nc.scalar.copy(dKH[:, G % 2, :], tk1[:]).then_inc(kh_ready, 1)
                if part == 3:
                    for f in range(2):
                        act.wait_ge(pa_ready, 6 * G + 5 + f)
                        if f:
                            act.wait_ge(pa_used, 6 * G + 5)
                        nc.scalar.activation(dQH[:, G % 2, T * f:T * (f + 1)], PA[:], ACT.Identity,
                                             bias=wqk_b[:, 0:1]).then_inc(qh_ready, 1)

        @block.tensor
        def _(pe):
            issued = {"neg": 0, "z": 0, "yt": 0, "o": 0}

            def m_free():
                for key, s in (("neg", negT_copied), ("z", z_used), ("yt", ynT_copied), ("o", o_added)):
                    if issued[key]:
                        pe.wait_ge(s, issued[key])

            for n in range(FIRST, LAST):
                if 0 <= n - 1 < STEPS:
                    m = n - 1
                    h = m % HG
                    vs = v[:, m // HG % 3]
                    pe.wait_ge(pb_used, 5 * (m // HG) + 5)
                    if m:
                        pe.wait_ge(y_copied, m)
                    else:
                        pe.wait_ge(y_clear, 1)
                    for j in range(QT):
                        pe.wait_ge(cut_done, 4 * m + j + 1)
                        for b in range(2):
                            q = 2 * b + j % 2
                            c0 = T - PW[j]
                            last = nc.tensor.matmul(Y[L * q:L * q + VW, c0:T], vs[:, QT * b + j, h, :],
                                                    prob[:, m % 2, b, POFF[j]:POFF[j] + PW[j]],
                                                    start=(j < 2), stop=(j >= 2), skip_group_check=True)
                    last.then_inc(pv_done, 1)
                if 0 <= n + 1 < STEPS:
                    m = n + 1
                    pe.wait_ge(neg_ready, m + 1)
                    m_free()
                    nc.tensor.transpose(M[0:4 * QT, 0:P], nm[:, m % 2, :].bitcast(F32), ident[:]
                                        ).then_inc(negT_ready, 1)
                    issued["neg"] += 1
                for i in range(8):
                    if 0 <= n + 2 < STEPS:
                        m = n + 2
                        k = 8 * m + i
                        b, q = i // QT, i % QT
                        if i == 0:
                            pe.wait_ge(filled[m % SLOTS], 96 * (m // SLOTS + 1))
                        if k >= 2:
                            pe.wait_ge(s_max, k - 1)
                        w = max(P * (q + 1), 2 * P)
                        nc.tensor.matmul(S[i % 2][:, 0:w],
                                         Qst[0:KROWS, m % SLOTS, T * b + P * q:T * b + P * (q + 1)],
                                         Kst[0:KROWS, m % SLOTS, T * b:T * b + w],
                                         start=True, stop=True).then_inc(s_ready, 1)
                    if 0 <= n < STEPS:
                        k = 8 * n + i
                        j, b = i // 2, i % 2
                        q0 = min(P * j, T - 2 * P)
                        if i == 0:
                            pe.wait_ge(neg_in[n % 2], 16 * (n // 2 + 1))
                        if k >= 2:
                            pe.wait_ge(exp_done, k - 1)
                        nc.tensor.matmul(ST[i % 2][:, 0:T - q0],
                                         Kst[0:SROWS, n % SLOTS, T * b + P * j:T * b + P * (j + 1)],
                                         Qst[0:SROWS, n % SLOTS, T * b + q0:T * (b + 1)],
                                         start=True, stop=True).then_inc(st_ready, 1)
                if 0 <= n - 1 < STEPS:
                    pe.wait_ge(y_copied, n)
                    m_free()
                    for q in range(QT):
                        last = nc.tensor.matmul(M[:, 2 * VW * q:2 * VW * (q + 1)], ysb[:, P * q:P * (q + 1)],
                                                sumsel[:], start=True, stop=True, skip_group_check=True)
                    last.then_inc(z_ready, 1)
                    issued["z"] += 1
                pair, part = out_part(n)
                if part in (0, 2):
                    m_free()
                    for t in range(QT):
                        last = nc.tensor.transpose(M[:, P * t:P * (t + 1)], yn[:, pair % 2, 2 * part + t, :],
                                                   ident[:])
                    last.then_inc(ynT_ready, 1)
                    issued["yt"] += 1
                if part in (1, 3):
                    m_free()
                    for t in range(QT):
                        last = nc.tensor.matmul(M[:, C * t:C * (t + 1)], yT[:, P * t:P * (t + 1)], wout[:],
                                                start=True, stop=True, skip_group_check=True)
                    last.then_inc(o_ready2, 1)
                    issued["o"] += 1
                G, part = chunk(n)
                if G is not None:
                    g = G % G_PER_PAIR
                    cols = slice(P * g, P * (g + 1))
                    if part == 0:
                        pe.wait_ge(xh_ready, G // G_PER_PAIR + 1)
                        pe.wait_ge(xl_ready, G // G_PER_PAIR + 1)
                    if part in (0, 1):
                        kind = 2 - 2 * part
                        for f in range(2):
                            ua, ub = 6 * G + 2 * part + f, 5 * G + 2 * part + f
                            for bk, kd, use, used, rdy in ((PA, kind, ua, pa_used, pa_ready),
                                                           (PB, kind + 1, ub, pb_used, pb_ready)):
                                if use:
                                    pe.wait_ge(used, use)
                                xs = slice(T * f, T * (f + 1))
                                nc.tensor.matmul(bk[:], wf[:, kd, 0, cols], xH[:, xs], start=True, stop=False)
                                nc.tensor.matmul(bk[:], wf[:, kd, 1, cols], xH[:, xs], start=False, stop=False)
                                nc.tensor.matmul(bk[:], wf[:, kd, 0, cols], xL[:, xs], start=False,
                                                 stop=True).then_inc(rdy, 1)
                    if part == 2:
                        pe.wait_ge(pb_used, 5 * G + 4)
                        for t in range(2 * QT):
                            tok = PT * (G // G_PER_PAIR) + P * t
                            last = nc.tensor.matmul(PB[:, HG * HD * t:HG * HD * (t + 1)], xnT[:, tok:tok + P],
                                                    wvT[:, HG * HD * g:HG * HD * (g + 1)], start=True, stop=True,
                                                    skip_group_check=True)
                        last.then_inc(pb_ready, 1)
                    if part == 3:
                        pe.wait_ge(q_roped, G + 1)
                        for f in range(2):
                            pe.wait_ge(pa_used, 6 * G + 4 + f)
                            nc.tensor.matmul(PA[:], wqk[:], tq1[:, T * f:T * (f + 1)], start=True,
                                             stop=True).then_inc(pa_ready, 1)

        @block.vector
        def _(dve):
            nc.vector.memset(Y[:], 0.0).then_inc(y_clear, 1)
            for n in range(FIRST, LAST):
                if 0 <= n + 2 < STEPS:
                    m = n + 2
                    for i in range(8):
                        q = i % QT
                        w = P * (q + 1)
                        dve.wait_ge(s_ready, 8 * m + i + 1)
                        if 8 * m + i >= 2:
                            dve.wait_ge(s_max, 8 * m + i - 1)
                        nc.vector.tensor_tensor_reduce(scratch[:, i % 2, 0:w], S[i % 2][:, 0:w], mask[:, T - w:T], 1.0,
                                                       MASKED, ALU.add, ALU.max, mx[:, m % 2, i:i + 1]
                                                       ).then_inc(s_max, 1)
                    dve.wait_ge(s_max, 8 * m + 8)
                    if m >= 2:
                        dve.wait_ge(negT_ready, m - 1)
                    nc.vector.tensor_scalar(nm[:, m % 2, 0:2 * QT], mx[:, m % 2, :], -1.0, None, ALU.mult
                                            ).then_inc(neg_high, 1)
                    dve.wait_ge(neg_high, m + 1)
                    nc.vector.scalar_tensor_tensor(nm[:, m % 2, 2 * QT:4 * QT], mx[:, m % 2, :], -1.0,
                                                   nm[:, m % 2, 0:2 * QT].bitcast(F32), ALU.mult, ALU.subtract
                                                   ).then_inc(neg_ready, 1)
                if 0 <= n - 1 < STEPS:
                    m = n - 1
                    Z = M[:, 0:2 * VW * QT].rearrange("p (q b c) -> p q b c", q=QT, b=2)
                    dve.wait_ge(z_ready, m + 1)
                    nc.vector.reciprocal(rz[:], Z[:, :, :, HD]).then_inc(rz_ready, 1)
                    dve.wait_ge(rz_ready, m + 1)
                    pair, head = m // H, m % H
                    if head == 0 and pair >= 2:
                        dve.wait_ge(ynT_ready, 2 * (pair - 1))
                    o = yn[:, pair % 2, :, HD * head:HD * (head + 1)].rearrange("p (b q) c -> p q b c", b=2)
                    nc.vector.tensor_tensor(o, Z[:, :, :, 0:HD], rz[:].unsqueeze(3).to_broadcast([P, QT, 2, HD]),
                                            ALU.mult).then_inc(z_used, 1)
                pair, part = out_part(n)
                if part in (1, 3):
                    dve.wait_ge(o_ready2, 2 * pair + part // 2 + 1)
                    dve.wait_ge(xres_const, pair + 1)
                    half = xres[:, 2 * (part - 1):2 * (part - 1) + QT, :].rearrange("p t c -> p (t c)")
                    nc.vector.tensor_tensor(half, half, M[:], ALU.add).then_inc(o_added, 1)
                G, part = chunk(n)
                if G is not None:
                    g = G % G_PER_PAIR
                    if part in (0, 1):
                        kind = 2 - 2 * part
                        t1 = (tk1, tq1)[part]
                        if part == 0 and G:
                            dve.wait_ge(kl_ready, G)
                            dve.wait_ge(q_roped, G)
                        if part == 1:
                            dve.wait_ge(k_roped, G + 1)
                            if G:
                                dve.wait_ge(pa_ready, 6 * G)
                        for f in range(2):
                            xs = slice(T * f, T * (f + 1))
                            dve.wait_ge(pa_ready, 6 * G + 2 * part + f + 1)
                            nc.vector.scalar_tensor_tensor(t1[:, xs], PA[:], biases[:, kind * G_PER_PAIR + g:kind * G_PER_PAIR + g + 1],
                                                           cosr[:], ALU.add, ALU.mult).then_inc(pa_used, 1)
                            dve.wait_ge(pb_ready, 5 * G + 2 * part + f + 1)
                            nc.vector.scalar_tensor_tensor(t2[:, xs], PB[:], biases[:, (kind + 1) * G_PER_PAIR + g:(kind + 1) * G_PER_PAIR + g + 1],
                                                           sinr[:], ALU.add, ALU.mult).then_inc(pb_used, 1)
                    if part == 2:
                        dve.wait_ge(pb_ready, 5 * G + 5)
                        if G >= 3:
                            dve.wait_ge(pv_done, HG * (G - 2))
                        nc.vector.tensor_copy(v[:, G % 3, :, :, 0:HD].rearrange("p t h d -> p (t h) d"),
                                              PB[:, 0:2 * QT * HG * HD].rearrange("p (t d) -> p t d", d=HD)
                                              ).then_inc(pb_used, 1)
                    if part == 3:
                        for f in range(2):
                            xs = slice(T * f, T * (f + 1))
                            dve.wait_ge(qh_ready, 2 * G + f + 1)
                            nc.vector.scalar_tensor_tensor(dQL[:, G % 2, xs], PA[:], wqk_b[:, 0:1],
                                                           dQH[:, G % 2, xs].bitcast(F32), ALU.add, ALU.subtract
                                                           ).then_inc(pa_used, 1)


def experts(nc, d, bank, sem, ident, xnT, pos, w_shared, w_expert, tile_expert, sorted_x, sorted_y, mixed, out):
    tmp = ExitStack()
    with tmp:
        def sb(name, shape, dt):
            return tmp.enter_context(nc.sbuf_tensor(name, shape, dt))

        w13 = sb("w13", [C, (E + 1), 2 * I], F32)
        w2 = sb("w2", [P, (E + 1), 3, C], F32)
        xs = sb("xs", [P, 4, C], F32)
        xsT = sb("xsT", [C, 2, P], F32)
        g1 = sb("g1", [P, 2, I], F32)
        gg = sb("gg", [P, 2, I], F32)
        gT = sb("gT", [P, 2, 3, P], F32)
        ye = sb("ye", [P, 4, C], F32)
        h1 = sb("h1", [P, 2, 512], F32)
        hT = sb("hT", [P, 2, 3, 512], F32)
        acc = sb("acc", [P, NT, C], F32)
        yg = sb("yg", [P, NT, C], F32)

        w_in = sem("w_in")
        shared_in = sem("shared_in")
        xs_in = [sem(f"xs_in{i}") for i in range(4)]
        xsT_ready, xsT_copied = sem("xsT_ready"), sem("xsT_copied")
        h_ready, silu_done, gate_done = sem("h_ready"), sem("silu_done"), sem("gate_done")
        gT_ready, gT_copied, y_ready, y_copied = (sem("gT_ready"), sem("gT_copied"), sem("ye_ready"),
                                                  sem("ye_copied"))
        y_out = [sem(f"y_out{i}") for i in range(4)]
        acc_in = sem("acc_in")
        gathered = sem("gathered")
        sh_ready, sh_silu, sh_gate = sem("sh_ready"), sem("sh_silu"), sem("sh_gate")
        so_ready, so_added, e_added, out_done = sem("so_ready"), sem("so_added"), sem("e_added"), sem("out_done")
        XT, GT, YB = bank[6], bank[7], bank[4:6]

        xs_rows = sorted_x.rearrange("(t p) c -> t p c", p=P)
        sy_rows = sorted_y.rearrange("(t p) c -> t p c", p=P)

        with nc.Block() as block:
            @block.sync
            def _(sp):
                sp.dma_start(w13[:, 0:E, :], d["w13"][:, 0:E, :]).then_inc(w_in, 16)
                sp.dma_start(w2[:, 0:E, :, :], d["w2"][:, 0:E, :, :]).then_inc(w_in, 16)
                for t in range(ETILES + 1):
                    if t >= 4:
                        sp.wait_ge(xsT_ready, t - 3)
                    sp.dma_start(xs[:, t % 4, :], xs_rows[t]).then_inc(xs_in[t % 4], 16)
                    if t == 4:
                        sp.dma_start(w13[:, E, :], d["w13"][:, E, :]).then_inc(shared_in, 16)
                        sp.dma_start(w2[:, E, :, :], d["w2"][:, E, :, :]).then_inc(shared_in, 16)
                        sp.dma_start(acc[:], mixed.rearrange("(t p) c -> p t c", p=P)).then_inc(acc_in, 16)
                    if t >= 2:
                        u = t - 2
                        sp.wait_ge(y_copied, u + 1)
                        sp.dma_start(sy_rows[u], ye[:, u % 4, :]).then_inc(y_out[u % 4], 16)
                u = ETILES - 1
                sp.wait_ge(y_copied, u + 1)
                sp.dma_start(sy_rows[u], ye[:, u % 4, :]).then_inc(y_out[u % 4], 16)
                for c in range(N // 512):
                    sp.wait_ge(e_added, c + 1)
                    sp.dma_start(out[512 * c:512 * (c + 1), :].rearrange("(t p) c -> p t c", p=P),
                                 acc[:, 4 * c:4 * (c + 1), :]).then_inc(out_done, 16)
                sp.wait_ge(out_done, 16 * (N // 512))

            @block.gpsimd
            def _(pool):
                for i in range(4):
                    pool.wait_ge(y_out[i], 16 * len(range(i, ETILES, 4)))
                for t in range(NT):
                    pool.indirect_dma_start(yg[:, t, :], None, sorted_y,
                                            bass.IndirectOffsetOnAxis(pos[:, t:t + 1], 0)).then_inc(gathered, 16)
                    if t % 4 == 3:
                        pool.wait_ge(gathered, 16 * (t + 1))

            @block.scalar
            def _(act):
                for t in range(ETILES + 1):
                    act.wait_ge(xsT_ready, t + 1)
                    if t >= 2:
                        act.wait_ge(h_ready, t - 1)
                    nc.scalar.copy(xsT[:, t % 2, :], XT[:, P * (t % 2):P * (t % 2 + 1)]).then_inc(xsT_copied, 1)
                    if t:
                        u = t - 1
                        act.wait_ge(h_ready, u + 1)
                        if u >= 2:
                            act.wait_ge(gate_done, u - 1)
                        nc.scalar.activation(g1[:, u % 2, :], bank[2 * (u % 2)][:, 0:I], ACT.Silu
                                             ).then_inc(silu_done, 1)
                        act.wait_ge(y_ready, u + 1)
                        if u >= 4:
                            act.wait_ge(y_out[u % 4], 16 * (u // 4))
                        nc.scalar.copy(ye[:, u % 4, :], YB[u % 2][:, 0:C]).then_inc(y_copied, 1)
                for c in range(N // 512):
                    for k in range(3):
                        u = 3 * c + k
                        act.wait_ge(sh_ready, u + 1)
                        if u >= 2:
                            act.wait_ge(sh_gate, u - 1)
                        nc.scalar.activation(h1[0:IC[k], u % 2, :], bank[2 * (u % 2)][0:IC[k], :], ACT.Silu
                                             ).then_inc(sh_silu, 1)

            @block.tensor
            def _(pe):
                pe.wait_ge(w_in, 32)
                for t in range(ETILES + 2):
                    if t <= ETILES:
                        pe.wait_ge(xs_in[t % 4], 16 * (t // 4 + 1))
                        if t >= 1:
                            pe.wait_ge(xsT_copied, t)
                        nc.tensor.transpose(XT[:, P * (t % 2):P * (t % 2 + 1)], xs[:, t % 4, :], ident[:]
                                            ).then_inc(xsT_ready, 1)
                    if 1 <= t <= ETILES:
                        u = t - 1
                        e = pe.value_load(tile_expert[0:1, u:u + 1], min_val=0, max_val=E - 1)
                        if u >= 2:
                            pe.wait_ge(gate_done, u - 1)
                        nc.tensor.matmul(bank[2 * (u % 2)][:, 0:I], xsT[:, u % 2, :], w13[:, bass.ds(e, 1), 0:I],
                                         start=True, stop=True)
                        nc.tensor.matmul(bank[2 * (u % 2) + 1][:, 0:I], xsT[:, u % 2, :],
                                         w13[:, bass.ds(e, 1), I:2 * I], start=True, stop=True).then_inc(h_ready, 1)
                        pe.wait_ge(gate_done, u + 1)
                        if u >= 1:
                            pe.wait_ge(gT_copied, u)
                        for k in range(3):
                            last = nc.tensor.transpose(GT[0:IC[k], P * k:P * (k + 1)],
                                                       gg[:, u % 2, P * k:P * k + IC[k]], ident[:])
                        last.then_inc(gT_ready, 1)
                        pe.wait_ge(gT_copied, u + 1)
                        if u >= 2:
                            pe.wait_ge(y_copied, u - 1)
                        for k in range(3):
                            last = nc.tensor.matmul(YB[u % 2][:, 0:C], gT[0:IC[k], u % 2, k, :],
                                                    w2[0:IC[k], bass.ds(e, 1), k, :], start=(k == 0), stop=(k == 2))
                        last.then_inc(y_ready, 1)
                pe.wait_ge(shared_in, 32)
                pe.wait_ge(y_copied, ETILES)
                for c in range(N // 512):
                    for k in range(3):
                        u = 3 * c + k
                        if u >= 2:
                            pe.wait_ge(sh_gate, u - 1)
                        for half in range(2):
                            last = nc.tensor.matmul(bank[2 * (u % 2) + half][0:IC[k], :],
                                                    w13[:, E, half * I + P * k:half * I + P * k + IC[k]],
                                                    xnT[:, 512 * c:512 * (c + 1)], start=True, stop=True)
                        last.then_inc(sh_ready, 1)
                    pe.wait_ge(sh_gate, 3 * c + 3)
                    if c >= 2:
                        pe.wait_ge(so_added, c - 1)
                    for t in range(4):
                        for k in range(3):
                            last = nc.tensor.matmul(YB[c % 2][:, C * t:C * (t + 1)],
                                                    hT[0:IC[k], c % 2, k, P * t:P * (t + 1)],
                                                    w2[0:IC[k], E, k, :], start=(k == 0), stop=(k == 2),
                                                    skip_group_check=True)
                    last.then_inc(so_ready, 1)

            @block.vector
            def _(dve):
                for t in range(ETILES):
                    dve.wait_ge(silu_done, t + 1)
                    if t >= 2:
                        dve.wait_ge(gT_ready, t - 1)
                    nc.vector.tensor_tensor(gg[:, t % 2, :], g1[:, t % 2, :], bank[2 * (t % 2) + 1][:, 0:I],
                                            ALU.mult).then_inc(gate_done, 1)
                    dve.wait_ge(gT_ready, t + 1)
                    if t >= 2:
                        dve.wait_ge(y_ready, t - 1)
                    nc.vector.tensor_copy(gT[:, t % 2, 0:2, :].rearrange("p k t -> p (k t)"), GT[:, 0:2 * P])
                    nc.vector.tensor_copy(gT[0:IC[2], t % 2, 2, :], GT[0:IC[2], 2 * P:3 * P]).then_inc(gT_copied, 1)
                dve.wait_ge(acc_in, 16)
                for c in range(N // 512):
                    for k in range(3):
                        u = 3 * c + k
                        dve.wait_ge(sh_silu, u + 1)
                        if c >= 2:
                            dve.wait_ge(so_ready, c - 1)
                        nc.vector.tensor_tensor(hT[0:IC[k], c % 2, k, :], h1[0:IC[k], u % 2, :],
                                                bank[2 * (u % 2) + 1][0:IC[k], :], ALU.mult).then_inc(sh_gate, 1)
                    dve.wait_ge(so_ready, c + 1)
                    for t in range(4):
                        tt = 4 * c + t
                        last = nc.vector.scalar_tensor_tensor(acc[:, tt, :], YB[c % 2][:, C * t:C * (t + 1)],
                                                              w_shared[:, tt:tt + 1], acc[:, tt, :], ALU.mult,
                                                              ALU.add)
                    last.then_inc(so_added, 1)
                    dve.wait_ge(so_added, c + 1)
                    dve.wait_ge(gathered, 64 * (c + 1))
                    for t in range(4):
                        tt = 4 * c + t
                        last = nc.vector.scalar_tensor_tensor(acc[:, tt, :], yg[:, tt, :], w_expert[:, tt:tt + 1],
                                                              acc[:, tt, :], ALU.mult, ALU.add)
                    last.then_inc(e_added, 1)


def block_diagonal(w):
    a, b = w.shape
    out = np.zeros((H * a, H * b), w.dtype)
    for h in range(H):
        out[h * a:(h + 1) * a, h * b:(h + 1) * b] = w
    return out


def kernel(L0_attn_x, L0_attn_c_attn_w, L0_attn_c_attn_b, L0_attn_q2l_w, L0_attn_q2l_b, L0_attn_kv2l_w,
           L0_attn_kv2l_b, L0_attn_l2o_w, L0_attn_l2o_b, L0_attn_wqk_w, L0_attn_wqk_b, L0_attn_cproj_w,
           L0_attn_cproj_b, L0_ffn_router_w, L0_ffn_routing_bias, L0_ffn_sw1, L0_ffn_sw2, L0_ffn_sw3, L0_ffn_ew1,
           L0_ffn_ew2, L0_ffn_ew3):
    import concourse.bacc as bacc
    from concourse.bass_utils import run_bass_kernel_spmd

    a = lambda z: np.asarray(z)
    swap = np.arange(L) ^ 1
    q2l, kv2l, l2o, wqk = a(L0_attn_q2l_w), a(L0_attn_kv2l_w), a(L0_attn_l2o_w), a(L0_attn_wqk_w)
    q2lb, kv2lb = a(L0_attn_q2l_b), a(L0_attn_kv2l_b)
    cw, cb = a(L0_attn_c_attn_w), a(L0_attn_c_attn_b)
    spread = np.stack([block_diagonal(w.T) for w in (q2l, q2l[swap], kv2l, kv2l[swap])], axis=1)
    kvT = block_diagonal(kv2l).reshape(G_PER_PAIR, P, C).transpose(1, 0, 2)
    oproj = block_diagonal(l2o.T).reshape(G_PER_PAIR, P, C).transpose(1, 0, 2)
    wqk_bd = np.zeros((P, P), wqk.dtype)
    for h in range(HG):
        wqk_bd[L * h:L * (h + 1), L * h:L * (h + 1)] = wqk.T
    lat_b = np.stack([np.tile(z, HG) for z in (q2lb, q2lb[swap], kv2lb, kv2lb[swap], kv2lb)
                      for _ in range(G_PER_PAIR)], axis=1)
    w1 = np.concatenate([a(L0_ffn_ew1), a(L0_ffn_sw1)[None]])
    w3 = np.concatenate([a(L0_ffn_ew3), a(L0_ffn_sw3)[None]])
    w2 = np.concatenate([a(L0_ffn_ew2), a(L0_ffn_sw2)[None]])
    w13 = np.concatenate([w1, w3], axis=1).transpose(2, 0, 1)
    w2t = np.zeros((E + 1, 3 * P, C), w2.dtype)
    w2t[:, :I] = w2.transpose(0, 2, 1)
    arrays = {
        "x": a(L0_attn_x).reshape(N, C),
        "wqk_nat": cw[:2 * C].reshape(2, C, C).transpose(1, 0, 2),
        "spread": spread, "kvT": kvT, "oproj": oproj, "bqkv": cb.reshape(3, C).T, "lat_b": lat_b,
        "out_b": np.tile(a(L0_attn_l2o_b), H)[:, None], "cprojT": a(L0_attn_cproj_w).T,
        "cproj_b": np.broadcast_to(a(L0_attn_cproj_b), (P, C)), "routerT": a(L0_ffn_router_w).T,
        "router_b": np.broadcast_to(a(L0_ffn_routing_bias), (P, E)), "wqk_bd": wqk_bd,
        "wqk_b": np.tile(a(L0_attn_wqk_b), HG)[:, None], "wvT": cw[2 * C:].T, "w13": w13,
        "w2": w2t.reshape(E + 1, 3, P, C).transpose(2, 0, 1, 3), **shape_constants(),
    }
    nc = bacc.Bacc("TRN2", target_bir_lowering=False, num_devices=1)
    arrays = {f"in_{k}": np.ascontiguousarray(z) for k, z in arrays.items()}
    d = {k[3:]: nc.dram_tensor(k, z.shape, mybir.dt.from_np(z.dtype), kind="ExternalInput").ap()
         for k, z in arrays.items()}
    out = nc.dram_tensor("out_0", (N, C), F32, kind="ExternalOutput").ap()
    build(nc, d, out)
    r = run_bass_kernel_spmd(nc, [arrays], core_ids=[0])
    return r.results[0]["out_0"].reshape(B, T, C)
```

```python
import numpy as np

import concourse.bass as bass
from concourse import mybir
from contextlib import ExitStack

F32 = mybir.dt.float32
F32R = mybir.dt.float32r
BF16 = mybir.dt.bfloat16
I32 = mybir.dt.int32
U32 = mybir.dt.uint32
ALU = mybir.AluOpType
ACT = mybir.ActivationFunctionType
AX = mybir.AxisListType

B, T, C = 8, 512, 128
H = 16
HD = C // H
L = 32
I = 352
E = 7
P = 128
N = B * T
NT = N // P
HG = P // L
G_PER_PAIR = H // HG
PAIRS = B // 2
PT = 2 * T
QT = T // P
STEPS = PAIRS * H
GROUPS = STEPS // HG
SLOTS = 8
KROWS = 3 * L
SROWS = KROWS + 2
VW = HD + 1
PW = [T, T, T // 2, P]
POFF = [0, T, 2 * T, 2 * T + T // 2]
PCOLS = sum(PW)
IC = [P, P, I - 2 * P]
PA_USES, PB_USES = 5, 6
TC = 512
TT = TC // P
CHUNKS = N // TC
ETILES = NT + E - 1
ETABLE = ETILES + 2
MASKED = -3.0e38
SCALE = float(L) ** -0.5

CONSTS = ["ident", "mask", "cosr", "sinr", "sumsel", "tri", "ones", "rank", "thresh", "tileno"]


def shape_constants():
    inv = (1.0 / np.float32(10000.0) ** (np.arange(0, L, 2, dtype=np.float32) / np.float32(L))).astype(np.float32)
    ang = np.outer(np.arange(T, dtype=np.float32), inv).astype(np.float32)
    cos = np.repeat(np.cos(ang), 2, axis=1).T
    sin = np.repeat(np.sin(ang), 2, axis=1).T
    sign = np.where(np.arange(L) % 2 == 0, -1.0, 1.0)[:, None]
    mask = np.zeros((P, T), np.float32)
    mask[:, T - P:] = np.where(np.arange(P)[None, :] <= np.arange(P)[:, None], 0.0, MASKED)
    sumsel = np.zeros((P, 2 * VW), np.float32)
    for q in range(4):
        for d in range(VW):
            sumsel[L * q + d, (q // 2) * VW + d] = 1.0
    r = np.arange(P)
    return {
        "ident": np.eye(P, dtype=np.float32),
        "mask": mask,
        "cosr": np.ascontiguousarray(np.tile(cos, (HG, 1)).astype(np.float32)),
        "sinr": np.ascontiguousarray(np.tile(sin * sign, (HG, 1)).astype(np.float32)),
        "sumsel": sumsel,
        "tri": (r[:, None] < r[None, :]).astype(np.float32),
        "ones": np.ones((P, P), np.float32),
        "rank": np.ascontiguousarray(np.broadcast_to(np.arange(E, 0, -1, dtype=np.float32), (P, E))),
        "thresh": np.ascontiguousarray(np.broadcast_to(np.arange(NT, dtype=np.float32) * P, (P, NT))),
        "tileno": np.ascontiguousarray(np.broadcast_to(np.arange(ETABLE, dtype=np.float32), (P, ETABLE))),
    }


def build(nc, d, out):
    ctx = ExitStack()
    with ctx:
        def keep(name, shape, dt):
            return ctx.enter_context(nc.sbuf_tensor(name, shape, dt))

        def sem(name):
            return ctx.enter_context(nc.semaphore(name))

        bank = [ctx.enter_context(nc.psum_tensor(f"bank{i}", [P, 512], F32)) for i in range(8)]

        xn_rows = nc.dram_tensor("xn_rows", [N, C], F32, kind="Internal").ap()
        sorted_x = nc.dram_tensor("sorted_x", [ETABLE * P, C], F32, kind="Internal").ap()
        sorted_y = nc.dram_tensor("sorted_y", [ETILES * P, C], F32, kind="Internal").ap()
        mixed = nc.dram_tensor("mixed", [N, C], F32, kind="Internal").ap()

        ident = keep("ident_sb", [P, P], F32)
        xnT = keep("xnT", [C, N], F32)
        pos = keep("pos", [P, NT], U32)
        w_shared = keep("w_shared", [P, NT], F32)
        w_expert = keep("w_expert", [P, NT], F32)
        tile_expert = keep("tile_expert", [P, ETABLE], I32)

        attn_stack = ExitStack()
        with attn_stack:
            def sb(name, shape, dt):
                return attn_stack.enter_context(nc.sbuf_tensor(name, shape, dt))

            xH = sb("xH", [C, PT], F32R)
            xL = sb("xL", [C, PT], F32R)
            wf = sb("wf", [C, 4, 2, H * L], F32R)
            biases = sb("biases", [P, 4 * G_PER_PAIR + G_PER_PAIR], F32)
            wqk = sb("wqk", [P, P], F32)
            wqk_b = sb("wqk_b", [P, 1], F32)
            wvT = sb("wvT", [C, C], F32)
            wout = sb("wout", [C, C], F32)
            const_row = sb("const_row", [P, C], F32)
            cosr = sb("cosr_sb", [P, T], F32)
            sinr = sb("sinr_sb", [P, T], F32)
            mask = sb("mask_sb", [P, T], F32)
            sumsel = sb("sumsel_sb", [P, 2 * VW], F32)

            prologue(nc, d, bank, sem, ident, xnT, pos, w_shared, w_expert, tile_expert, wf, biases, wqk, wqk_b,
                     wvT, wout, const_row, cosr, sinr, mask, sumsel, xn_rows, sorted_x)
            attention(nc, d, bank, sem, sb, ident, xnT, pos, xH, xL, wf, biases, wqk, wqk_b, wvT, wout, const_row,
                      cosr, sinr, mask, sumsel, xn_rows, sorted_x, mixed)
        experts(nc, d, bank, sem, ident, xnT, pos, w_shared, w_expert, tile_expert, sorted_x, sorted_y, mixed, out)


def prologue(nc, d, bank, sem, ident, xnT, pos, w_shared, w_expert, tile_expert, wf, biases, wqk, wqk_b, wvT, wout,
             const_row, cosr, sinr, mask, sumsel, xn_rows, sorted_x):
    tmp = ExitStack()
    with tmp:
        def sb(name, shape, dt):
            return tmp.enter_context(nc.sbuf_tensor(name, shape, dt))

        x = sb("x", [P, NT, C], F32)
        stats = sb("stats", [P, NT, 6], F32)
        mv = sb("mv", [P, NT, 2], F32)
        sd = sb("sd", [P, NT], F32)
        rstd = sb("rstd", [P, NT], F32)
        wqk_nat = sb("wqk_nat", [P, 2, C], F32)
        spread = sb("spread", [P, 4, H * L], F32)
        kvT = sb("kvT", [P, G_PER_PAIR, C], F32)
        oproj = sb("oproj", [P, G_PER_PAIR, C], F32)
        bqkv = sb("bqkv", [P, 3], F32)
        lat_b = sb("lat_b", [P, 5 * G_PER_PAIR], F32)
        out_b = sb("out_b", [P, 1], F32)
        cprojT = sb("cprojT", [C, C], F32)
        cproj_b = sb("cproj_b", [P, C], F32)
        m1T = sb("m1T", [C, C], F32)
        o_col = sb("o_col", [C, 1], F32)
        o_rep = sb("o_rep", [C, C], F32)
        routerT = sb("routerT", [C, E], F32)
        router_b = sb("router_b", [P, E], F32)
        tri = sb("tri_sb", [P, P], F32)
        ones = sb("ones_sb", [P, P], F32)
        rank = sb("rank_sb", [P, E], F32)
        thresh = sb("thresh_sb", [P, NT], F32)
        tileno = sb("tileno_sb", [P, ETABLE], F32)
        zeros = sb("zeros", [P, 4 * C], F32)
        lg = sb("lg", [P, E, NT], F32)
        pr = sb("pr", [P, E, NT], F32)
        oh = sb("oh", [P, E, NT], F32)
        pm = sb("pm", [P, NT], F32)
        ms = sb("ms", [P, NT], F32)
        tot = sb("tot", [P, E, NT], F32)
        cum = sb("cum", [P, E, NT], F32)
        before = sb("before", [P, E], F32)
        cnt = sb("cnt", [P, E], F32)
        gt = sb("gt", [P, E, NT], F32)
        nt_e = sb("nt_e", [P, E], F32)
        end_e = sb("end_e", [P, E], F32)
        off_e = sb("off_e", [P, E], F32)
        ge = sb("ge", [P, ETABLE, E], F32)
        te = sb("te", [P, ETABLE], F32)
        posf = sb("posf", [P, NT], F32)
        small = sb("small", [P, NT], F32)

        first_in = sem("first_in")
        x_in = [sem(f"x_in{i}") for i in range(4)]
        fold_in = sem("fold_in")
        rest_in = sem("rest_in")
        zeros_set = sem("zeros_set")
        zero_rows = sem("zero_rows")
        norm_step = sem("norm_step")
        sd_ready = sem("sd_ready")
        xn_ready = sem("xn_ready")
        xn_stored = sem("xn_stored")
        xt_ready = sem("xt_ready")
        xt_copied = sem("xt_copied")
        fold_ready = sem("fold_ready")
        fold_high = sem("fold_high")
        fold_low = sem("fold_low")
        bias_ready = sem("bias_ready")
        m1_ready = sem("m1_ready")
        vec = sem("vec")
        o_ready = sem("o_ready")
        o_spread = sem("o_spread")
        wout_ready = sem("wout_ready")
        bias_used = sem("bias_used")
        logits_ready = sem("logits_ready")
        neg_exp = sem("neg_exp")
        l_clipped = sem("l_clipped")
        onehot_ready = sem("onehot_ready")
        prefix_ready = sem("prefix_ready")
        XB = NT // 4
        X3 = d["x"].rearrange("(t p) c -> p t c", p=P)
        FOLD = [(wqk_nat[:], d["wqk_nat"]), (spread[:], d["spread"])]
        REST = [(kvT[:], d["kvT"]), (oproj[:], d["oproj"]), (bqkv[:], d["bqkv"]), (lat_b[:], d["lat_b"]),
                (out_b[:], d["out_b"]), (cprojT[:], d["cprojT"]), (cproj_b[:], d["cproj_b"]),
                (routerT[:], d["routerT"]), (router_b[:], d["router_b"]), (tri[:], d["tri"]), (ones[:], d["ones"]),
                (rank[:], d["rank"]), (thresh[:], d["thresh"]), (tileno[:], d["tileno"]), (wqk[:], d["wqk_bd"]),
                (wqk_b[:], d["wqk_b"]), (wvT[:], d["wvT"]), (cosr[:], d["cosr"]), (sinr[:], d["sinr"]),
                (mask[:], d["mask"]), (sumsel[:], d["sumsel"])]

        with nc.Block() as block:
            @block.sync
            def _(sp):
                sp.dma_start(ident[:], d["ident"]).then_inc(first_in, 16)
                for i in range(4):
                    sp.dma_start(x[:, XB * i:XB * (i + 1), :], X3[:, XB * i:XB * (i + 1), :]).then_inc(x_in[i], 16)
                for dst, src in REST[4:]:
                    sp.dma_start(dst, src).then_inc(rest_in, 16)
                sp.wait_ge(xn_ready, NT)
                sp.dma_start(xn_rows.rearrange("(t p) c -> p t c", p=P), x[:]).then_inc(xn_stored, 16)
                sp.wait_ge(xn_stored, 16)
                sp.wait_ge(zero_rows, 16 * (ETABLE // 4))

            @block.gpsimd
            def _(pool):
                nc.gpsimd.memset(zeros[:], 0.0).then_inc(zeros_set, 1)
                pool.wait_ge(zeros_set, 1)
                for i in range(ETABLE // 4):
                    pool.dma_start(sorted_x[4 * P * i:4 * P * (i + 1), :].rearrange("(p a) c -> p (a c)", p=P),
                                   zeros[:]).then_inc(zero_rows, 16)

            @block.scalar
            def _(act):
                for dst, src in FOLD:
                    act.dma_start(dst, src).then_inc(fold_in, 16)
                for dst, src in REST[:4]:
                    act.dma_start(dst, src).then_inc(rest_in, 16)
                for k in range(4):
                    act.wait_ge(fold_ready, k + 1)
                    nc.scalar.copy(wf[:, k, 0, :], bank[4 + k][:]).then_inc(fold_high, 1)
                act.wait_ge(norm_step, 2)
                nc.scalar.activation(sd[:], sd[:], ACT.Sqrt).then_inc(sd_ready, 1)
                for i in range(NT // 4):
                    act.wait_ge(xt_ready, 4 * i + 4)
                    nc.scalar.copy(xnT[:, 512 * i:512 * (i + 1)], bank[i % 2][:]).then_inc(xt_copied, 1)
                act.wait_ge(l_clipped, 1)
                nc.scalar.activation(pr[:], lg[:], ACT.Exp, scale=-1.0).then_inc(neg_exp, 1)

            @block.tensor
            def _(pe):
                pe.wait_ge(fold_in, 32)
                for k in range(4):
                    nc.tensor.matmul(bank[4 + k][:], wqk_nat[:, k // 2, :], spread[:, k, :],
                                     start=True, stop=True).then_inc(fold_ready, 1)
                pe.wait_ge(rest_in, 16 * len(REST))
                for k in range(5):
                    for g in range(G_PER_PAIR):
                        at = k * G_PER_PAIR + g
                        kind, col = (k, k // 2) if k < 4 else (2, 2)
                        last = nc.tensor.matmul(bank[3][:, at:at + 1], spread[:, kind, P * g:P * (g + 1)],
                                                bqkv[:, col:col + 1], start=True, stop=True)
                last.then_inc(bias_ready, 1)
                for g in range(G_PER_PAIR):
                    last = nc.tensor.matmul(bank[2][:, 0:C], oproj[:, g, :], kvT[:, g, :],
                                            start=(g == 0), stop=(g == G_PER_PAIR - 1))
                last.then_inc(m1_ready, 1)
                pe.wait_ge(vec, 2)
                for g in range(G_PER_PAIR):
                    at = 4 * G_PER_PAIR + g
                    last = nc.tensor.matmul(bank[2][:, C:C + 1], oproj[:, g, :], biases[:, at:at + 1],
                                            start=(g == 0), stop=(g == G_PER_PAIR - 1))
                last.then_inc(o_ready, 1)
                pe.wait_ge(o_spread, 2)
                nc.tensor.matmul(bank[2][:, 2 * C:3 * C], m1T[:], cprojT[:], start=True, stop=True)
                nc.tensor.matmul(bank[2][:, 3 * C:4 * C], o_rep[:], cprojT[:], start=True,
                                 stop=True).then_inc(wout_ready, 1)
                pe.wait_ge(first_in, 16)
                for t in range(NT):
                    pe.wait_ge(xn_ready, t + 1)
                    if t % 4 == 0 and t >= 8:
                        pe.wait_ge(xt_copied, t // 4 - 1)
                    nc.tensor.transpose(bank[t // 4 % 2][:, P * (t % 4):P * (t % 4 + 1)], x[:, t, :],
                                        ident[:]).then_inc(xt_ready, 1)
                pe.wait_ge(bias_used, 1)
                for t in range(NT):
                    pe.wait_ge(xt_copied, t // 4 + 1)
                    last = nc.tensor.matmul(bank[3][:, E * t:E * (t + 1)], xnT[:, P * t:P * (t + 1)], routerT[:],
                                            start=True, stop=True)
                last.then_inc(logits_ready, 1)
                pe.wait_ge(onehot_ready, 1)
                pe.wait_ge(fold_low, 4)
                nc.tensor.matmul(bank[4][:, 0:E * NT], tri[:], oh[:].rearrange("p e t -> p (e t)"),
                                 start=True, stop=True)
                nc.tensor.matmul(bank[5][:, 0:E * NT], ones[:], oh[:].rearrange("p e t -> p (e t)"),
                                 start=True, stop=True).then_inc(prefix_ready, 1)

            @block.vector
            def _(dve):
                chained = [0]

                def chain(ins):
                    chained[0] += 1
                    ins.then_inc(vec, 1)
                    dve.wait_ge(vec, chained[0])

                dve.wait_ge(bias_ready, 1)
                chain(nc.vector.tensor_tensor(biases[:], bank[3][:, 0:5 * G_PER_PAIR], lat_b[:], ALU.add))
                dve.sem_inc(bias_used, 1)
                dve.wait_ge(m1_ready, 1)
                chain(nc.vector.tensor_copy(m1T[:], bank[2][:, 0:C]))
                for k in range(4):
                    dve.wait_ge(fold_high, k + 1)
                    nc.vector.tensor_tensor(wf[:, k, 1, :], bank[4 + k][:], wf[:, k, 0, :].bitcast(F32),
                                            ALU.subtract).then_inc(fold_low, 1)
                dve.wait_ge(o_ready, 1)
                nc.vector.tensor_tensor(o_col[:], bank[2][:, C:C + 1], out_b[:], ALU.add).then_inc(o_spread, 1)
                dve.wait_ge(o_spread, 1)
                nc.vector.tensor_scalar(o_rep[:], ones[:], o_col[:, 0:1], None, ALU.mult).then_inc(o_spread, 1)
                dve.wait_ge(wout_ready, 1)
                nc.vector.tensor_copy(wout[:], bank[2][:, 2 * C:3 * C])
                nc.vector.tensor_tensor(const_row[:], bank[2][:, 3 * C:4 * C], cproj_b[:], ALU.add)

                for t in range(NT):
                    if t % XB == 0:
                        dve.wait_ge(x_in[t // XB], 16)
                    ins = nc.vector.bn_stats(stats[:, t, :], x[:, t, :])
                chain(ins)
                for t in range(NT):
                    ins = nc.vector.bn_aggr(mv[:, t, :], stats[:, t, :])
                ins.then_inc(norm_step, 1)
                dve.wait_ge(norm_step, 1)
                nc.vector.tensor_scalar(sd[:], mv[:, :, 1], 1e-5, None, ALU.add).then_inc(norm_step, 1)
                dve.wait_ge(sd_ready, 1)
                chain(nc.vector.reciprocal(rstd[:], sd[:]))
                for t in range(NT):
                    nc.vector.tensor_scalar(x[:, t, :], x[:, t, :], mv[:, t, 0:1], rstd[:, t:t + 1],
                                            ALU.subtract, ALU.mult).then_inc(xn_ready, 1)

                dve.wait_ge(logits_ready, 1)
                chain(nc.vector.tensor_tensor(lg[:], bank[3][:, 0:E * NT].rearrange("p (t e) -> p e t", e=E),
                                              router_b[:].unsqueeze(2).to_broadcast([P, E, NT]), ALU.add))
                nc.vector.tensor_scalar(lg[:], lg[:], -50.0, 50.0, ALU.max, ALU.min).then_inc(l_clipped, 1)
                dve.wait_ge(neg_exp, 1)
                chain(nc.vector.tensor_scalar(pr[:], pr[:], 1.0, None, ALU.add))
                chain(nc.vector.reciprocal(pr[:], pr[:]))
                chain(nc.vector.tensor_reduce(pm[:], pr[:].rearrange("p e t -> p t e"), AX.X, ALU.max))
                chain(nc.vector.tensor_tensor(oh[:], pr[:], pm[:].unsqueeze(1).to_broadcast([P, E, NT]),
                                              ALU.is_equal))
                chain(nc.vector.tensor_tensor(oh[:], oh[:], rank[:].unsqueeze(2).to_broadcast([P, E, NT]), ALU.mult))
                chain(nc.vector.tensor_reduce(ms[:], oh[:].rearrange("p e t -> p t e"), AX.X, ALU.max))
                nc.vector.tensor_tensor(oh[:], oh[:], ms[:].unsqueeze(1).to_broadcast([P, E, NT]),
                                        ALU.is_equal).then_inc(onehot_ready, 1)
                chain(nc.vector.tensor_scalar(pm[:], pm[:], 1e-8, 1.0, ALU.max, ALU.min))
                chain(nc.vector.tensor_scalar(small[:], pm[:], 0.5, 1e-8, ALU.add, ALU.add))
                chain(nc.vector.tensor_scalar(small[:], small[:], 0.5, 2.0, ALU.max, ALU.min))
                chain(nc.vector.reciprocal(small[:], small[:]))
                nc.vector.tensor_scalar(w_shared[:], small[:], 0.5, None, ALU.mult)
                nc.vector.tensor_tensor(w_expert[:], small[:], pm[:], ALU.mult)
                dve.wait_ge(prefix_ready, 1)
                chain(nc.vector.tensor_copy(tot[:].rearrange("p e t -> p (e t)"), bank[5][:, 0:E * NT]))
                chain(nc.vector.tensor_tensor_scan(cum[:].rearrange("p e t -> p (e t)"),
                                                   tot[:].rearrange("p e t -> p (e t)"),
                                                   tot[:].rearrange("p e t -> p (e t)"), 0.0, ALU.add, ALU.bypass))
                nc.vector.memset(before[:, 0:1], 0.0)
                chain(nc.vector.tensor_copy(before[:, 1:E], cum[:, 0:E - 1, NT - 1]))
                chain(nc.vector.tensor_tensor(cnt[:], cum[:, :, NT - 1], before[:], ALU.subtract))
                chain(nc.vector.tensor_tensor(gt[:], cnt[:].unsqueeze(2).to_broadcast([P, E, NT]),
                                              thresh[:].unsqueeze(1).to_broadcast([P, E, NT]), ALU.is_gt))
                chain(nc.vector.tensor_reduce(nt_e[:], gt[:], AX.X, ALU.add))
                chain(nc.vector.tensor_tensor_scan(end_e[:], nt_e[:], nt_e[:], 0.0, ALU.add, ALU.bypass))
                chain(nc.vector.tensor_tensor(ge[:], tileno[:].unsqueeze(2).to_broadcast([P, ETABLE, E]),
                                              end_e[:].unsqueeze(1).to_broadcast([P, ETABLE, E]), ALU.is_ge))
                chain(nc.vector.tensor_reduce(te[:], ge[:], AX.X, ALU.add))
                nc.vector.tensor_scalar(tile_expert[:], te[:], float(E - 1), None, ALU.min)
                chain(nc.vector.tensor_tensor(off_e[:], end_e[:], nt_e[:], ALU.subtract))
                chain(nc.vector.scalar_tensor_tensor(off_e[:], off_e[:], float(P), before[:], ALU.mult,
                                                     ALU.subtract))
                chain(nc.vector.tensor_tensor(cum[:], cum[:], tot[:], ALU.subtract))
                chain(nc.vector.tensor_tensor(cum[:].rearrange("p e t -> p (e t)"),
                                              cum[:].rearrange("p e t -> p (e t)"), bank[4][:, 0:E * NT], ALU.add))
                chain(nc.vector.tensor_tensor(cum[:], cum[:], off_e[:].unsqueeze(2).to_broadcast([P, E, NT]),
                                              ALU.add))
                chain(nc.vector.tensor_tensor(cum[:], cum[:], oh[:], ALU.mult))
                chain(nc.vector.tensor_reduce(posf[:], cum[:].rearrange("p e t -> p t e"), AX.X, ALU.add))
                nc.vector.tensor_copy(pos[:], posf[:])


def attention(nc, d, bank, sem, sb, ident, xnT, pos, xH, xL, wf, biases, wqk, wqk_b, wvT, wout, const_row, cosr,
              sinr, mask, sumsel, xn_rows, sorted_x, mixed):
    Kst = sb("Kst", [P, SLOTS, PT], F32R)
    Qst = sb("Qst", [P, SLOTS, PT], F32R)
    dKH = sb("dKH", [P, 2, PT], F32R)
    dKL = sb("dKL", [P, 2, PT], F32R)
    dQH = sb("dQH", [P, 2, PT], F32R)
    dQL = sb("dQL", [P, 2, PT], F32R)
    tk1 = sb("tk1", [P, PT], F32)
    tq1 = sb("tq1", [P, PT], F32)
    t2 = sb("t2", [P, PT], F32)
    prob = sb("prob", [P, 2, 2, PCOLS], F32)
    v = sb("v", [P, 3, 2 * QT, HG, VW], F32)
    ysb = sb("ysb", [P, T], F32)
    yn = sb("yn", [P, 2, 2 * QT, C], F32)
    yT = sb("yT", [C, QT * P], F32)
    xres = sb("xres", [P, 2 * QT, C], F32)
    scratch = sb("scratch", [P, 2, T], BF16)
    mx = sb("mx", [P, 2, 2 * QT], F32)
    nm = sb("nm", [P, 2, 4 * QT], F32R)
    nmT = sb("nmT", [4 * QT, 2, P], F32R)
    rz = sb("rz", [P, QT, 2], F32)
    xrow = sb("xrow", [P, 4, C], F32)

    S = bank[0:2]
    ST = bank[2:4]
    Y, PA, PB, M = bank[4], bank[5], bank[6], bank[7]

    set_up = sem("set_up")
    y_clear = sem("y_clear")
    xh_ready, xl_ready = sem("xh_ready"), sem("xl_ready")
    pa_ready, pb_ready, pa_used, pb_used = sem("pa_ready"), sem("pb_ready"), sem("pa_used"), sem("pb_used")
    k_roped, q_roped, kh_ready, kl_ready, qh_ready = (sem("k_roped"), sem("q_roped"), sem("kh_ready"),
                                                      sem("kl_ready"), sem("qh_ready"))
    filled = [sem(f"filled{i}") for i in range(SLOTS)]
    neg_in = [sem(f"neg_in{i}") for i in range(2)]
    s_ready, s_max = sem("s_ready"), sem("s_max")
    neg_high, neg_ready, negT_ready, negT_copied = (sem("neg_high"), sem("neg_ready"), sem("negT_ready"),
                                                    sem("negT_copied"))
    st_ready, exp_done, cut_done, pv_done = sem("st_ready"), sem("exp_done"), sem("cut_done"), sem("pv_done")
    y_copied, z_ready, rz_ready, z_used = sem("y_copied"), sem("z_ready"), sem("rz_ready"), sem("z_used")
    ynT_ready, ynT_copied, o_ready2, o_added = sem("ynT_ready"), sem("ynT_copied"), sem("o_ready2"), sem("o_added")
    xres_in, xres_const, mixed_out = sem("xres_in"), sem("xres_const"), sem("mixed_out")
    row_in = [sem(f"row_in{i}") for i in range(4)]
    row_sorted = [sem(f"row_sorted{i}") for i in range(4)]

    FIRST, LAST = -2 * HG - 2, STEPS + 5

    def chunk(n):
        G = n // HG + 2
        return (G, n % HG) if 0 <= G < GROUPS and n >= -2 * HG else (None, None)

    def split_pair(n):
        return (n + 10) // H if (n + 10) % H == 0 and (n + 10) // H < PAIRS else None

    def out_part(n):
        pair, part = n // H - 1, n % H - 1
        return (pair, part) if 0 <= pair < PAIRS and 0 <= part < 4 else (None, None)

    with nc.Block() as block:
        @block.sync
        def _(sp):
            for n in range(FIRST, LAST):
                m = n + HG
                if 0 <= m < STEPS:
                    G, h, slot = m // HG, m % HG, m % SLOTS
                    if h == 0:
                        sp.wait_ge(kh_ready, G + 1)
                        sp.wait_ge(kl_ready, G + 1)
                        sp.wait_ge(qh_ready, 2 * G + 2)
                        sp.wait_ge(pa_used, PA_USES * G + 5)
                        sp.wait_ge(pb_used, PB_USES * G + 6)
                    if m == 0:
                        sp.wait_ge(set_up, 4)
                    if m >= SLOTS:
                        sp.wait_ge(st_ready, 8 * (m - SLOTS) + 8)
                    rows = slice(L * h, L * h + L)
                    for r, (kd, qd) in enumerate(((dKH, dQH), (dKL, dQH), (dKH, dQL))):
                        sp.dma_start(Kst[L * r:L * r + L, slot, :].bitcast(F32), kd[rows, G % 2, :].bitcast(F32)).then_inc(filled[slot], 16)
                        sp.dma_start(Qst[L * r:L * r + L, slot, :].bitcast(F32), qd[rows, G % 2, :].bitcast(F32)).then_inc(filled[slot], 16)
                if 0 <= n < NT:
                    if n >= 4:
                        sp.wait_ge(row_sorted[n % 4], 16 * (n // 4))
                    sp.dma_start(xrow[:, n % 4, :], xn_rows[P * n:P * (n + 1), :]).then_inc(row_in[n % 4], 16)
                m = n + 1
                if 0 <= m < STEPS:
                    sp.wait_ge(negT_copied, m + 1)
                    if m < 2:
                        sp.wait_ge(set_up, 4)
                    if m >= SLOTS:
                        sp.wait_ge(st_ready, 8 * (m - SLOTS) + 8)
                    sp.dma_start(Qst[KROWS:SROWS, m % SLOTS, :].bitcast(F32), nmT[:, m % 2, :].bitcast(F32)).then_inc(neg_in[m % 2], 16)
                if n % H == 7 and 0 <= n < STEPS:
                    pair = n // H
                    if pair:
                        sp.wait_ge(mixed_out, 16 * pair)
                    sp.dma_start(xres[:], d["x"][PT * pair:PT * (pair + 1), :].rearrange("(t p) c -> p t c", p=P)
                                 ).then_inc(xres_in, 16)
                pair, part = out_part(n)
                if part == 3:
                    sp.wait_ge(o_added, 2 * pair + 2)
                    sp.dma_start(mixed[PT * pair:PT * (pair + 1), :].rearrange("(t p) c -> p t c", p=P),
                                 xres[:]).then_inc(mixed_out, 16)
            sp.wait_ge(mixed_out, 16 * PAIRS)
            for i in range(4):
                sp.wait_ge(row_sorted[i], 16 * (NT // 4))

        @block.gpsimd
        def _(pool):
            nc.gpsimd.memset(Kst[KROWS:P, :, :].bitcast(F32), 1.0).then_inc(set_up, 1)
            pool.wait_ge(set_up, 1)
            nc.gpsimd.memset(v[:, :, :, :, HD:VW], 1.0).then_inc(set_up, 1)
            for par in range(2):
                nc.gpsimd.memset(prob[:, par, :, POFF[1]:POFF[1] + P], 0.0).then_inc(set_up, 1)
            for n in range(FIRST, LAST):
                pair = split_pair(n)
                if pair is not None:
                    pool.wait_ge(xh_ready, pair + 1)
                    nc.gpsimd.tensor_tensor(xL[:], xnT[:, PT * pair:PT * (pair + 1)], xH[:].bitcast(F32),
                                            ALU.subtract).then_inc(xl_ready, 1)
                G, part = chunk(n)
                if part == 1:
                    pool.wait_ge(pa_used, PA_USES * G + 2)
                    pool.wait_ge(pb_used, PB_USES * G + 2)
                    nc.gpsimd.tensor_tensor(tk1[:], tk1[:], t2[:], ALU.add).then_inc(k_roped, 1)
                if part == 2:
                    pool.wait_ge(pa_used, PA_USES * G + 4)
                    pool.wait_ge(pb_used, PB_USES * G + 4)
                    nc.gpsimd.tensor_tensor(tq1[:], tq1[:], t2[:], ALU.add).then_inc(q_roped, 1)
                if part == 3:
                    pool.wait_ge(kh_ready, G + 1)
                    nc.gpsimd.tensor_tensor(dKL[:, G % 2, :], tk1[:], dKH[:, G % 2, :].bitcast(F32),
                                            ALU.subtract).then_inc(kl_ready, 1)
                if n % H == 11 and 0 <= n < STEPS:
                    pair = n // H
                    pool.wait_ge(xres_in, 16 * (pair + 1))
                    nc.gpsimd.tensor_tensor(xres[:], xres[:], const_row[:].unsqueeze(1).to_broadcast([P, 2 * QT, C]),
                                            ALU.add).then_inc(xres_const, 1)
                if 0 <= n < STEPS:
                    for j in range(QT):
                        pool.wait_ge(exp_done, 8 * n + 2 * j + 2)
                        at = POFF[j] + (P if j == 1 else 0)
                        diag = prob[:, n % 2, :, at:at + P]
                        nc.gpsimd.affine_select(out=diag, in_=diag, compare_op=ALU.is_ge, fill=0.0, base=0,
                                                pattern=[[0, 2], [1, P]], channel_multiplier=-1
                                                ).then_inc(cut_done, 1)
                if 0 <= n < NT:
                    pool.wait_ge(row_in[n % 4], 16 * (n // 4 + 1))
                    pool.indirect_dma_start(sorted_x, bass.IndirectOffsetOnAxis(pos[:, n:n + 1], 0),
                                            xrow[:, n % 4, :], None).then_inc(row_sorted[n % 4], 16)

        @block.scalar
        def _(act):
            for n in range(FIRST, LAST):
                pair = split_pair(n)
                if pair is not None:
                    if pair:
                        act.wait_ge(pa_ready, PA_USES * (G_PER_PAIR * pair - 1) + 4)
                        act.wait_ge(pb_ready, PB_USES * (G_PER_PAIR * pair - 1) + 4)
                        act.wait_ge(xl_ready, pair)
                    nc.scalar.copy(xH[:], xnT[:, PT * pair:PT * (pair + 1)]).then_inc(xh_ready, 1)
                G, part = chunk(n)
                for i in range(8):
                    if 0 <= n < STEPS:
                        if i == 0 and n >= 2:
                            act.wait_ge(pv_done, n - 1)
                        j, b = i // 2, i % 2
                        act.wait_ge(st_ready, 8 * n + i + 1)
                        lo, q0 = P * j, min(P * j, T - 2 * P)
                        at = POFF[j] + (P if j == 1 else 0)
                        nc.scalar.activation(prob[:, n % 2, b, at:at + T - lo], ST[i % 2][:, lo - q0:T - q0],
                                             ACT.Exp, scale=SCALE).then_inc(exp_done, 1)
                    m = n + 1
                    if i == 1 and 0 <= m < STEPS:
                        act.wait_ge(negT_ready, m + 1)
                        if m >= 2:
                            act.wait_ge(neg_in[m % 2], 16 * (m // 2))
                        nc.scalar.copy(nmT[:, m % 2, :], M[0:4 * QT, 0:P]).then_inc(negT_copied, 1)
                    if i == 3 and 0 <= n - 1 < STEPS:
                        act.wait_ge(pv_done, n)
                        if n >= 2:
                            act.wait_ge(z_ready, n - 1)
                        nc.scalar.copy(ysb[:], Y[:]).then_inc(y_copied, 1)
                    if i == 5 and part == 1:
                        act.wait_ge(k_roped, G + 1)
                        if G >= 2:
                            for h in range(HG):
                                m = HG * (G - 2) + h
                                act.wait_ge(filled[m % SLOTS], 96 * (m // SLOTS + 1))
                        nc.scalar.copy(dKH[:, G % 2, :], tk1[:]).then_inc(kh_ready, 1)
                    if part == 3 and i in (5, 6):
                        f = i - 5
                        if f == 0:
                            act.wait_ge(pa_ready, PA_USES * G + 5)
                        else:
                            act.wait_ge(pb_ready, PB_USES * G + 6)
                        nc.scalar.activation(dQH[:, G % 2, T * f:T * (f + 1)], (PA, PB)[f][:], ACT.Identity,
                                             bias=wqk_b[:, 0:1]).then_inc(qh_ready, 1)
                pair, part = out_part(n)
                if part in (0, 2):
                    act.wait_ge(ynT_ready, 2 * pair + part // 2 + 1)
                    if 2 * pair + part // 2:
                        act.wait_ge(o_ready2, 2 * pair + part // 2)
                    nc.scalar.copy(yT[:], M[:]).then_inc(ynT_copied, 1)

        @block.tensor
        def _(pe):
            issued = {"neg": 0, "z": 0, "yt": 0, "o": 0}

            def m_free():
                for key, s in (("neg", negT_copied), ("z", z_used), ("yt", ynT_copied), ("o", o_added)):
                    if issued[key]:
                        pe.wait_ge(s, issued[key])

            def pv(m, j):
                h = m % HG
                vs = v[:, m // HG % 3]
                if j == 0:
                    pe.wait_ge(pb_used, PB_USES * (m // HG) + 5)
                    if m:
                        pe.wait_ge(y_copied, m)
                    else:
                        pe.wait_ge(y_clear, 1)
                pe.wait_ge(cut_done, 4 * m + j + 1)
                for b in range(2):
                    q = 2 * b + j % 2
                    c0 = T - PW[j]
                    last = nc.tensor.matmul(Y[L * q:L * q + VW, c0:T], vs[:, QT * b + j, h, :],
                                            prob[:, m % 2, b, POFF[j]:POFF[j] + PW[j]],
                                            start=(j < 2), stop=(j >= 2), skip_group_check=True)
                if j == QT - 1:
                    last.then_inc(pv_done, 1)

            def project(G, part, piece):
                g = G % G_PER_PAIR
                cols = slice(P * g, P * (g + 1))
                f, ab = piece // 2, piece % 2
                if part == 0 and piece == 0:
                    pe.wait_ge(xh_ready, G // G_PER_PAIR + 1)
                    pe.wait_ge(xl_ready, G // G_PER_PAIR + 1)
                kd = 2 - 2 * part + ab
                bk, used, rdy, use = ((PA, pa_used, pa_ready, PA_USES * G + 2 * part + f),
                                      (PB, pb_used, pb_ready, PB_USES * G + 2 * part + f))[ab]
                if use:
                    pe.wait_ge(used, use)
                xs = slice(T * f, T * (f + 1))
                nc.tensor.matmul(bk[:], wf[:, kd, 0, cols], xH[:, xs], start=True, stop=False)
                nc.tensor.matmul(bk[:], wf[:, kd, 1, cols], xH[:, xs], start=False, stop=False)
                nc.tensor.matmul(bk[:], wf[:, kd, 0, cols], xL[:, xs], start=False, stop=True).then_inc(rdy, 1)

            for n in range(FIRST, LAST):
                G, part = chunk(n)
                for i in range(8):
                    if 0 <= n + 2 < STEPS:
                        m = n + 2
                        k = 8 * m + i
                        b, q = i // QT, i % QT
                        if i == 0:
                            pe.wait_ge(filled[m % SLOTS], 96 * (m // SLOTS + 1))
                        if k >= 2:
                            pe.wait_ge(s_max, k - 1)
                        w = max(P * (q + 1), 2 * P)
                        nc.tensor.matmul(S[i % 2][:, 0:w],
                                         Qst[0:KROWS, m % SLOTS, T * b + P * q:T * b + P * (q + 1)],
                                         Kst[0:KROWS, m % SLOTS, T * b:T * b + w],
                                         start=True, stop=True).then_inc(s_ready, 1)
                    if 0 <= n < STEPS:
                        k = 8 * n + i
                        j, b = i // 2, i % 2
                        q0 = min(P * j, T - 2 * P)
                        if i == 0:
                            pe.wait_ge(neg_in[n % 2], 16 * (n // 2 + 1))
                        if k >= 2:
                            pe.wait_ge(exp_done, k - 1)
                        nc.tensor.matmul(ST[i % 2][:, 0:T - q0],
                                         Kst[0:SROWS, n % SLOTS, T * b + P * j:T * b + P * (j + 1)],
                                         Qst[0:SROWS, n % SLOTS, T * b + q0:T * (b + 1)],
                                         start=True, stop=True).then_inc(st_ready, 1)
                    if 0 <= n - 1 < STEPS:
                        if i in (0, 1, 2):
                            pv(n - 1, i)
                        if i == 2:
                            pv(n - 1, 3)
                    if i == 1 and 0 <= n + 1 < STEPS:
                        m = n + 1
                        pe.wait_ge(neg_ready, m + 1)
                        m_free()
                        nc.tensor.transpose(M[0:4 * QT, 0:P], nm[:, m % 2, :].bitcast(F32), ident[:]
                                            ).then_inc(negT_ready, 1)
                        issued["neg"] += 1
                    if part in (0, 1) and i >= 4:
                        project(G, part, i - 4)
                    if part == 2 and i == 4:
                        pe.wait_ge(pb_used, PB_USES * G + 4)
                        for t in range(2 * QT):
                            tok = PT * (G // G_PER_PAIR) + P * t
                            g = G % G_PER_PAIR
                            last = nc.tensor.matmul(PB[:, HG * HD * t:HG * HD * (t + 1)], xnT[:, tok:tok + P],
                                                    wvT[:, HG * HD * g:HG * HD * (g + 1)], start=True, stop=True,
                                                    skip_group_check=True)
                        last.then_inc(pb_ready, 1)
                    if part == 3 and i in (4, 5):
                        f = i - 4
                        if f == 0:
                            pe.wait_ge(q_roped, G + 1)
                            pe.wait_ge(pa_used, PA_USES * G + 4)
                        else:
                            pe.wait_ge(pb_used, PB_USES * G + 5)
                        nc.tensor.matmul((PA, PB)[f][:], wqk[:], tq1[:, T * f:T * (f + 1)], start=True,
                                         stop=True).then_inc((pa_ready, pb_ready)[f], 1)
                if 0 <= n - 1 < STEPS:
                    pe.wait_ge(y_copied, n)
                    m_free()
                    for q in range(QT):
                        last = nc.tensor.matmul(M[:, 2 * VW * q:2 * VW * (q + 1)], ysb[:, P * q:P * (q + 1)],
                                                sumsel[:], start=True, stop=True, skip_group_check=True)
                    last.then_inc(z_ready, 1)
                    issued["z"] += 1
                pair, part = out_part(n)
                if part in (0, 2):
                    m_free()
                    for t in range(QT):
                        last = nc.tensor.transpose(M[:, P * t:P * (t + 1)], yn[:, pair % 2, 2 * part + t, :],
                                                   ident[:])
                    last.then_inc(ynT_ready, 1)
                    issued["yt"] += 1
                if part in (1, 3):
                    m_free()
                    for t in range(QT):
                        last = nc.tensor.matmul(M[:, C * t:C * (t + 1)], yT[:, P * t:P * (t + 1)], wout[:],
                                                start=True, stop=True, skip_group_check=True)
                    last.then_inc(o_ready2, 1)
                    issued["o"] += 1

        @block.vector
        def _(dve):
            nc.vector.memset(Y[:], 0.0).then_inc(y_clear, 1)

            def rope(G, part, piece):
                g = G % G_PER_PAIR
                t1 = (tk1, tq1)[part]
                if piece == 0:
                    if part == 0 and G:
                        dve.wait_ge(kl_ready, G)
                        dve.wait_ge(q_roped, G)
                    if part == 1:
                        dve.wait_ge(k_roped, G + 1)
                        if G:
                            dve.wait_ge(pa_ready, PA_USES * G)
                            dve.wait_ge(pb_ready, PB_USES * G)
                f, ab = piece // 2, piece % 2
                kind = 2 - 2 * part + ab
                bias = biases[:, kind * G_PER_PAIR + g:kind * G_PER_PAIR + g + 1]
                xs = slice(T * f, T * (f + 1))
                if ab == 0:
                    dve.wait_ge(pa_ready, PA_USES * G + 2 * part + f + 1)
                    nc.vector.scalar_tensor_tensor(t1[:, xs], PA[:], bias, cosr[:], ALU.add, ALU.mult
                                                   ).then_inc(pa_used, 1)
                else:
                    dve.wait_ge(pb_ready, PB_USES * G + 2 * part + f + 1)
                    nc.vector.scalar_tensor_tensor(t2[:, xs], PB[:], bias, sinr[:], ALU.add, ALU.mult
                                                   ).then_inc(pb_used, 1)

            for n in range(FIRST, LAST):
                G, part = chunk(n)
                for i in range(8):
                    if 0 <= n + 2 < STEPS:
                        m = n + 2
                        q = i % QT
                        w = P * (q + 1)
                        dve.wait_ge(s_ready, 8 * m + i + 1)
                        if 8 * m + i >= 2:
                            dve.wait_ge(s_max, 8 * m + i - 1)
                        nc.vector.tensor_tensor_reduce(scratch[:, i % 2, 0:w], S[i % 2][:, 0:w], mask[:, T - w:T],
                                                       1.0, MASKED, ALU.add, ALU.max, mx[:, m % 2, i:i + 1]
                                                       ).then_inc(s_max, 1)
                    if part in (0, 1) and i >= 4:
                        rope(G, part, i - 4)
                    if part == 2 and i == 5:
                        dve.wait_ge(pb_ready, PB_USES * G + 5)
                        if G >= 3:
                            dve.wait_ge(pv_done, HG * (G - 2))
                        nc.vector.tensor_copy(v[:, G % 3, :, :, 0:HD].rearrange("p t h d -> p (t h) d"),
                                              PB[:, 0:2 * QT * HG * HD].rearrange("p (t d) -> p t d", d=HD)
                                              ).then_inc(pb_used, 1)
                    if part == 3 and i in (6, 7):
                        f = i - 6
                        xs = slice(T * f, T * (f + 1))
                        dve.wait_ge(qh_ready, 2 * G + f + 1)
                        nc.vector.scalar_tensor_tensor(dQL[:, G % 2, xs], (PA, PB)[f][:], wqk_b[:, 0:1],
                                                       dQH[:, G % 2, xs].bitcast(F32), ALU.add, ALU.subtract
                                                       ).then_inc((pa_used, pb_used)[f], 1)
                if 0 <= n + 2 < STEPS:
                    m = n + 2
                    dve.wait_ge(s_max, 8 * m + 8)
                    if m >= 2:
                        dve.wait_ge(negT_ready, m - 1)
                    nc.vector.tensor_scalar(nm[:, m % 2, 0:2 * QT], mx[:, m % 2, :], -1.0, None, ALU.mult
                                            ).then_inc(neg_high, 1)
                    dve.wait_ge(neg_high, m + 1)
                    nc.vector.scalar_tensor_tensor(nm[:, m % 2, 2 * QT:4 * QT], mx[:, m % 2, :], -1.0,
                                                   nm[:, m % 2, 0:2 * QT].bitcast(F32), ALU.mult, ALU.subtract
                                                   ).then_inc(neg_ready, 1)
                if 0 <= n - 1 < STEPS:
                    m = n - 1
                    Z = M[:, 0:2 * VW * QT].rearrange("p (q b c) -> p q b c", q=QT, b=2)
                    dve.wait_ge(z_ready, m + 1)
                    nc.vector.reciprocal(rz[:], Z[:, :, :, HD]).then_inc(rz_ready, 1)
                    dve.wait_ge(rz_ready, m + 1)
                    pair, head = m // H, m % H
                    if head == 0 and pair >= 2:
                        dve.wait_ge(ynT_ready, 2 * (pair - 1))
                    o = yn[:, pair % 2, :, HD * head:HD * (head + 1)].rearrange("p (b q) c -> p q b c", b=2)
                    nc.vector.tensor_tensor(o, Z[:, :, :, 0:HD], rz[:].unsqueeze(3).to_broadcast([P, QT, 2, HD]),
                                            ALU.mult).then_inc(z_used, 1)
                pair, part = out_part(n)
                if part in (1, 3):
                    dve.wait_ge(o_ready2, 2 * pair + part // 2 + 1)
                    dve.wait_ge(xres_const, pair + 1)
                    half = xres[:, 2 * (part - 1):2 * (part - 1) + QT, :].rearrange("p t c -> p (t c)")
                    nc.vector.tensor_tensor(half, half, M[:], ALU.add).then_inc(o_added, 1)


def experts(nc, d, bank, sem, ident, xnT, pos, w_shared, w_expert, tile_expert, sorted_x, sorted_y, mixed, out):
    tmp = ExitStack()
    with tmp:
        def sb(name, shape, dt):
            return tmp.enter_context(nc.sbuf_tensor(name, shape, dt))

        w13 = sb("w13", [C, (E + 1), 2 * I], F32)
        w2 = sb("w2", [P, (E + 1), 3, C], F32)
        xs = sb("xs", [P, ETABLE, C], F32)
        xsT = sb("xsT", [C, 2, P], F32)
        g1 = sb("g1", [P, 2, I], F32)
        gg = sb("gg", [P, 2, I], F32)
        gT = sb("gT", [P, 2, 3, P], F32)
        ye = sb("ye", [P, ETILES, C], F32)
        h1 = sb("h1", [P, 2, TC], F32)
        hT = sb("hT", [P, 2, 3, TC], F32)
        acc = sb("acc", [P, NT, C], F32)
        yg = sb("yg", [P, NT, C], F32)

        shared_in, w_in, xs_in, acc_in = sem("shared_in"), sem("w_in"), sem("xs_in"), sem("acc_in")
        xsT_ready, xsT_copied = sem("xsT_ready"), sem("xsT_copied")
        h_ready, silu_done, gate_done = sem("h_ready"), sem("silu_done"), sem("gate_done")
        gT_ready, gT_copied, y_ready, y_copied = (sem("gT_ready"), sem("gT_copied"), sem("ye_ready"),
                                                  sem("ye_copied"))
        y_out, gathered = sem("y_out"), sem("gathered")
        sh_ready, sh_silu, sh_gate = sem("sh_ready"), sem("sh_silu"), sem("sh_gate")
        so_ready, so_added, e_added, out_done = sem("so_ready"), sem("so_added"), sem("e_added"), sem("out_done")
        XT, Y, GT, SY = bank[4], bank[5], bank[6:8], bank[6:8]

        xs_rows = sorted_x.rearrange("(t p) c -> p t c", p=P)
        sy_rows = sorted_y.rearrange("(t p) c -> p t c", p=P)
        WL = 4
        XL = 5
        XW = ETABLE // XL

        with nc.Block() as block:
            @block.sync
            def _(sp):
                sp.dma_start(w13[:, E, :], d["w13"][:, E, :]).then_inc(shared_in, 16)
                sp.dma_start(w2[:, E, :, :], d["w2"][:, E, :, :]).then_inc(shared_in, 16)
                for i in range(XL):
                    sp.dma_start(xs[:, XW * i:XW * (i + 1), :], xs_rows[:, XW * i:XW * (i + 1), :]
                                 ).then_inc(xs_in, 16)
                sp.dma_start(acc[:], mixed.rearrange("(t p) c -> p t c", p=P)).then_inc(acc_in, 16)
                for i in range(0, E, 2):
                    j = min(i + 2, E)
                    sp.dma_start(w13[:, i:j, :], d["w13"][:, i:j, :]).then_inc(w_in, 16)
                    sp.dma_start(w2[:, i:j, :, :], d["w2"][:, i:j, :, :]).then_inc(w_in, 16)
                for t in range(1, ETILES, 2):
                    sp.wait_ge(y_copied, t + 1)
                    sp.dma_start(sy_rows[:, t - 1:t + 1, :], ye[:, t - 1:t + 1, :]).then_inc(y_out, 16)
                for c in range(CHUNKS):
                    sp.wait_ge(e_added, c + 1)
                    sp.dma_start(out[TC * c:TC * (c + 1), :].rearrange("(t p) c -> p t c", p=P),
                                 acc[:, TT * c:TT * (c + 1), :]).then_inc(out_done, 16)
                sp.wait_ge(out_done, 16 * CHUNKS)

            @block.gpsimd
            def _(pool):
                pool.wait_ge(y_out, 16 * (ETILES // 2))
                for t in range(NT):
                    pool.indirect_dma_start(yg[:, t, :], None, sorted_y,
                                            bass.IndirectOffsetOnAxis(pos[:, t:t + 1], 0)).then_inc(gathered, 16)
                    if t % 4 == 3:
                        pool.wait_ge(gathered, 16 * (t + 1))

            @block.scalar
            def _(act):
                def shared_silu(c):
                    for k in range(3):
                        u = 3 * c + k
                        act.wait_ge(sh_ready, u + 1)
                        if u >= 2:
                            act.wait_ge(sh_gate, u - 1)
                        nc.scalar.activation(h1[0:IC[k], u % 2, :], bank[2 * (u % 2)][0:IC[k], :], ACT.Silu
                                             ).then_inc(sh_silu, 1)

                def copy_xT(t):
                    act.wait_ge(xsT_ready, t + 1)
                    if t >= 2:
                        act.wait_ge(h_ready, t - 1)
                    nc.scalar.copy(xsT[:, t % 2, :], XT[:, P * (t % 2):P * (t % 2 + 1)]).then_inc(xsT_copied, 1)

                for c in range(CHUNKS // 2):
                    shared_silu(c)
                for t in range(2):
                    copy_xT(t)
                for t in range(ETILES + 2):
                    if t < ETILES:
                        act.wait_ge(h_ready, t + 1)
                        if t >= 2:
                            act.wait_ge(gate_done, t - 1)
                        nc.scalar.activation(g1[:, t % 2, :], bank[2 * (t % 2)][:, 0:I], ACT.Silu
                                             ).then_inc(silu_done, 1)
                    if t + 2 < ETILES:
                        copy_xT(t + 2)
                    if t >= 2:
                        u = t - 2
                        act.wait_ge(y_ready, u + 1)
                        nc.scalar.copy(ye[:, u, :], Y[:, P * (u % 2):P * (u % 2 + 1)]).then_inc(y_copied, 1)
                for c in range(CHUNKS // 2, CHUNKS):
                    shared_silu(c)

            @block.tensor
            def _(pe):
                def shared_hidden(c):
                    for k in range(3):
                        u = 3 * c + k
                        if u >= 2:
                            pe.wait_ge(sh_gate, u - 1)
                        for half in range(2):
                            last = nc.tensor.matmul(bank[2 * (u % 2) + half][0:IC[k], :],
                                                    w13[:, E, half * I + P * k:half * I + P * k + IC[k]],
                                                    xnT[:, TC * c:TC * (c + 1)], start=True, stop=True)
                        last.then_inc(sh_ready, 1)

                def shared_out(c):
                    pe.wait_ge(sh_gate, 3 * c + 3)
                    if c >= 2:
                        pe.wait_ge(so_added, c - 1)
                    for t in range(TT):
                        for k in range(3):
                            last = nc.tensor.matmul(SY[c % 2][:, C * t:C * (t + 1)],
                                                    hT[0:IC[k], c % 2, k, P * t:P * (t + 1)],
                                                    w2[0:IC[k], E, k, :], start=(k == 0), stop=(k == 2),
                                                    skip_group_check=True)
                    last.then_inc(so_ready, 1)

                def x_transpose(t):
                    pe.wait_ge(xs_in, 16 * XL)
                    if t >= 1:
                        pe.wait_ge(xsT_copied, t)
                    nc.tensor.transpose(XT[:, P * (t % 2):P * (t % 2 + 1)], xs[:, t, :], ident[:]
                                        ).then_inc(xsT_ready, 1)

                pe.wait_ge(shared_in, 32)
                half_chunks = CHUNKS // 2
                for c in range(half_chunks):
                    shared_hidden(c)
                    if c:
                        shared_out(c - 1)
                x_transpose(0)
                x_transpose(1)
                shared_out(half_chunks - 1)
                pe.wait_ge(w_in, 16 * 2 * WL)
                e_of = {}
                for t in range(ETILES + 2):
                    if t < ETILES:
                        e = pe.value_load(tile_expert[0:1, t:t + 1], min_val=0, max_val=E - 1)
                        e_of[t] = e
                        pe.wait_ge(xsT_copied, t + 1)
                        if t >= 2:
                            pe.wait_ge(gate_done, t - 1)
                        else:
                            pe.wait_ge(sh_gate, 3 * half_chunks)
                        nc.tensor.matmul(bank[2 * (t % 2)][:, 0:I], xsT[:, t % 2, :], w13[:, bass.ds(e, 1), 0:I],
                                         start=True, stop=True)
                        nc.tensor.matmul(bank[2 * (t % 2) + 1][:, 0:I], xsT[:, t % 2, :],
                                         w13[:, bass.ds(e, 1), I:2 * I], start=True, stop=True).then_inc(h_ready, 1)
                    if t + 2 < ETILES:
                        x_transpose(t + 2)
                    if 1 <= t <= ETILES:
                        u = t - 1
                        pe.wait_ge(gate_done, u + 1)
                        if u >= 2:
                            pe.wait_ge(gT_copied, u - 1)
                        else:
                            pe.wait_ge(so_added, half_chunks - 1 + u)
                        for k in range(3):
                            last = nc.tensor.transpose(GT[u % 2][0:IC[k], P * k:P * (k + 1)],
                                                       gg[:, u % 2, P * k:P * k + IC[k]], ident[:])
                        last.then_inc(gT_ready, 1)
                    if t >= 2:
                        u = t - 2
                        pe.wait_ge(gT_copied, u + 1)
                        if u >= 1:
                            pe.wait_ge(y_copied, u)
                        for k in range(3):
                            last = nc.tensor.matmul(Y[:, P * (u % 2):P * (u % 2 + 1)], gT[0:IC[k], u % 2, k, :],
                                                    w2[0:IC[k], bass.ds(e_of[u], 1), k, :], start=(k == 0),
                                                    stop=(k == 2), skip_group_check=True)
                        last.then_inc(y_ready, 1)
                pe.wait_ge(gate_done, ETILES)
                pe.wait_ge(gT_copied, ETILES)
                for c in range(half_chunks, CHUNKS):
                    shared_hidden(c)
                    if c > half_chunks:
                        shared_out(c - 1)
                shared_out(CHUNKS - 1)

            @block.vector
            def _(dve):
                def shared_gate(c):
                    for k in range(3):
                        u = 3 * c + k
                        dve.wait_ge(sh_silu, u + 1)
                        if c >= 2:
                            dve.wait_ge(so_ready, c - 1)
                        nc.vector.tensor_tensor(hT[0:IC[k], c % 2, k, :], h1[0:IC[k], u % 2, :],
                                                bank[2 * (u % 2) + 1][0:IC[k], :], ALU.mult).then_inc(sh_gate, 1)

                def shared_add(c):
                    dve.wait_ge(so_ready, c + 1)
                    for t in range(TT * c, TT * (c + 1)):
                        last = nc.vector.scalar_tensor_tensor(acc[:, t, :], SY[c % 2][:, C * (t % TT):C * (t % TT + 1)],
                                                              w_shared[:, t:t + 1], acc[:, t, :], ALU.mult, ALU.add)
                    last.then_inc(so_added, 1)

                def expert_add(c):
                    dve.wait_ge(so_added, c + 1)
                    dve.wait_ge(gathered, 16 * TT * (c + 1))
                    for t in range(TT * c, TT * (c + 1)):
                        last = nc.vector.scalar_tensor_tensor(acc[:, t, :], yg[:, t, :], w_expert[:, t:t + 1],
                                                              acc[:, t, :], ALU.mult, ALU.add)
                    last.then_inc(e_added, 1)

                half_chunks = CHUNKS // 2
                for c in range(half_chunks):
                    shared_gate(c)
                    if c == 1:
                        dve.wait_ge(acc_in, 16)
                    if c:
                        shared_add(c - 1)
                shared_add(half_chunks - 1)
                for t in range(ETILES + 1):
                    if t < ETILES:
                        dve.wait_ge(silu_done, t + 1)
                        if t >= 2:
                            dve.wait_ge(gT_ready, t - 1)
                        nc.vector.tensor_tensor(gg[:, t % 2, :], g1[:, t % 2, :], bank[2 * (t % 2) + 1][:, 0:I],
                                                ALU.mult).then_inc(gate_done, 1)
                    if t:
                        u = t - 1
                        dve.wait_ge(gT_ready, u + 1)
                        if u >= 2:
                            dve.wait_ge(y_ready, u - 1)
                        nc.vector.tensor_copy(gT[:, u % 2, 0:2, :].rearrange("p k t -> p (k t)"),
                                              GT[u % 2][:, 0:2 * P])
                        nc.vector.tensor_copy(gT[0:IC[2], u % 2, 2, :], GT[u % 2][0:IC[2], 2 * P:3 * P]
                                              ).then_inc(gT_copied, 1)
                for c in range(half_chunks, CHUNKS):
                    shared_gate(c)
                    if c > half_chunks:
                        shared_add(c - 1)
                        expert_add(c - half_chunks - 1)
                shared_add(CHUNKS - 1)
                for c in range(half_chunks - 1, CHUNKS):
                    expert_add(c)


def block_diagonal(w):
    a, b = w.shape
    out = np.zeros((H * a, H * b), w.dtype)
    for h in range(H):
        out[h * a:(h + 1) * a, h * b:(h + 1) * b] = w
    return out


def kernel(L0_attn_x, L0_attn_c_attn_w, L0_attn_c_attn_b, L0_attn_q2l_w, L0_attn_q2l_b, L0_attn_kv2l_w,
           L0_attn_kv2l_b, L0_attn_l2o_w, L0_attn_l2o_b, L0_attn_wqk_w, L0_attn_wqk_b, L0_attn_cproj_w,
           L0_attn_cproj_b, L0_ffn_router_w, L0_ffn_routing_bias, L0_ffn_sw1, L0_ffn_sw2, L0_ffn_sw3, L0_ffn_ew1,
           L0_ffn_ew2, L0_ffn_ew3):
    import concourse.bacc as bacc
    from concourse.bass_utils import run_bass_kernel_spmd

    a = lambda z: np.asarray(z)
    swap = np.arange(L) ^ 1
    q2l, kv2l, l2o, wqk = a(L0_attn_q2l_w), a(L0_attn_kv2l_w), a(L0_attn_l2o_w), a(L0_attn_wqk_w)
    q2lb, kv2lb = a(L0_attn_q2l_b), a(L0_attn_kv2l_b)
    cw, cb = a(L0_attn_c_attn_w), a(L0_attn_c_attn_b)
    spread = np.stack([block_diagonal(w.T) for w in (q2l, q2l[swap], kv2l, kv2l[swap])], axis=1)
    kvT = block_diagonal(kv2l).reshape(G_PER_PAIR, P, C).transpose(1, 0, 2)
    oproj = block_diagonal(l2o.T).reshape(G_PER_PAIR, P, C).transpose(1, 0, 2)
    wqk_bd = np.zeros((P, P), wqk.dtype)
    for h in range(HG):
        wqk_bd[L * h:L * (h + 1), L * h:L * (h + 1)] = wqk.T
    lat_b = np.stack([np.tile(z, HG) for z in (q2lb, q2lb[swap], kv2lb, kv2lb[swap], kv2lb)
                      for _ in range(G_PER_PAIR)], axis=1)
    w1 = np.concatenate([a(L0_ffn_ew1), a(L0_ffn_sw1)[None]])
    w3 = np.concatenate([a(L0_ffn_ew3), a(L0_ffn_sw3)[None]])
    w2 = np.concatenate([a(L0_ffn_ew2), a(L0_ffn_sw2)[None]])
    w13 = np.concatenate([w1, w3], axis=1).transpose(2, 0, 1)
    w2t = np.zeros((E + 1, 3 * P, C), w2.dtype)
    w2t[:, :I] = w2.transpose(0, 2, 1)
    arrays = {
        "x": a(L0_attn_x).reshape(N, C),
        "wqk_nat": cw[:2 * C].reshape(2, C, C).transpose(1, 0, 2),
        "spread": spread, "kvT": kvT, "oproj": oproj, "bqkv": cb.reshape(3, C).T, "lat_b": lat_b,
        "out_b": np.tile(a(L0_attn_l2o_b), H)[:, None], "cprojT": a(L0_attn_cproj_w).T,
        "cproj_b": np.broadcast_to(a(L0_attn_cproj_b), (P, C)), "routerT": a(L0_ffn_router_w).T,
        "router_b": np.broadcast_to(a(L0_ffn_routing_bias), (P, E)), "wqk_bd": wqk_bd,
        "wqk_b": np.tile(a(L0_attn_wqk_b), HG)[:, None], "wvT": cw[2 * C:].T, "w13": w13,
        "w2": w2t.reshape(E + 1, 3, P, C).transpose(2, 0, 1, 3), **shape_constants(),
    }
    nc = bacc.Bacc("TRN2", target_bir_lowering=False, num_devices=1)
    arrays = {f"in_{k}": np.ascontiguousarray(z) for k, z in arrays.items()}
    d = {k[3:]: nc.dram_tensor(k, z.shape, mybir.dt.from_np(z.dtype), kind="ExternalInput").ap()
         for k, z in arrays.items()}
    out = nc.dram_tensor("out_0", (N, C), F32, kind="ExternalOutput").ap()
    build(nc, d, out)
    r = run_bass_kernel_spmd(nc, [arrays], core_ids=[0])
    return r.results[0]["out_0"].reshape(B, T, C)
```

```python
import numpy as np

import concourse.bass as bass
from concourse import mybir
from contextlib import ExitStack

F32 = mybir.dt.float32
F32R = mybir.dt.float32r
BF16 = mybir.dt.bfloat16
I32 = mybir.dt.int32
U32 = mybir.dt.uint32
ALU = mybir.AluOpType
ACT = mybir.ActivationFunctionType
AX = mybir.AxisListType

B, T, C = 8, 512, 128
H = 16
HD = C // H
L = 32
I = 352
E = 7
P = 128
N = B * T
NT = N // P
HG = P // L
G_PER_PAIR = H // HG
PAIRS = B // 2
PT = 2 * T
QT = T // P
STEPS = PAIRS * H
GROUPS = STEPS // HG
SLOTS = 6
KROWS = 3 * L
SROWS = KROWS + 2
VW = HD + 1
YW = 2 * VW
PW = [T, T, T // 2, P]
POFF = [0, T, 2 * T, 2 * T + T // 2]
PCOLS = sum(PW)
IC = [P, P, I - 2 * P]
PB_USES = 5
TC = 512
TT = TC // P
CHUNKS = N // TC
FIRST_CHUNKS = 3
ETILES = NT + E - 1
ETABLE = ETILES + 2
MASKED = -3.0e38
SCALE = float(L) ** -0.5


def shape_constants():
    inv = (1.0 / np.float32(10000.0) ** (np.arange(0, L, 2, dtype=np.float32) / np.float32(L))).astype(np.float32)
    ang = np.outer(np.arange(T, dtype=np.float32), inv).astype(np.float32)
    cos = np.repeat(np.cos(ang), 2, axis=1).T
    sin = np.repeat(np.sin(ang), 2, axis=1).T
    sign = np.where(np.arange(L) % 2 == 0, -1.0, 1.0)[:, None]
    mask = np.zeros((P, T), np.float32)
    mask[:, T - P:] = np.where(np.arange(P)[None, :] <= np.arange(P)[:, None], 0.0, MASKED)
    sumsel = np.zeros((P, 2 * YW), np.float32)
    for q in range(4):
        for d in range(YW):
            sumsel[L * q + d, (q // 2) * YW + d] = 1.0
    r = np.arange(P)
    return {
        "ident": np.eye(P, dtype=np.float32),
        "mask": mask,
        "cosr": np.ascontiguousarray(np.tile(cos, (HG, 1)).astype(np.float32)),
        "sinr": np.ascontiguousarray(np.tile(sin * sign, (HG, 1)).astype(np.float32)),
        "sumsel": sumsel,
        "tri": (r[:, None] < r[None, :]).astype(np.float32),
        "ones": np.ones((P, P), np.float32),
        "rank": np.ascontiguousarray(np.broadcast_to(np.arange(E, 0, -1, dtype=np.float32), (P, E))),
        "thresh": np.ascontiguousarray(np.broadcast_to(np.arange(NT, dtype=np.float32) * P, (P, NT))),
        "tileno": np.ascontiguousarray(np.broadcast_to(np.arange(ETABLE, dtype=np.float32), (P, ETABLE))),
    }


def build(nc, d, out):
    ctx = ExitStack()
    with ctx:
        def keep(name, shape, dt):
            return ctx.enter_context(nc.sbuf_tensor(name, shape, dt))

        def sem(name):
            return ctx.enter_context(nc.semaphore(name))

        bank = [ctx.enter_context(nc.psum_tensor(f"bank{i}", [P, 512], F32)) for i in range(8)]

        xn_rows = nc.dram_tensor("xn_rows", [N, C], F32, kind="Internal").ap()
        sorted_x = nc.dram_tensor("sorted_x", [ETABLE * P, C], F32, kind="Internal").ap()
        sorted_y = nc.dram_tensor("sorted_y", [ETILES * P, C], F32, kind="Internal").ap()
        mixed = nc.dram_tensor("mixed", [N, C], F32, kind="Internal").ap()

        ident = keep("ident_sb", [P, P], F32)
        xnT = keep("xnT", [C, N], F32)
        pos = keep("pos", [P, NT], U32)
        w_shared = keep("w_shared", [P, NT], F32)
        w_expert = keep("w_expert", [P, NT], F32)
        tile_expert = keep("tile_expert", [P, ETABLE], I32)
        w13s = keep("w13s", [C, 2 * I], F32)
        w2s = keep("w2s", [P, 3, C], F32)
        xres = keep("xres", [P, 2 * QT, C], F32)
        shared_in, mixed_out = sem("shared_in"), sem("mixed_out")

        attn_stack = ExitStack()
        with attn_stack:
            def sb(name, shape, dt):
                return attn_stack.enter_context(nc.sbuf_tensor(name, shape, dt))

            xH = sb("xH", [C, PT], F32R)
            xL = sb("xL", [C, PT], F32R)
            wf = sb("wf", [C, 4, 2, H * L], F32R)
            biases = sb("biases", [P, 4 * G_PER_PAIR + G_PER_PAIR], F32)
            wqk = sb("wqk", [P, P], F32)
            wqk_b = sb("wqk_b", [P, 1], F32)
            wvT = sb("wvT", [C, C], F32)
            wout = sb("wout", [C, C], F32)
            const_row = sb("const_row", [P, C], F32)
            cosr = sb("cosr_sb", [P, T], F32)
            sinr = sb("sinr_sb", [P, T], F32)
            mask = sb("mask_sb", [P, T], F32)
            sumsel = sb("sumsel_sb", [P, 2 * YW], F32)
            routerT = sb("routerT", [C, E], F32)
            router_b = sb("router_b", [P, E], F32)
            tri = sb("tri_sb", [P, P], F32)
            ones = sb("ones_sb", [P, P], F32)
            rank = sb("rank_sb", [P, E], F32)
            thresh = sb("thresh_sb", [P, NT], F32)
            tileno = sb("tileno_sb", [P, ETABLE], F32)
            logits_ready = sem("logits_ready")
            consts = (logits_ready, bank[3], routerT, router_b, tri, ones, rank, thresh, tileno)

            prologue(nc, d, bank, sem, ident, xnT, wf, biases, wqk, wqk_b, wvT, wout, const_row, cosr, sinr, mask,
                     sumsel, consts, xn_rows, sorted_x)
            attention(nc, d, bank, sem, sb, shared_in, w13s, w2s, xres, mixed_out, consts, ident, xnT, pos, w_shared,
                      w_expert, tile_expert, xH, xL, wf, biases, wqk, wqk_b, wvT, wout, const_row, cosr, sinr, mask,
                      sumsel, xn_rows, sorted_x, mixed)
        experts(nc, d, bank, sem, shared_in, w13s, w2s, mixed_out, ident, xnT, pos, w_shared, w_expert, tile_expert,
                sorted_x, sorted_y, mixed, out)


def prologue(nc, d, bank, sem, ident, xnT, wf, biases, wqk, wqk_b, wvT, wout, const_row, cosr, sinr, mask, sumsel,
             consts, xn_rows, sorted_x):
    logits_ready, LG, routerT, router_b, tri, ones, rank, thresh, tileno = consts
    tmp = ExitStack()
    with tmp:
        def sb(name, shape, dt):
            return tmp.enter_context(nc.sbuf_tensor(name, shape, dt))

        x = sb("x", [P, NT, C], F32)
        stats = sb("stats", [P, NT, 6], F32)
        mv = sb("mv", [P, NT, 2], F32)
        sd = sb("sd", [P, NT], F32)
        rstd = sb("rstd", [P, NT], F32)
        wqk_nat = sb("wqk_nat", [P, 2, C], F32)
        spread = sb("spread", [P, 4, H * L], F32)
        bqkv = sb("bqkv", [P, 3], F32)
        lat_b = sb("lat_b", [P, 5 * G_PER_PAIR], F32)
        zeros = sb("zeros", [P, 4 * C], F32)

        first_in = sem("first_in")
        x_in = [sem(f"x_in{i}") for i in range(4)]
        fold_in = sem("fold_in")
        behind_in = sem("behind_in")
        rest_in = sem("rest_in")
        zeros_set = sem("zeros_set")
        zero_rows = sem("zero_rows")
        stats_ready, mean_ready, var_ready = sem("stats_ready"), sem("mean_ready"), sem("var_ready")
        rstd_ready = sem("rstd_ready")
        sd_ready = sem("sd_ready")
        xn_ready = sem("xn_ready")
        xn_stored = sem("xn_stored")
        xt_ready = sem("xt_ready")
        xt_copied = sem("xt_copied")
        fold_ready = sem("fold_ready")
        fold_high = sem("fold_high")
        fold_low = sem("fold_low")
        bias_ready = sem("bias_ready")
        XB = NT // 4
        X3 = d["x"].rearrange("(t p) c -> p t c", p=P)
        FOLD = [(wqk_nat[:], d["wqk_nat"]), (spread[:], d["spread"])]
        BEHIND = [(bqkv[:], d["bqkv"]), (lat_b[:], d["lat_b"])]
        REST = [(ones[:], d["ones"]), (routerT[:], d["routerT"]), (cosr[:], d["cosr"]), (sinr[:], d["sinr"]),
                (wqk[:], d["wqk_bd"]),
                (wqk_b[:], d["wqk_b"]), (wvT[:], d["wvT"]), (mask[:], d["mask"]), (sumsel[:], d["sumsel"]),
                (router_b[:], d["router_b"]), (rank[:], d["rank"]), (tri[:], d["tri"]), (thresh[:], d["thresh"]),
                (tileno[:], d["tileno"])]

        with nc.Block() as block:
            @block.sync
            def _(sp):
                for i in range(4):
                    sp.dma_start(x[:, XB * i:XB * (i + 1), :], X3[:, XB * i:XB * (i + 1), :]).then_inc(x_in[i], 16)
                for dst, src in REST:
                    sp.dma_start(dst, src).then_inc(rest_in, 16)
                for i in range(4):
                    sp.wait_ge(xn_ready, XB * (i + 1))
                    sp.dma_start(xn_rows.rearrange("(t p) c -> p t c", p=P)[:, XB * i:XB * (i + 1), :],
                                 x[:, XB * i:XB * (i + 1), :]).then_inc(xn_stored, 16)
                sp.wait_ge(rest_in, 16 * len(REST))
                sp.wait_ge(xn_stored, 16 * 4)
                sp.wait_ge(zero_rows, 16 * (ETABLE // 4))

            @block.gpsimd
            def _(pool):
                nc.gpsimd.memset(zeros[:], 0.0).then_inc(zeros_set, 1)
                pool.wait_ge(zeros_set, 1)
                pool.wait_ge(behind_in, 16 * len(BEHIND))
                for i in range(ETABLE // 4):
                    pool.dma_start(sorted_x[4 * P * i:4 * P * (i + 1), :].rearrange("(p a) c -> p (a c)", p=P),
                                   zeros[:]).then_inc(zero_rows, 16)

            @block.scalar
            def _(act):
                for dst, src in FOLD:
                    act.dma_start(dst, src).then_inc(fold_in, 16)
                act.dma_start(ident[:], d["ident"]).then_inc(first_in, 16)
                for dst, src in BEHIND:
                    act.dma_start(dst, src).then_inc(behind_in, 16)

                def root(i):
                    act.wait_ge(var_ready, i + 1)
                    block_i = slice(XB * i, XB * (i + 1))
                    nc.scalar.activation(sd[:, block_i], sd[:, block_i], ACT.Sqrt).then_inc(sd_ready, 1)

                def copy_transposed(i):
                    act.wait_ge(xt_ready, 4 * i + 4)
                    nc.scalar.copy(xnT[:, 512 * i:512 * (i + 1)], bank[i % 2][:]).then_inc(xt_copied, 1)

                root(0)
                for k in range(2):
                    act.wait_ge(fold_ready, k + 1)
                    nc.scalar.copy(wf[:, k, 0, :], bank[4 + k][:]).then_inc(fold_high, 1)
                root(1)
                for k in range(2, 4):
                    act.wait_ge(fold_ready, k + 1)
                    nc.scalar.copy(wf[:, k, 0, :], bank[4 + k][:]).then_inc(fold_high, 1)
                copy_transposed(0)
                copy_transposed(1)
                root(2)
                copy_transposed(2)
                copy_transposed(3)
                root(3)
                for i in range(4, NT // 4):
                    copy_transposed(i)

            @block.tensor
            def _(pe):
                def transposes(i):
                    for t in range(XB * i, XB * (i + 1)):
                        pe.wait_ge(xn_ready, t + 1)
                        if t % 4 == 0 and t >= 8:
                            pe.wait_ge(xt_copied, t // 4 - 1)
                        nc.tensor.transpose(bank[t // 4 % 2][:, P * (t % 4):P * (t % 4 + 1)], x[:, t, :],
                                            ident[:]).then_inc(xt_ready, 1)

                def logits(i):
                    for t in range(XB * i, XB * (i + 1)):
                        if t % 4 == 0:
                            pe.wait_ge(xt_copied, t // 4 + 1)
                        last = nc.tensor.matmul(LG[:, E * t:E * (t + 1)], xnT[:, P * t:P * (t + 1)], routerT[:],
                                                start=True, stop=True, skip_group_check=True)
                    last.then_inc(logits_ready, 1)

                pe.wait_ge(fold_in, 32)
                for k in range(4):
                    nc.tensor.matmul(bank[4 + k][:], wqk_nat[:, k // 2, :], spread[:, k, :],
                                     start=True, stop=True).then_inc(fold_ready, 1)
                pe.wait_ge(behind_in, 16 * len(BEHIND))
                for k in range(4):
                    for g in range(G_PER_PAIR):
                        first, n = k // 2, 2 if k == 2 else 1
                        at = k * G_PER_PAIR + g
                        step = 2 * G_PER_PAIR
                        dst = bank[2][:, at:at + 1] if n == 1 else bank[2][:, at:at + step + 1:step]
                        last = nc.tensor.matmul(dst, spread[:, k, P * g:P * (g + 1)], bqkv[:, first:first + n],
                                                start=True, stop=True, skip_group_check=True)
                last.then_inc(bias_ready, 1)
                pe.wait_ge(first_in, 16)
                transposes(0)
                transposes(1)
                pe.wait_ge(rest_in, 16 * len(REST))
                logits(0)
                transposes(2)
                logits(1)
                transposes(3)

            @block.vector
            def _(dve):
                def norm_stats(i):
                    dve.wait_ge(x_in[i], 16)
                    for t in range(XB * i, XB * (i + 1)):
                        last = nc.vector.bn_stats(stats[:, t, :], x[:, t, :])
                    last.then_inc(stats_ready, 1)
                    dve.wait_ge(stats_ready, i + 1)
                    for t in range(XB * i, XB * (i + 1)):
                        last = nc.vector.bn_aggr(mv[:, t, :], stats[:, t, :])
                    last.then_inc(mean_ready, 1)
                    dve.wait_ge(mean_ready, i + 1)
                    nc.vector.tensor_scalar(sd[:, XB * i:XB * (i + 1)], mv[:, XB * i:XB * (i + 1), 1], 1e-5, None,
                                            ALU.add).then_inc(var_ready, 1)

                def normalise(i):
                    dve.wait_ge(sd_ready, i + 1)
                    nc.vector.reciprocal(rstd[:, XB * i:XB * (i + 1)], sd[:, XB * i:XB * (i + 1)]
                                         ).then_inc(rstd_ready, 1)
                    dve.wait_ge(rstd_ready, i + 1)
                    for t in range(XB * i, XB * (i + 1)):
                        nc.vector.tensor_scalar(x[:, t, :], x[:, t, :], mv[:, t, 0:1], rstd[:, t:t + 1],
                                                ALU.subtract, ALU.mult).then_inc(xn_ready, 1)

                def fold_rest(k):
                    dve.wait_ge(fold_high, k + 1)
                    nc.vector.tensor_tensor(wf[:, k, 1, :], bank[4 + k][:], wf[:, k, 0, :].bitcast(F32),
                                            ALU.subtract).then_inc(fold_low, 1)

                norm_stats(0)
                norm_stats(1)
                normalise(0)
                fold_rest(0)
                norm_stats(2)
                normalise(1)
                fold_rest(1)
                fold_rest(2)
                fold_rest(3)
                dve.wait_ge(bias_ready, 1)
                nc.vector.tensor_tensor(biases[:], bank[2][:, 0:5 * G_PER_PAIR], lat_b[:], ALU.add)
                norm_stats(3)
                normalise(2)
                normalise(3)


def attention(nc, d, bank, sem, sb, shared_in, w13s, w2s, xres, mixed_out, consts, ident, xnT, pos, w_shared,
              w_expert, tile_expert, xH, xL, wf, biases, wqk, wqk_b, wvT, wout, const_row, cosr, sinr, mask, sumsel,
              xn_rows, sorted_x, mixed):
    Kst = sb("Kst", [P, SLOTS, PT], F32R)
    Qst = sb("Qst", [P, SLOTS, PT], F32R)
    dKH = sb("dKH", [P, 2, PT], F32R)
    dKL = sb("dKL", [P, 2, PT], F32R)
    dQH = sb("dQH", [P, 2, PT], F32R)
    dQL = sb("dQL", [P, 2, PT], F32R)
    tk1 = sb("tk1", [P, PT], F32)
    tq1 = sb("tq1", [P, PT], F32)
    tk2 = sb("tk2", [P, PT], F32)
    tq2 = sb("tq2", [P, PT], F32)
    prob = sb("prob", [P, 2, 2, PCOLS], F32)
    v = sb("v", [P, 2, 2 * QT, 2 * HG, YW], F32)
    ysb = sb("ysb", [P, T], F32)
    yn = sb("yn", [P, 2, 2 * QT, C], F32)
    yT = sb("yT", [C, QT * P], F32)
    scratch = sb("scratch", [P, 2, T], BF16)
    mx = sb("mx", [P, 2, 2 * QT], F32)
    nm = sb("nm", [P, 2, 4 * QT], F32R)
    nmT = sb("nmT", [4 * QT, 2, P], F32R)
    rz = sb("rz", [P, 2 * QT, 2], F32)
    xrow = sb("xrow", [P, 4, C], F32)
    yn_flat = yn[:].rearrange("p a t c -> p (a t c)")
    GC = G_PER_PAIR * C
    kvT = yn_flat[:, 0:GC].rearrange("p (g c) -> p g c", c=C)
    oproj = yn_flat[:, GC:2 * GC].rearrange("p (g c) -> p g c", c=C)
    cprojT, cproj_b, m1T, o_rep = (yn_flat[:, 2 * GC + C * i:2 * GC + C * (i + 1)] for i in range(4))
    out_b, o_col = (yn_flat[:, 2 * GC + 4 * C + i:2 * GC + 4 * C + i + 1] for i in range(2))
    logits_ready, LG, routerT, router_b, tri, ones, rank, thresh, tileno = consts
    lg = sb("lg", [P, E, NT], F32)
    pr = sb("pr", [P, E, NT], F32)
    oh = sb("oh", [P, E, NT], F32)
    pm = sb("pm", [P, NT], F32)
    ms = sb("ms", [P, NT], F32)
    tot = pr
    cum = sb("cum", [P, E, NT], F32)
    before = sb("before", [P, E], F32)
    cnt = sb("cnt", [P, E], F32)
    nt_e = sb("nt_e", [P, E], F32)
    end_e = sb("end_e", [P, E], F32)
    off_e = sb("off_e", [P, E], F32)
    ge = yT[:, 0:ETABLE * E].rearrange("p (t e) -> p t e", e=E)
    te = sb("te", [P, ETABLE], F32)
    posf = sb("posf", [P, NT], F32)
    small = sb("small", [P, NT], F32)

    S = bank[0:2]
    ST = bank[2:4]
    Y, PA, PB, M = bank[4], bank[5], bank[6], bank[7]

    l_clipped, neg_exp, onehot_ready = sem("l_clipped"), sem("neg_exp"), sem("onehot_ready")
    out_in, m1_ready, m1_copied, o_ready = sem("out_in"), sem("m1_ready"), sem("m1_copied"), sem("o_ready")
    o_spread, wout_ready, wout_copied = sem("o_spread"), sem("wout_ready"), sem("wout_copied")
    prefix_ready, routed, pos_ready = sem("prefix_ready"), sem("routed"), sem("pos_ready")
    set_up = sem("set_up")
    y_clear = sem("y_clear")
    xh_ready, xl_ready = sem("xh_ready"), sem("xl_ready")
    pa_ready, pb_ready, pa_used, pb_used = sem("pa_ready"), sem("pb_ready"), sem("pa_used"), sem("pb_used")
    k_roped, q_roped, kh_ready, kl_ready, qh_ready = (sem("k_roped"), sem("q_roped"), sem("kh_ready"),
                                                      sem("kl_ready"), sem("qh_ready"))
    ql_ready = sem("ql_ready")
    filled = [sem(f"filled{i}") for i in range(SLOTS)]
    neg_in = [sem(f"neg_in{i}") for i in range(2)]
    s_ready, s_max = sem("s_ready"), sem("s_max")
    neg_high, neg_ready, negT_ready, negT_copied = (sem("neg_high"), sem("neg_ready"), sem("negT_ready"),
                                                    sem("negT_copied"))
    st_ready, exp_done, cut_done, pv_done = sem("st_ready"), sem("exp_done"), sem("cut_done"), sem("pv_done")
    y_copied, z_ready, rz_ready, z_used = sem("y_copied"), sem("z_ready"), sem("rz_ready"), sem("z_used")
    ynT_ready, ynT_copied, out_ready, o_added = sem("ynT_ready"), sem("ynT_copied"), sem("out_ready"), sem("o_added")
    xres_in, xres_const = sem("xres_in"), sem("xres_const")
    row_in = [sem(f"row_in{i}") for i in range(4)]
    row_sorted = [sem(f"row_sorted{i}") for i in range(4)]

    FIRST, LAST = -2 * HG - 1, STEPS + 1
    ROUTE = -5

    def chunk(n):
        G = n // HG + 2
        return (G, n % HG) if 0 <= G < GROUPS and n >= -2 * HG else (None, None)

    PIECES = {(0, 0): (0, 0), (0, 2): (0, 1), (0, 3): (0, 2), (1, 0): (0, 3), (1, 2): (1, 0), (1, 3): (1, 1),
              (2, 0): (1, 2), (2, 2): (1, 3)}
    ROPES = {(0, 3): (0, 0), (0, 6): (0, 1), (1, 1): (0, 2), (1, 3): (0, 3), (1, 6): (1, 0), (2, 1): (1, 1),
             (2, 3): (1, 2), (2, 6): (1, 3)}

    def split_pair(n):
        return (n + 9) // H if (n + 9) % H == 0 and (n + 9) // H < PAIRS else None

    def out_part(n):
        pair, part = n // H - 1, n % H - 1
        return (pair, part) if 0 <= pair < PAIRS - 1 and 0 <= part < 4 else (None, None)

    def pa_base(G):
        return 5 * G + (G + 1) // 2

    def v_use(G):
        return pa_base(G - G % 2) + 6

    with nc.Block() as block:
        @block.sync
        def _(sp):
            for dst, src in ((kvT, d["kvT"]), (oproj, d["oproj"]), (out_b, d["out_b"]), (cprojT, d["cprojT"]),
                             (cproj_b, d["cproj_b"])):
                sp.dma_start(dst, src).then_inc(out_in, 16)
            sp.dma_start(w13s[:], d["w13"][:, E, :]).then_inc(shared_in, 16)
            sp.dma_start(w2s[:], d["w2"][:, E, :, :]).then_inc(shared_in, 16)
            for n in range(FIRST, LAST):
                r = n + 2
                if 0 <= r < NT:
                    if r >= 4:
                        sp.wait_ge(row_sorted[r % 4], 16 * (r // 4))
                    sp.dma_start(xrow[:, r % 4, :], xn_rows[P * r:P * (r + 1), :]).then_inc(row_in[r % 4], 16)
                m = n + 1
                if 0 <= m < STEPS:
                    sp.wait_ge(negT_copied, m + 1)
                    if m < 2:
                        sp.wait_ge(set_up, 5)
                    if m >= SLOTS:
                        sp.wait_ge(st_ready, 8 * (m - SLOTS) + 8)
                    sp.dma_start(Qst[KROWS:SROWS, m % SLOTS, :].bitcast(F32), nmT[:, m % 2, :].bitcast(F32)
                                 ).then_inc(neg_in[m % 2], 16)
                m = n + HG
                if 0 <= m < STEPS:
                    G, h, slot = m // HG, m % HG, m % SLOTS
                    if h == 0:
                        sp.wait_ge(kh_ready, 2 * G + 2)
                        sp.wait_ge(kl_ready, 2 * G + 2)
                        sp.wait_ge(qh_ready, 2 * G + 2)
                        sp.wait_ge(ql_ready, 2 * G + 2)
                    if m == 0:
                        sp.wait_ge(set_up, 5)
                    if m >= SLOTS:
                        sp.wait_ge(st_ready, 8 * (m - SLOTS) + 8)
                    rows = slice(L * h, L * h + L)
                    for r, (kd, qd) in enumerate(((dKH, dQH), (dKL, dQH), (dKH, dQL))):
                        sp.dma_start(Kst[L * r:L * r + L, slot, :].bitcast(F32),
                                     kd[rows, G % 2, :].bitcast(F32)).then_inc(filled[slot], 16)
                        sp.dma_start(Qst[L * r:L * r + L, slot, :].bitcast(F32),
                                     qd[rows, G % 2, :].bitcast(F32)).then_inc(filled[slot], 16)
                if n % H == 7 and 0 <= n < STEPS:
                    pair = n // H
                    if pair:
                        sp.wait_ge(mixed_out, 16 * pair)
                    sp.dma_start(xres[:], d["x"][PT * pair:PT * (pair + 1), :].rearrange("(t p) c -> p t c", p=P)
                                 ).then_inc(xres_in, 16)
                pair, part = out_part(n)
                if part == 3:
                    sp.wait_ge(o_added, 2 * pair + 2)
                    sp.dma_start(mixed[PT * pair:PT * (pair + 1), :].rearrange("(t p) c -> p t c", p=P),
                                 xres[:]).then_inc(mixed_out, 16)
            for half in range(2):
                sp.wait_ge(o_added, 2 * (PAIRS - 1) + half + 1)
                rows = slice(PT * (PAIRS - 1) + T * half, PT * (PAIRS - 1) + T * (half + 1))
                sp.dma_start(mixed[rows, :].rearrange("(t p) c -> p t c", p=P),
                             xres[:, QT * half:QT * (half + 1), :]).then_inc(mixed_out, 16)
            for i in range(4):
                sp.wait_ge(row_sorted[i], 16 * (NT // 4))

        @block.gpsimd
        def _(pool):
            for n in range(FIRST, LAST):
                if n == FIRST + 1:
                    pool.wait_ge(xl_ready, 1)
                    nc.gpsimd.memset(Kst[KROWS:P, :, :].bitcast(F32), 1.0).then_inc(set_up, 1)
                    pool.wait_ge(set_up, 1)
                    nc.gpsimd.memset(v[:, :, :, :, HD:VW], 1.0).then_inc(set_up, 1)
                    nc.gpsimd.memset(v[:, :, :, :, VW:YW], 0.0).then_inc(set_up, 1)
                    for par in range(2):
                        nc.gpsimd.memset(prob[:, par, :, POFF[1]:POFF[1] + P], 0.0).then_inc(set_up, 1)
                G, part = chunk(n)
                if part == 3:
                    pool.wait_ge(pa_used, pa_base(G) + 4)
                    pool.wait_ge(pb_used, PB_USES * G + 4)
                    nc.gpsimd.tensor_tensor(tq1[:, T:PT], tq1[:, T:PT], tq2[:, T:PT], ALU.add).then_inc(q_roped, 1)
                if n % H == 11 and 0 <= n < STEPS:
                    pair = n // H
                    pool.wait_ge(xres_in, 16 * (pair + 1))
                    pool.wait_ge(wout_copied, 1)
                    nc.gpsimd.tensor_tensor(xres[:], xres[:], const_row[:].unsqueeze(1).to_broadcast([P, 2 * QT, C]),
                                            ALU.add).then_inc(xres_const, 1)
                for j in range(QT):
                    if 0 <= n < STEPS:
                        pool.wait_ge(exp_done, 8 * n + 2 * j + 2)
                        at = POFF[j] + (P if j == 1 else 0)
                        diag = prob[:, n % 2, :, at:at + P]
                        nc.gpsimd.affine_select(out=diag, in_=diag, compare_op=ALU.is_ge, fill=0.0, base=0,
                                                pattern=[[0, 2], [1, P]], channel_multiplier=-1
                                                ).then_inc(cut_done, 1)
                    pair = split_pair(n)
                    if pair is not None and j == 1:
                        pool.wait_ge(xh_ready, pair + 1)
                        nc.gpsimd.tensor_tensor(xL[:], xnT[:, PT * pair:PT * (pair + 1)], xH[:].bitcast(F32),
                                                ALU.subtract).then_inc(xl_ready, 1)
                    f = j // 2
                    half = slice(T * f, T * (f + 1))
                    if part == 1 and j in (0, 2):
                        pool.wait_ge(pa_used, pa_base(G) + 1 + f)
                        pool.wait_ge(pb_used, PB_USES * G + 1 + f)
                        nc.gpsimd.tensor_tensor(tk1[:, half], tk1[:, half], tk2[:, half], ALU.add
                                                ).then_inc(k_roped, 1)
                    if part == 2 and j == 0:
                        pool.wait_ge(pa_used, pa_base(G) + 3)
                        pool.wait_ge(pb_used, PB_USES * G + 3)
                        nc.gpsimd.tensor_tensor(tq1[:, 0:T], tq1[:, 0:T], tq2[:, 0:T], ALU.add).then_inc(q_roped, 1)
                    if part == 3 and j >= 2:
                        half = slice(T * (j - 2), T * (j - 1))
                        pool.wait_ge(qh_ready, 2 * G + j - 1)
                        if j == 2:
                            pool.wait_ge(pa_used, pa_base(G) + 5)
                        else:
                            pool.wait_ge(pb_used, PB_USES * (G + 1))
                        nc.gpsimd.tensor_tensor(dQL[:, G % 2, half], tq2[:, half], dQH[:, G % 2, half].bitcast(F32),
                                                ALU.subtract).then_inc(ql_ready, 1)
                    if part == 2 and j >= 2:
                        half = slice(T * (j - 2), T * (j - 1))
                        pool.wait_ge(kh_ready, 2 * G + j - 1)
                        nc.gpsimd.tensor_tensor(dKL[:, G % 2, half], tk1[:, half], dKH[:, G % 2, half].bitcast(F32),
                                                ALU.subtract).then_inc(kl_ready, 1)
                if 0 <= n < NT:
                    if n == 0:
                        pool.wait_ge(pos_ready, 1)
                    pool.wait_ge(row_in[n % 4], 16 * (n // 4 + 1))
                    pool.indirect_dma_start(sorted_x, bass.IndirectOffsetOnAxis(pos[:, n:n + 1], 0),
                                            xrow[:, n % 4, :], None).then_inc(row_sorted[n % 4], 16)

        @block.scalar
        def _(act):
            for n in range(FIRST, LAST):
                if n == ROUTE:
                    act.wait_ge(l_clipped, 1)
                    nc.scalar.activation(pr[:], lg[:], ACT.Exp, scale=-1.0).then_inc(neg_exp, 1)
                G, part = chunk(n)
                for i in range(8):
                    if 0 <= n < STEPS:
                        if i == 0 and n >= 2:
                            act.wait_ge(pv_done, n - 1)
                        j, b = i // 2, i % 2
                        act.wait_ge(st_ready, 8 * n + i + 1)
                        lo, q0 = P * j, min(P * j, T - 2 * P)
                        at = POFF[j] + (P if j == 1 else 0)
                        nc.scalar.activation(prob[:, n % 2, b, at:at + T - lo], ST[i % 2][:, lo - q0:T - q0],
                                             ACT.Exp, scale=SCALE).then_inc(exp_done, 1)
                    m = n + 1
                    if i == 3 and 0 <= m < STEPS:
                        act.wait_ge(negT_ready, m + 1)
                        if m >= 2:
                            act.wait_ge(neg_in[m % 2], 16 * (m // 2))
                        nc.scalar.copy(nmT[:, m % 2, :], M[0:4 * QT, 0:P]).then_inc(negT_copied, 1)
                    if i == 5 and 0 <= n - 1 < STEPS and n % 2 == 0:
                        act.wait_ge(pv_done, n)
                        if n >= 4:
                            act.wait_ge(z_ready, n // 2 - 1)
                        nc.scalar.copy(ysb[:], Y[:]).then_inc(y_copied, 1)
                    pair, opart = out_part(n)
                    if opart in (0, 2) and i == 6:
                        act.wait_ge(ynT_ready, 2 * pair + opart // 2 + 1)
                        if 2 * pair + opart // 2:
                            act.wait_ge(out_ready, 2 * pair + opart // 2)
                        nc.scalar.copy(yT[:], M[:]).then_inc(ynT_copied, 1)
                    pair = split_pair(n)
                    if pair is not None and i == 2:
                        if pair:
                            act.wait_ge(pa_ready, pa_base(G_PER_PAIR * pair - 1) + 4)
                            act.wait_ge(pb_ready, PB_USES * (G_PER_PAIR * pair - 1) + 4)
                            act.wait_ge(xl_ready, pair)
                        nc.scalar.copy(xH[:], xnT[:, PT * pair:PT * (pair + 1)]).then_inc(xh_ready, 1)
                    if i in (1, 3) and part == 2:
                        f = i // 2
                        act.wait_ge(k_roped, 2 * G + f + 1)
                        if G >= 2 and f == 0:
                            for h in range(HG):
                                m = HG * (G - 2) + h
                                act.wait_ge(filled[m % SLOTS], 96 * (m // SLOTS + 1))
                        nc.scalar.copy(dKH[:, G % 2, T * f:T * (f + 1)], tk1[:, T * f:T * (f + 1)]
                                       ).then_inc(kh_ready, 1)
                    if part == 3 and i in (1, 4):
                        f = i // 4
                        if f == 0:
                            act.wait_ge(pa_ready, pa_base(G) + 5)
                        else:
                            act.wait_ge(pb_ready, PB_USES * (G + 1))
                        nc.scalar.activation(dQH[:, G % 2, T * f:T * (f + 1)], (PA, PB)[f][:], ACT.Identity,
                                             bias=wqk_b[:, 0:1]).then_inc(qh_ready, 1)
                    if part == 3 and i in (2, 5):
                        f = i // 5
                        nc.scalar.activation(tq2[:, T * f:T * (f + 1)], (PA, PB)[f][:], ACT.Identity,
                                             bias=wqk_b[:, 0:1]).then_inc((pa_used, pb_used)[f], 1)
                    if part == 3 and i == 7 and G % 2 == 0:
                        act.wait_ge(pa_ready, pa_base(G) + 6)
                        if G >= 4:
                            act.wait_ge(pv_done, HG * (G - 2))
                        nc.scalar.copy(v[:, G // 2 % 2, :, :, 0:HD].rearrange("p t h d -> p (t h) d"),
                                       PA[:].rearrange("p (t d) -> p t d", d=HD)).then_inc(pa_used, 1)

            for half in range(2):
                act.wait_ge(ynT_ready, 2 * (PAIRS - 1) + half + 1)
                if half == 0:
                    act.wait_ge(out_ready, 2 * (PAIRS - 1))
                nc.scalar.copy((yT, tk1)[half][:, 0:T], (PA, PB)[half][:]).then_inc(ynT_copied, 1)

        @block.tensor
        def _(pe):
            issued = {"neg": 0, "z": 0, "yt": 0, "o": 0}

            def m_free():
                for key, s in (("neg", negT_copied), ("z", z_used), ("yt", ynT_copied), ("o", o_added)):
                    if issued[key]:
                        pe.wait_ge(s, issued[key])
                if not issued["z"]:
                    pe.wait_ge(pos_ready, 1)

            def pv(m, js):
                head = m % (2 * HG)
                vs = v[:, m // (2 * HG) % 2].rearrange("p t h c -> p t (h c)")
                at = YW * head - (VW if m % 2 else 0)
                if js[0] == 0:
                    pe.wait_ge(pa_used, v_use(m // HG))
                    if m % 2 == 0:
                        if m:
                            pe.wait_ge(y_copied, m // 2)
                        else:
                            pe.wait_ge(y_clear, 1)
                            pe.wait_ge(set_up, 3)
                pe.wait_ge(cut_done, 4 * m + js[-1] + 1)
                for j in js:
                    for b in range(2):
                        q = 2 * b + j % 2
                        c0 = T - PW[j]
                        last = nc.tensor.matmul(Y[L * q:L * q + YW, c0:T], vs[:, QT * b + j, at:at + YW],
                                                prob[:, m % 2, b, POFF[j]:POFF[j] + PW[j]],
                                                start=(j < 2 and m % 2 == 0), stop=(j >= 2 and m % 2 == 1),
                                                skip_group_check=True)
                if js[-1] == QT - 1:
                    last.then_inc(pv_done, 1)

            def project(G, part, piece):
                g = G % G_PER_PAIR
                cols = slice(P * g, P * (g + 1))
                f, ab = piece // 2, piece % 2
                if part == 0 and piece == 0:
                    pe.wait_ge(xh_ready, G // G_PER_PAIR + 1)
                    pe.wait_ge(xl_ready, G // G_PER_PAIR + 1)
                kd = 2 - 2 * part + ab
                bk, used, rdy, use = ((PA, pa_used, pa_ready, pa_base(G) + 2 * part + f),
                                      (PB, pb_used, pb_ready, PB_USES * G + 2 * part + f))[ab]
                if use:
                    pe.wait_ge(used, use)
                xs = slice(T * f, T * (f + 1))
                nc.tensor.matmul(bk[:], wf[:, kd, 0, cols], xH[:, xs], start=True, stop=False)
                nc.tensor.matmul(bk[:], wf[:, kd, 1, cols], xH[:, xs], start=False, stop=False)
                nc.tensor.matmul(bk[:], wf[:, kd, 0, cols], xL[:, xs], start=False, stop=True).then_inc(rdy, 1)

            for t in range(NT // 2, NT):
                last = nc.tensor.matmul(LG[:, E * t:E * (t + 1)], xnT[:, P * t:P * (t + 1)], routerT[:],
                                        start=True, stop=True, skip_group_check=True)
            last.then_inc(logits_ready, 1)
            for n in range(FIRST, LAST):
                G, part = chunk(n)
                pair, opart = out_part(n)
                for slot in range(QT):
                    if 0 <= n < STEPS:
                        j = slot
                        q0 = min(P * j, T - 2 * P)
                        for b in range(2):
                            k = 8 * n + 2 * j + b
                            if slot == 0 and b == 0:
                                pe.wait_ge(neg_in[n % 2], 16 * (n // 2 + 1))
                            if k >= 2:
                                pe.wait_ge(exp_done, k - 1)
                            nc.tensor.matmul(ST[b][:, 0:T - q0],
                                             Kst[0:SROWS, n % SLOTS, T * b + P * j:T * b + P * (j + 1)],
                                             Qst[0:SROWS, n % SLOTS, T * b + q0:T * (b + 1)],
                                             start=True, stop=True).then_inc(st_ready, 1)
                    if 0 <= n + 2 < STEPS:
                        m, q = n + 2, QT - 1 - slot
                        w = max(P * (q + 1), 2 * P)
                        for b in range(2):
                            k = 8 * m + 2 * slot + b
                            if slot == 0 and b == 0:
                                pe.wait_ge(filled[m % SLOTS], 96 * (m // SLOTS + 1))
                            if k >= 2:
                                pe.wait_ge(s_max, k - 1)
                            nc.tensor.matmul(S[b][:, 0:w],
                                             Qst[0:KROWS, m % SLOTS, T * b + P * q:T * b + P * (q + 1)],
                                             Kst[0:KROWS, m % SLOTS, T * b:T * b + w],
                                             start=True, stop=True).then_inc(s_ready, 1)
                    if slot == 1 and 0 <= n + 1 < STEPS:
                        m = n + 1
                        pe.wait_ge(neg_ready, m + 1)
                        m_free()
                        nc.tensor.transpose(M[0:4 * QT, 0:P], nm[:, m % 2, :].bitcast(F32), ident[:]
                                            ).then_inc(negT_ready, 1)
                        issued["neg"] += 1
                    if slot in (1, 2) and 0 <= n - 1 < STEPS:
                        pv(n - 1, ((0, 1), (2, 3))[slot - 1])
                    if opart in (0, 2) and slot == 2:
                        m_free()
                        for t in range(QT):
                            last = nc.tensor.transpose(M[:, P * t:P * (t + 1)], yn[:, pair % 2, 2 * opart + t, :],
                                                       ident[:])
                        last.then_inc(ynT_ready, 1)
                        issued["yt"] += 1
                    if opart in (1, 3) and slot == 2:
                        m_free()
                        for t in range(QT):
                            last = nc.tensor.matmul(M[:, C * t:C * (t + 1)], yT[:, P * t:P * (t + 1)], wout[:],
                                                    start=True, stop=True, skip_group_check=True)
                        last.then_inc(out_ready, 1)
                        issued["o"] += 1
                    if (part, slot) in PIECES:
                        project(G, *PIECES[part, slot])
                    if part == 3 and slot in (0, 1):
                        f = slot
                        pe.wait_ge(q_roped, 2 * G + f + 1)
                        if f == 0:
                            pe.wait_ge(pa_used, pa_base(G) + 4)
                        else:
                            pe.wait_ge(pb_used, PB_USES * G + 4)
                        nc.tensor.matmul((PA, PB)[f][:], wqk[:], tq1[:, T * f:T * (f + 1)], start=True,
                                         stop=True).then_inc((pa_ready, pb_ready)[f], 1)
                    if part == 3 and slot >= 2 and G % 2 == 0:
                        pe.wait_ge(pa_used, pa_base(G) + 5)
                        for t in range(QT * (slot - 2), QT * (slot - 1)):
                            tok = PT * (G // G_PER_PAIR) + P * t
                            g = G % G_PER_PAIR
                            last = nc.tensor.matmul(PA[:, 2 * HG * HD * t:2 * HG * HD * (t + 1)],
                                                    xnT[:, tok:tok + P],
                                                    wvT[:, HG * HD * g:HG * HD * (g + 2)], start=True, stop=True,
                                                    skip_group_check=True)
                        if slot == 3:
                            last.then_inc(pa_ready, 1)
                if n == FIRST:
                    pe.wait_ge(out_in, 16 * 5)
                    for g in range(G_PER_PAIR):
                        last = nc.tensor.matmul(M[:, 0:C], oproj[:, g, :], kvT[:, g, :], start=(g == 0),
                                                stop=(g == G_PER_PAIR - 1), skip_group_check=True)
                    last.then_inc(m1_ready, 1)
                if n == FIRST + 1:
                    pe.wait_ge(m1_copied, 1)
                    for g in range(G_PER_PAIR):
                        at = 4 * G_PER_PAIR + g
                        last = nc.tensor.matmul(M[:, C:C + 1], oproj[:, g, :], biases[:, at:at + 1],
                                                start=(g == 0), stop=(g == G_PER_PAIR - 1), skip_group_check=True)
                    last.then_inc(o_ready, 1)
                if n == FIRST + 2:
                    pe.wait_ge(o_spread, 2)
                    nc.tensor.matmul(M[:, 2 * C:3 * C], m1T, cprojT, start=True, stop=True, skip_group_check=True)
                    nc.tensor.matmul(M[:, 3 * C:4 * C], o_rep, cprojT, start=True, stop=True,
                                     skip_group_check=True).then_inc(wout_ready, 1)
                if n == ROUTE + 1:
                    pe.wait_ge(onehot_ready, 1)
                    pe.wait_ge(wout_copied, 1)
                    nc.tensor.matmul(M[:, 0:E * NT], tri[:], oh[:].rearrange("p e t -> p (e t)"),
                                     start=True, stop=True, skip_group_check=True)
                    nc.tensor.matmul(M[:, 2 * P:2 * P + E * NT], ones[:], oh[:].rearrange("p e t -> p (e t)"),
                                     start=True, stop=True, skip_group_check=True).then_inc(prefix_ready, 1)
                if 0 <= n - 1 < STEPS and n % 2 == 0:
                    pe.wait_ge(y_copied, n // 2)
                    m_free()
                    Z = M[:, 0:2 * YW * QT].rearrange("p (b q c) -> p q b c", b=2, q=QT)
                    for q in range(QT):
                        last = nc.tensor.matmul(Z[:, q], ysb[:, P * q:P * (q + 1)],
                                                sumsel[:].rearrange("p (b c) -> p b c", b=2), start=True, stop=True,
                                                skip_group_check=True)
                    last.then_inc(z_ready, 1)
                    issued["z"] += 1

            pe.wait_ge(z_used, STEPS // 2)
            pe.wait_ge(pa_used, pa_base(GROUPS))
            pe.wait_ge(pb_used, PB_USES * GROUPS)
            pe.wait_ge(s_max, 8 * STEPS)
            for half in range(2):
                for t in range(QT):
                    last = nc.tensor.transpose((PA, PB)[half][:, P * t:P * (t + 1)],
                                               yn[:, (PAIRS - 1) % 2, QT * half + t, :], ident[:])
                last.then_inc(ynT_ready, 1)
            for half in range(2):
                pe.wait_ge(ynT_copied, 2 * (PAIRS - 1) + half + 1)
                for t in range(QT):
                    last = nc.tensor.matmul(S[half][:, C * t:C * (t + 1)], (yT, tk1)[half][:, P * t:P * (t + 1)],
                                            wout[:], start=True, stop=True, skip_group_check=True)
                last.then_inc(out_ready, 1)

        @block.vector
        def _(dve):
            nc.vector.memset(Y[:], 0.0).then_inc(y_clear, 1)

            chained = [0]

            def chain(ins):
                chained[0] += 1
                ins.then_inc(routed, 1)
                dve.wait_ge(routed, chained[0])

            def choose_expert():
                dve.wait_ge(logits_ready, 3)
                chain(nc.vector.tensor_tensor(lg[:], LG[:, 0:E * NT].rearrange("p (t e) -> p e t", e=E),
                                              router_b[:].unsqueeze(2).to_broadcast([P, E, NT]), ALU.add))
                nc.vector.tensor_scalar(lg[:], lg[:], -50.0, 50.0, ALU.max, ALU.min).then_inc(l_clipped, 1)
                dve.wait_ge(neg_exp, 1)
                chain(nc.vector.tensor_scalar(pr[:], pr[:], 1.0, None, ALU.add))
                chain(nc.vector.reciprocal(pr[:], pr[:]))
                chain(nc.vector.tensor_reduce(pm[:], pr[:].rearrange("p e t -> p t e"), AX.X, ALU.max))
                chain(nc.vector.tensor_tensor(oh[:], pr[:], pm[:].unsqueeze(1).to_broadcast([P, E, NT]),
                                              ALU.is_equal))
                chain(nc.vector.tensor_tensor(oh[:], oh[:], rank[:].unsqueeze(2).to_broadcast([P, E, NT]), ALU.mult))
                chain(nc.vector.tensor_reduce(ms[:], oh[:].rearrange("p e t -> p t e"), AX.X, ALU.max))
                nc.vector.tensor_tensor(oh[:], oh[:], ms[:].unsqueeze(1).to_broadcast([P, E, NT]),
                                        ALU.is_equal).then_inc(onehot_ready, 1)

            def expert_weights():
                chain(nc.vector.tensor_scalar(pm[:], pm[:], 1e-8, 1.0, ALU.max, ALU.min))
                chain(nc.vector.tensor_scalar(small[:], pm[:], 0.5, 1e-8, ALU.add, ALU.add))
                chain(nc.vector.tensor_scalar(small[:], small[:], 0.5, 2.0, ALU.max, ALU.min))
                chain(nc.vector.reciprocal(small[:], small[:]))
                chain(nc.vector.tensor_scalar(w_shared[:], small[:], 0.5, None, ALU.mult))
                chain(nc.vector.tensor_tensor(w_expert[:], small[:], pm[:], ALU.mult))

            def count_tokens():
                dve.wait_ge(prefix_ready, 1)
                chain(nc.vector.tensor_copy(tot[:].rearrange("p e t -> p (e t)"), M[:, 2 * P:2 * P + E * NT]))
                chain(nc.vector.tensor_tensor_scan(cum[:].rearrange("p e t -> p (e t)"),
                                                   tot[:].rearrange("p e t -> p (e t)"),
                                                   tot[:].rearrange("p e t -> p (e t)"), 0.0, ALU.add, ALU.bypass))
                nc.vector.memset(before[:, 0:1], 0.0)
                chain(nc.vector.tensor_copy(before[:, 1:E], cum[:, 0:E - 1, NT - 1]))
                chain(nc.vector.tensor_tensor(cnt[:], cum[:, :, NT - 1], before[:], ALU.subtract))
                chain(nc.vector.tensor_tensor(lg[:], cnt[:].unsqueeze(2).to_broadcast([P, E, NT]),
                                              thresh[:].unsqueeze(1).to_broadcast([P, E, NT]), ALU.is_gt))
                chain(nc.vector.tensor_reduce(nt_e[:], lg[:], AX.X, ALU.add))
                chain(nc.vector.tensor_tensor_scan(end_e[:], nt_e[:], nt_e[:], 0.0, ALU.add, ALU.bypass))
                chain(nc.vector.tensor_tensor(ge[:], tileno[:].unsqueeze(2).to_broadcast([P, ETABLE, E]),
                                              end_e[:].unsqueeze(1).to_broadcast([P, ETABLE, E]), ALU.is_ge))
                chain(nc.vector.tensor_reduce(te[:], ge[:], AX.X, ALU.add))
                chain(nc.vector.tensor_scalar(tile_expert[:], te[:], float(E - 1), None, ALU.min))

            def token_slots():
                chain(nc.vector.tensor_tensor(off_e[:], end_e[:], nt_e[:], ALU.subtract))
                chain(nc.vector.scalar_tensor_tensor(off_e[:], off_e[:], float(P), before[:], ALU.mult,
                                                     ALU.subtract))
                chain(nc.vector.tensor_tensor(cum[:], cum[:], tot[:], ALU.subtract))
                chain(nc.vector.tensor_tensor(cum[:].rearrange("p e t -> p (e t)"),
                                              cum[:].rearrange("p e t -> p (e t)"), M[:, 0:E * NT], ALU.add))
                chain(nc.vector.tensor_tensor(cum[:], cum[:], off_e[:].unsqueeze(2).to_broadcast([P, E, NT]),
                                              ALU.add))
                chain(nc.vector.tensor_tensor(cum[:], cum[:], oh[:], ALU.mult))
                chain(nc.vector.tensor_reduce(posf[:], cum[:].rearrange("p e t -> p t e"), AX.X, ALU.add))
                chain(nc.vector.tensor_copy(pos[:], posf[:]))
                dve.sem_inc(pos_ready, 1)

            def rope(G, part, piece):
                g = G % G_PER_PAIR
                t1, t2 = ((tk1, tk2), (tq1, tq2))[part]
                if piece == 0:
                    if part == 0 and G:
                        dve.wait_ge(kl_ready, 2 * G)
                    if part == 1:
                        if G:
                            dve.wait_ge(ql_ready, 2 * G)
                            dve.wait_ge(pa_ready, pa_base(G))
                            dve.wait_ge(pb_ready, PB_USES * G)
                f, ab = piece // 2, piece % 2
                kind = 2 - 2 * part + ab
                bias = biases[:, kind * G_PER_PAIR + g:kind * G_PER_PAIR + g + 1]
                xs = slice(T * f, T * (f + 1))
                if ab == 0:
                    dve.wait_ge(pa_ready, pa_base(G) + 2 * part + f + 1)
                    nc.vector.scalar_tensor_tensor(t1[:, xs], PA[:], bias, cosr[:], ALU.add, ALU.mult
                                                   ).then_inc(pa_used, 1)
                else:
                    dve.wait_ge(pb_ready, PB_USES * G + 2 * part + f + 1)
                    nc.vector.scalar_tensor_tensor(t2[:, xs], PB[:], bias, sinr[:], ALU.add, ALU.mult
                                                   ).then_inc(pb_used, 1)

            for n in range(FIRST, LAST):
                if n == ROUTE:
                    choose_expert()
                if n == ROUTE + 1:
                    expert_weights()
                if n == ROUTE + 2:
                    count_tokens()
                if n == ROUTE + 3:
                    token_slots()
                G, part = chunk(n)
                for i in range(8):
                    if 0 <= n + 2 < STEPS:
                        m = n + 2
                        b, q = i % 2, QT - 1 - i // 2
                        w = P * (q + 1)
                        dve.wait_ge(s_ready, 8 * m + i + 1)
                        if 8 * m + i >= 2:
                            dve.wait_ge(s_max, 8 * m + i - 1)
                        nc.vector.tensor_tensor_reduce(scratch[:, i % 2, 0:w], S[i % 2][:, 0:w], mask[:, T - w:T],
                                                       1.0, MASKED, ALU.add, ALU.max,
                                                       mx[:, m % 2, QT * b + q:QT * b + q + 1]
                                                       ).then_inc(s_max, 1)
                    pair, opart = out_part(n)
                    if opart in (1, 3) and i == 5:
                        dve.wait_ge(out_ready, 2 * pair + opart // 2 + 1)
                        dve.wait_ge(xres_const, pair + 1)
                        half = xres[:, 2 * (opart - 1):2 * (opart - 1) + QT, :].rearrange("p t c -> p (t c)")
                        nc.vector.tensor_tensor(half, half, M[:], ALU.add).then_inc(o_added, 1)
                    if (part, i) in ROPES:
                        rope(G, *ROPES[part, i])
                if 0 <= n + 2 < STEPS:
                    m = n + 2
                    dve.wait_ge(s_max, 8 * m + 8)
                    if m >= 2:
                        dve.wait_ge(negT_ready, m - 1)
                    nc.vector.tensor_scalar(nm[:, m % 2, 0:2 * QT], mx[:, m % 2, :], -1.0, None, ALU.mult
                                            ).then_inc(neg_high, 1)
                    dve.wait_ge(neg_high, m + 1)
                    nc.vector.scalar_tensor_tensor(nm[:, m % 2, 2 * QT:4 * QT], mx[:, m % 2, :], -1.0,
                                                   nm[:, m % 2, 0:2 * QT].bitcast(F32), ALU.mult, ALU.subtract
                                                   ).then_inc(neg_ready, 1)
                if n == FIRST:
                    dve.wait_ge(m1_ready, 1)
                    nc.vector.tensor_copy(m1T, M[:, 0:C]).then_inc(m1_copied, 1)
                if n == FIRST + 1:
                    dve.wait_ge(o_ready, 1)
                    nc.vector.tensor_tensor(o_col, M[:, C:C + 1], out_b, ALU.add).then_inc(o_spread, 1)
                    dve.wait_ge(o_spread, 1)
                    nc.vector.tensor_scalar(o_rep, ones[:], o_col, None, ALU.mult).then_inc(o_spread, 1)
                if n == FIRST + 2:
                    dve.wait_ge(wout_ready, 1)
                    nc.vector.tensor_copy(wout[:], M[:, 2 * C:3 * C])
                    nc.vector.tensor_tensor(const_row[:], M[:, 3 * C:4 * C], cproj_b, ALU.add).then_inc(wout_copied, 1)
                if 0 <= n - 1 < STEPS and n % 2 == 0:
                    m = n - 2
                    Z = M[:, 0:2 * YW * QT].rearrange("p (t h c) -> p t h c", t=2 * QT, h=2)
                    dve.wait_ge(z_ready, n // 2)
                    nc.vector.reciprocal(rz[:], Z[:, :, :, HD]).then_inc(rz_ready, 1)
                    dve.wait_ge(rz_ready, n // 2)
                    pair, head = m // H, m % H
                    if head == 0 and pair >= 2:
                        dve.wait_ge(ynT_ready, 2 * (pair - 1))
                    o = yn[:, pair % 2, :, HD * head:HD * (head + 2)].rearrange("p t (h d) -> p t h d", h=2)
                    nc.vector.tensor_tensor(o, Z[:, :, :, 0:HD], rz[:].unsqueeze(3).to_broadcast([P, 2 * QT, 2, HD]),
                                            ALU.mult).then_inc(z_used, 1)

            dve.wait_ge(xres_const, PAIRS)
            for half in range(2):
                dve.wait_ge(out_ready, 2 * (PAIRS - 1) + half + 1)
                rows = xres[:, QT * half:QT * (half + 1), :].rearrange("p t c -> p (t c)")
                nc.vector.tensor_tensor(rows, rows, S[half][:], ALU.add).then_inc(o_added, 1)


def experts(nc, d, bank, sem, shared_in, w13s, w2s, mixed_out, ident, xnT, pos, w_shared, w_expert, tile_expert,
            sorted_x, sorted_y, mixed, out):
    tmp = ExitStack()
    with tmp:
        def sb(name, shape, dt):
            return tmp.enter_context(nc.sbuf_tensor(name, shape, dt))

        w13 = sb("w13", [C, E, 2 * I], F32)
        w2 = sb("w2", [P, E, 3, C], F32)
        xs = sb("xs", [P, ETABLE, C], F32)
        w13H = sb("w13H", [C, E, 2 * I], F32R)
        w13L = sb("w13L", [C, E, 2 * I], F32R)
        w13sH = sb("w13sH", [C, 2 * I], F32R)
        w13sL = sb("w13sL", [C, 2 * I], F32R)
        xcH = sb("xcH", [C, 2, TC], F32R)
        xcL = sb("xcL", [C, 2, TC], F32R)
        xsH = sb("xsH", [C, 2, P], F32R)
        xsL = sb("xsL", [C, 2, P], F32R)
        g1 = sb("g1", [P, 2, I], F32)
        gg = sb("gg", [P, 2, I], F32)
        gT = sb("gT", [P, 2, 3, P], F32)
        ye = sb("ye", [P, ETILES, C], F32)
        h1 = sb("h1", [P, 2, TC], F32)
        hT = sb("hT", [P, 2, 3, TC], F32)
        acc = sb("acc", [P, NT, C], F32)
        yg = sb("yg", [P, NT, C], F32)

        xs_in, acc_in, w2_in = sem("xs_in"), sem("acc_in"), sem("w2_in")
        w13_in = [sem(f"w13_in{i}") for i in range((E + 1) // 2)]
        ws_high, ws_low, w_high, w_low = sem("ws_high"), sem("ws_low"), sem("w_high"), sem("w_low")
        xc_high, xc_low = sem("xc_high"), sem("xc_low")
        xsT_ready, xs_high, xs_low = sem("xsT_ready"), sem("xs_high"), sem("xs_low")
        h_ready, silu_done, gate_done = sem("h_ready"), sem("silu_done"), sem("gate_done")
        gT_ready, gT_copied, y_ready, y_copied = (sem("gT_ready"), sem("gT_copied"), sem("ye_ready"),
                                                  sem("ye_copied"))
        y_out = sem("y_out")
        gathered = [sem(f"gathered{c}") for c in range(CHUNKS)]
        sh_ready, sh_silu, sh_gate = sem("sh_ready"), sem("sh_silu"), sem("sh_gate")
        so_ready, so_added, e_added, out_done = sem("so_ready"), sem("so_added"), sem("e_added"), sem("out_done")
        XT, Y, GT, SY = bank[4], bank[5], bank[6:8], bank[6:8]

        xs_rows = sorted_x.rearrange("(t p) c -> p t c", p=P)
        sy_rows = sorted_y.rearrange("(t p) c -> p t c", p=P)
        XL = 5
        XW = ETABLE // XL

        with nc.Block() as block:
            @block.sync
            def _(sp):
                for i in range(0, E, 2):
                    j = min(i + 2, E)
                    sp.dma_start(w13[:, i:j, :], d["w13"][:, i:j, :]).then_inc(w13_in[i // 2], 16)
                sp.wait_ge(mixed_out, 16 * (PAIRS + 1))
                sp.dma_start(acc[:], mixed.rearrange("(t p) c -> p t c", p=P)).then_inc(acc_in, 16)
                for i in range(XL):
                    sp.dma_start(xs[:, XW * i:XW * (i + 1), :], xs_rows[:, XW * i:XW * (i + 1), :]
                                 ).then_inc(xs_in, 16)
                sp.dma_start(w2[:], d["w2"][:, 0:E, :, :]).then_inc(w2_in, 16)
                for t in range(1, ETILES, 2):
                    sp.wait_ge(y_copied, t + 1)
                    sp.dma_start(sy_rows[:, t - 1:t + 1, :], ye[:, t - 1:t + 1, :]).then_inc(y_out, 16)
                for c in range(CHUNKS):
                    sp.wait_ge(e_added, c + 1)
                    sp.dma_start(out[TC * c:TC * (c + 1), :].rearrange("(t p) c -> p t c", p=P),
                                 acc[:, TT * c:TT * (c + 1), :]).then_inc(out_done, 16)
                sp.wait_ge(out_done, 16 * CHUNKS)

            @block.gpsimd
            def _(pool):
                for e in range(0, E, 2):
                    pool.wait_ge(w_high, e + 1)
                    nc.gpsimd.tensor_tensor(w13L[:, e, :], w13[:, e, :], w13H[:, e, :].bitcast(F32), ALU.subtract
                                            ).then_inc(w_low, 1)
                pool.wait_ge(y_out, 16 * (ETILES // 2))
                for t in range(NT):
                    pool.indirect_dma_start(yg[:, t, :], None, sorted_y,
                                            bass.IndirectOffsetOnAxis(pos[:, t:t + 1], 0)
                                            ).then_inc(gathered[t // TT], 16)

            @block.scalar
            def _(act):
                def high(c):
                    if c >= 2:
                        act.wait_ge(sh_ready, 3 * (c - 1))
                        act.wait_ge(xc_low, c - 1)
                    nc.scalar.copy(xcH[:, c % 2, :], xnT[:, TC * c:TC * (c + 1)]).then_inc(xc_high, 1)

                def weights_high(e):
                    act.wait_ge(w13_in[e // 2], 16)
                    nc.scalar.copy(w13H[:, e, :], w13[:, e, :]).then_inc(w_high, 1)

                WEIGHTS = {1: [0], 2: [1], 3: [2], 4: [3], 5: [4], 6: [5], 7: [6]}

                def shared_silu(c):
                    if c + 1 < CHUNKS:
                        high(c + 1)
                    for k in range(3):
                        u = 3 * c + k
                        for e in WEIGHTS.get(u, ()):
                            weights_high(e)
                        act.wait_ge(sh_ready, u + 1)
                        if u >= 2:
                            act.wait_ge(sh_gate, u - 1)
                        nc.scalar.activation(h1[0:IC[k], u % 2, :], bank[2 * (u % 2)][0:IC[k], :], ACT.Silu
                                             ).then_inc(sh_silu, 1)

                def copy_xT(t):
                    act.wait_ge(xsT_ready, t + 1)
                    if t >= 2:
                        act.wait_ge(h_ready, t - 1)
                    nc.scalar.copy(xsH[:, t % 2, :], XT[:, P * (t % 2):P * (t % 2 + 1)]).then_inc(xs_high, 1)

                act.wait_ge(shared_in, 32)
                nc.scalar.copy(w13sH[:], w13s[:]).then_inc(ws_high, 1)
                high(0)
                for c in range(FIRST_CHUNKS):
                    shared_silu(c)
                for t in range(2):
                    copy_xT(t)
                for t in range(ETILES + 2):
                    if t < ETILES:
                        act.wait_ge(h_ready, t + 1)
                        if t >= 2:
                            act.wait_ge(gate_done, t - 1)
                        nc.scalar.activation(g1[:, t % 2, :], bank[2 * (t % 2)][:, 0:I], ACT.Silu
                                             ).then_inc(silu_done, 1)
                    if t + 2 < ETILES:
                        copy_xT(t + 2)
                    if t >= 2:
                        u = t - 2
                        act.wait_ge(y_ready, u + 1)
                        nc.scalar.copy(ye[:, u, :], Y[:, P * (u % 2):P * (u % 2 + 1)]).then_inc(y_copied, 1)
                for c in range(FIRST_CHUNKS, CHUNKS):
                    shared_silu(c)

            @block.tensor
            def _(pe):
                def split_product(out_, wH, wL, aH, aL):
                    nc.tensor.matmul(out_, wH, aH, start=True, stop=False)
                    nc.tensor.matmul(out_, wH, aL, start=False, stop=False)
                    return nc.tensor.matmul(out_, wL, aH, start=False, stop=True)

                def shared_hidden(c):
                    pe.wait_ge(xc_low, c + 1)
                    for k in range(3):
                        u = 3 * c + k
                        if u >= 2:
                            pe.wait_ge(sh_gate, u - 1)
                        for half in range(2):
                            cols = slice(half * I + P * k, half * I + P * k + IC[k])
                            last = split_product(bank[2 * (u % 2) + half][0:IC[k], :], w13sH[:, cols],
                                                 w13sL[:, cols], xcH[:, c % 2, :], xcL[:, c % 2, :])
                        last.then_inc(sh_ready, 1)

                def shared_out(c):
                    pe.wait_ge(sh_gate, 3 * c + 3)
                    if c >= 2:
                        pe.wait_ge(so_added, c - 1)
                    for t in range(TT):
                        for k in range(3):
                            last = nc.tensor.matmul(SY[c % 2][:, C * t:C * (t + 1)],
                                                    hT[0:IC[k], c % 2, k, P * t:P * (t + 1)],
                                                    w2s[0:IC[k], k, :], start=(k == 0), stop=(k == 2),
                                                    skip_group_check=True)
                    last.then_inc(so_ready, 1)

                def x_transpose(t):
                    pe.wait_ge(xs_in, 16 * XL)
                    if t >= 1:
                        pe.wait_ge(xs_low, t)
                    nc.tensor.transpose(XT[:, P * (t % 2):P * (t % 2 + 1)], xs[:, t, :], ident[:]
                                        ).then_inc(xsT_ready, 1)

                pe.wait_ge(ws_low, 1)
                for c in range(FIRST_CHUNKS):
                    shared_hidden(c)
                    if c:
                        shared_out(c - 1)
                x_transpose(0)
                x_transpose(1)
                shared_out(FIRST_CHUNKS - 1)
                pe.wait_ge(w2_in, 16)
                pe.wait_ge(w_low, E)
                e_of = {}
                for t in range(ETILES + 2):
                    if t < ETILES:
                        e = pe.value_load(tile_expert[0:1, t:t + 1], min_val=0, max_val=E - 1)
                        e_of[t] = e
                        pe.wait_ge(xs_low, t + 1)
                        if t >= 2:
                            pe.wait_ge(gate_done, t - 1)
                        else:
                            pe.wait_ge(sh_gate, 3 * FIRST_CHUNKS)
                        for half in range(2):
                            cols = slice(I * half, I * (half + 1))
                            last = split_product(bank[2 * (t % 2) + half][:, 0:I], xsH[:, t % 2, :], xsL[:, t % 2, :],
                                                 w13H[:, bass.ds(e, 1), cols], w13L[:, bass.ds(e, 1), cols])
                        last.then_inc(h_ready, 1)
                    if t + 2 < ETILES:
                        x_transpose(t + 2)
                    if 1 <= t <= ETILES:
                        u = t - 1
                        pe.wait_ge(gate_done, u + 1)
                        if u >= 2:
                            pe.wait_ge(gT_copied, u - 1)
                        else:
                            pe.wait_ge(so_added, FIRST_CHUNKS - 1 + u)
                        for k in range(3):
                            last = nc.tensor.transpose(GT[u % 2][0:IC[k], P * k:P * (k + 1)],
                                                       gg[:, u % 2, P * k:P * k + IC[k]], ident[:])
                        last.then_inc(gT_ready, 1)
                    if t >= 2:
                        u = t - 2
                        pe.wait_ge(gT_copied, u + 1)
                        if u >= 1:
                            pe.wait_ge(y_copied, u)
                        for k in range(3):
                            last = nc.tensor.matmul(Y[:, P * (u % 2):P * (u % 2 + 1)], gT[0:IC[k], u % 2, k, :],
                                                    w2[0:IC[k], bass.ds(e_of[u], 1), k, :], start=(k == 0),
                                                    stop=(k == 2), skip_group_check=True)
                        last.then_inc(y_ready, 1)
                pe.wait_ge(gate_done, ETILES)
                pe.wait_ge(gT_copied, ETILES)
                for c in range(FIRST_CHUNKS, CHUNKS):
                    shared_hidden(c)
                    if c > FIRST_CHUNKS:
                        shared_out(c - 1)
                shared_out(CHUNKS - 1)

            @block.vector
            def _(dve):
                def low(c):
                    dve.wait_ge(xc_high, c + 1)
                    if c >= 2:
                        dve.wait_ge(sh_ready, 3 * (c - 1))
                    nc.vector.tensor_tensor(xcL[:, c % 2, :], xnT[:, TC * c:TC * (c + 1)],
                                            xcH[:, c % 2, :].bitcast(F32), ALU.subtract).then_inc(xc_low, 1)

                def low_xT(t):
                    dve.wait_ge(xs_high, t + 1)
                    if t >= 2:
                        dve.wait_ge(h_ready, t - 1)
                    nc.vector.tensor_tensor(xsL[:, t % 2, :], XT[:, P * (t % 2):P * (t % 2 + 1)],
                                            xsH[:, t % 2, :].bitcast(F32), ALU.subtract).then_inc(xs_low, 1)

                dve.wait_ge(ws_high, 1)
                nc.vector.tensor_tensor(w13sL[:], w13s[:], w13sH[:].bitcast(F32), ALU.subtract).then_inc(ws_low, 1)
                low(0)

                def weights_low(e):
                    dve.wait_ge(w_high, e + 1)
                    nc.vector.tensor_tensor(w13L[:, e, :], w13[:, e, :], w13H[:, e, :].bitcast(F32), ALU.subtract
                                            ).then_inc(w_low, 1)

                def shared_gate(c):
                    if c + 1 < CHUNKS:
                        low(c + 1)
                    for k in range(3):
                        u = 3 * c + k
                        if u in (3, 5, 7):
                            weights_low(u - 2)
                        dve.wait_ge(sh_silu, u + 1)
                        if c >= 2:
                            dve.wait_ge(so_ready, c - 1)
                        nc.vector.tensor_tensor(hT[0:IC[k], c % 2, k, :], h1[0:IC[k], u % 2, :],
                                                bank[2 * (u % 2) + 1][0:IC[k], :], ALU.mult).then_inc(sh_gate, 1)

                def shared_add(c):
                    dve.wait_ge(so_ready, c + 1)
                    for t in range(TT * c, TT * (c + 1)):
                        last = nc.vector.scalar_tensor_tensor(
                            acc[:, t, :], SY[c % 2][:, C * (t % TT):C * (t % TT + 1)], w_shared[:, t:t + 1],
                            acc[:, t, :], ALU.mult, ALU.add)
                    last.then_inc(so_added, 1)

                ADDS = {4: [0], 5: [1], 6: [2], 7: [3, 4], CHUNKS: [5, 6, 7]}

                def expert_add(c):
                    dve.wait_ge(so_added, c + 1)
                    dve.wait_ge(gathered[c], 16 * TT)
                    for t in range(TT * c, TT * (c + 1)):
                        last = nc.vector.scalar_tensor_tensor(acc[:, t, :], yg[:, t, :], w_expert[:, t:t + 1],
                                                              acc[:, t, :], ALU.mult, ALU.add)
                    last.then_inc(e_added, 1)

                for c in range(FIRST_CHUNKS):
                    shared_gate(c)
                    if c == 1:
                        dve.wait_ge(acc_in, 16)
                    if c:
                        shared_add(c - 1)
                low_xT(0)
                low_xT(1)
                shared_add(FIRST_CHUNKS - 1)
                for t in range(ETILES + 1):
                    if t < ETILES:
                        dve.wait_ge(silu_done, t + 1)
                        if t >= 2:
                            dve.wait_ge(gT_ready, t - 1)
                        nc.vector.tensor_tensor(gg[:, t % 2, :], g1[:, t % 2, :], bank[2 * (t % 2) + 1][:, 0:I],
                                                ALU.mult).then_inc(gate_done, 1)
                    if t + 2 < ETILES:
                        low_xT(t + 2)
                    if t:
                        u = t - 1
                        dve.wait_ge(gT_ready, u + 1)
                        if u >= 2:
                            dve.wait_ge(y_ready, u - 1)
                        nc.vector.tensor_copy(gT[:, u % 2, 0:2, :].rearrange("p k t -> p (k t)"),
                                              GT[u % 2][:, 0:2 * P])
                        nc.vector.tensor_copy(gT[0:IC[2], u % 2, 2, :], GT[u % 2][0:IC[2], 2 * P:3 * P]
                                              ).then_inc(gT_copied, 1)
                for c in range(FIRST_CHUNKS, CHUNKS):
                    shared_gate(c)
                    if c > FIRST_CHUNKS:
                        shared_add(c - 1)
                        for a in ADDS[c]:
                            expert_add(a)
                shared_add(CHUNKS - 1)
                for a in ADDS[CHUNKS]:
                    expert_add(a)


def block_diagonal(w):
    a, b = w.shape
    out = np.zeros((H * a, H * b), w.dtype)
    for h in range(H):
        out[h * a:(h + 1) * a, h * b:(h + 1) * b] = w
    return out


def kernel(L0_attn_x, L0_attn_c_attn_w, L0_attn_c_attn_b, L0_attn_q2l_w, L0_attn_q2l_b, L0_attn_kv2l_w,
           L0_attn_kv2l_b, L0_attn_l2o_w, L0_attn_l2o_b, L0_attn_wqk_w, L0_attn_wqk_b, L0_attn_cproj_w,
           L0_attn_cproj_b, L0_ffn_router_w, L0_ffn_routing_bias, L0_ffn_sw1, L0_ffn_sw2, L0_ffn_sw3, L0_ffn_ew1,
           L0_ffn_ew2, L0_ffn_ew3):
    import concourse.bacc as bacc
    from concourse.bass_utils import run_bass_kernel_spmd

    a = lambda z: np.asarray(z)
    swap = np.arange(L) ^ 1
    q2l, kv2l, l2o, wqk = a(L0_attn_q2l_w), a(L0_attn_kv2l_w), a(L0_attn_l2o_w), a(L0_attn_wqk_w)
    q2lb, kv2lb = a(L0_attn_q2l_b), a(L0_attn_kv2l_b)
    cw, cb = a(L0_attn_c_attn_w), a(L0_attn_c_attn_b)
    spread = np.stack([block_diagonal(w.T) for w in (q2l, q2l[swap], kv2l, kv2l[swap])], axis=1)
    kvT = block_diagonal(kv2l).reshape(G_PER_PAIR, P, C).transpose(1, 0, 2)
    oproj = block_diagonal(l2o.T).reshape(G_PER_PAIR, P, C).transpose(1, 0, 2)
    wqk_bd = np.zeros((P, P), wqk.dtype)
    for h in range(HG):
        wqk_bd[L * h:L * (h + 1), L * h:L * (h + 1)] = wqk.T
    lat_b = np.stack([np.tile(z, HG) for z in (q2lb, q2lb[swap], kv2lb, kv2lb[swap], kv2lb)
                      for _ in range(G_PER_PAIR)], axis=1)
    w1 = np.concatenate([a(L0_ffn_ew1), a(L0_ffn_sw1)[None]])
    w3 = np.concatenate([a(L0_ffn_ew3), a(L0_ffn_sw3)[None]])
    w2 = np.concatenate([a(L0_ffn_ew2), a(L0_ffn_sw2)[None]])
    w13 = np.concatenate([w1, w3], axis=1).transpose(2, 0, 1)
    w2t = np.zeros((E + 1, 3 * P, C), w2.dtype)
    w2t[:, :I] = w2.transpose(0, 2, 1)
    arrays = {
        "x": a(L0_attn_x).reshape(N, C),
        "wqk_nat": cw[:2 * C].reshape(2, C, C).transpose(1, 0, 2),
        "spread": spread, "kvT": kvT, "oproj": oproj, "bqkv": cb.reshape(3, C).T, "lat_b": lat_b,
        "out_b": np.tile(a(L0_attn_l2o_b), H)[:, None], "cprojT": a(L0_attn_cproj_w).T,
        "cproj_b": np.broadcast_to(a(L0_attn_cproj_b), (P, C)), "routerT": a(L0_ffn_router_w).T,
        "router_b": np.broadcast_to(a(L0_ffn_routing_bias), (P, E)), "wqk_bd": wqk_bd,
        "wqk_b": np.tile(a(L0_attn_wqk_b), HG)[:, None], "wvT": cw[2 * C:].T, "w13": w13,
        "w2": w2t.reshape(E + 1, 3, P, C).transpose(2, 0, 1, 3), **shape_constants(),
    }
    nc = bacc.Bacc("TRN2", target_bir_lowering=False, num_devices=1)
    arrays = {f"in_{k}": np.ascontiguousarray(z) for k, z in arrays.items()}
    d = {k[3:]: nc.dram_tensor(k, z.shape, mybir.dt.from_np(z.dtype), kind="ExternalInput").ap()
         for k, z in arrays.items()}
    out = nc.dram_tensor("out_0", (N, C), F32, kind="ExternalOutput").ap()
    build(nc, d, out)
    r = run_bass_kernel_spmd(nc, [arrays], core_ids=[0])
    return r.results[0]["out_0"].reshape(B, T, C)
```
